# Optimizing a Trainium2 kernel written in Bass

```python
import numpy as np
import jax
import jax.numpy as jnp

def _softmax(x, axis=-1):
    return jax.nn.softmax(x, axis=axis)

def _gelu(x):
    return jax.nn.gelu(x, approximate=True)

def _silu(x):
    return jax.nn.silu(x)

def _sigmoid(x):
    return jax.nn.sigmoid(x)

def _layernorm(x, axis=-1, eps=1e-05):
    m = jnp.mean(x, axis=axis, keepdims=True)
    v = jnp.var(x, axis=axis, keepdims=True)
    return (x - m) / jnp.sqrt(v + eps)

def _scatter_add(tgt, idx, src, axis=0):
    return tgt.at[idx].add(src)

def _segment_sum(src, seg, n):
    return jax.ops.segment_sum(src, seg, n)
kernel_name = 'mk_decoder_postln_d2_seqx_r8_9709cf'

def setup_inputs(seed: int=0):
    np.random.seed(seed)
    _w = jnp.asarray

    def _rec_inputs():
        import jax
        import jax.numpy as jnp
        _rk = jax.random.key(seed)
        x = 7.22e-05 + 1 * jax.random.normal(jax.random.fold_in(_rk, 1), (2, 512, 128), jnp.float32)
        _lenS = 512 - jax.random.randint(jax.random.fold_in(_rk, 7), (2,), 0, max(1, 512 // 4) + 1, jnp.int32)
        _lenS2 = 154 - jax.random.randint(jax.random.fold_in(_rk, 8), (2,), 0, max(1, 154 // 4) + 1, jnp.int32)
        _ctx_768P = jax.random.normal(jax.random.fold_in(_rk, 11), (2, 16, 96), jnp.float32)
        _ctx_768c = jax.random.dirichlet(jax.random.fold_in(_rk, 511), 0.3 * jnp.ones((16,), jnp.float32), (2, 154))
        _ctx_768t = jnp.einsum('bsk,bkd->bsd', _ctx_768c, _ctx_768P)
        _ctx_768t = _ctx_768t * jax.lax.rsqrt(jnp.mean(jnp.square(_ctx_768t)) + 1e-12) * 0.953939
        ctx_768 = 3.88148e-05 + 0.999967 * (_ctx_768t + 0.3 * jax.random.normal(jax.random.fold_in(_rk, 611), (2, 154, 96), jnp.float32))
        _validS = jnp.arange(512)[None, :] < _lenS[:, None]
        _validS2 = jnp.arange(154)[None, :] < _lenS2[:, None]
        _causal = jnp.tril(jnp.ones((512, 512), dtype=bool))
        mask_BxS_bf1 = jnp.ones((2, 512), dtype=bool)
        mask_BxS2_bf1 = jnp.ones((2, 154), dtype=bool)
        mask_BxS2_bk0 = jnp.logical_not(jnp.broadcast_to(_validS2[:, :], (2, 154)))
        return (x, ctx_768, mask_BxS_bf1, mask_BxS2_bf1, mask_BxS2_bk0)
    x, ctx_768, mask_BxS_bf1, mask_BxS2_bf1, mask_BxS2_bk0 = _rec_inputs()

    def _L0_attn_setup():
        import jax, jax.numpy as jnp
        import numpy as np
        EXPAND = 2
        key = jax.random.key(seed)
        k1, k2, k3 = jax.random.split(key, 3)
        n, b, d = (512, 8, 128)
        x = jax.random.normal(k1, (n, b, d), dtype=jnp.float32)
        lower_bound = jnp.zeros((d,), dtype=jnp.float32)
        W_in = jax.random.normal(k2, (d, 3 * d), dtype=jnp.float32) / np.sqrt(d)
        W_out = jax.random.normal(k3, (d, d), dtype=jnp.float32) / np.sqrt(d)
        return {'x': x, 'lower_bound': lower_bound, 'W_in': W_in, 'W_out': W_out}
    _L0_attn_all = _L0_attn_setup()
    _L0_attn_in = {k: v for k, v in _L0_attn_all.items() if k in ('lower_bound', 'W_in', 'W_out')}
    del _L0_attn_all

    def _L0_xattn_setup():
        import jax, jax.numpy as jnp
        import numpy as np
        B, T, DT, G, DV = (16, 64, 128, 72, 96)
        H, DH = (4, 32)
        INNER = H * DH
        HID = 4 * DT
        N_STATE = 64
        K_TOP = 32

        def layernorm(x, g, b, eps=1e-05):
            m = x.mean(-1, keepdims=True)
            v = x.var(-1, keepdims=True)
            return (x - m) * jax.lax.rsqrt(v + eps) * g + b

        def s4d(x, log_dt, A_re, A_im, C_re, C_im, D_skip):
            Bb, L, D = x.shape
            dt = jnp.exp(log_dt)
            A = A_re + 1j * A_im
            C = C_re + 1j * C_im
            dtA = dt[:, None] * A
            dC = C * (jnp.exp(dtA) - 1.0) / A
            powers = jnp.exp(dtA[:, :, None] * jnp.arange(L))
            K = 2.0 * jnp.einsum('dn,dnl->dl', dC, powers).real
            n = 2 * L
            Kf = jnp.fft.rfft(K, n=n, axis=-1)
            xf = jnp.fft.rfft(x, n=n, axis=1)
            y = jnp.fft.irfft(xf * Kf.T[None], n=n, axis=1)[:, :L]
            return y + x * D_skip
        key = jax.random.key(seed)
        ks = jax.random.split(key, 16)
        s = 0.02
        inp = {'x_text': jax.random.normal(ks[0], (B, T, DT), jnp.float32), 'x_vision': jax.random.normal(ks[1], (B, G, DV), jnp.float32), 'text_mask': jnp.ones((B, T), bool), 'vision_mask': jnp.ones((B, G), bool), 'Wq': jax.random.normal(ks[2], (DT, INNER), jnp.float32) * s, 'Wk': jax.random.normal(ks[3], (DV, INNER), jnp.float32) * s, 'Wv': jax.random.normal(ks[4], (DV, DT), jnp.float32) * s, 'W_film_in': jax.random.normal(ks[5], (DT, 2 * DT), jnp.float32) * s, 'b_film_in': jnp.zeros((2 * DT,), jnp.float32), 'W_film_out': jax.random.normal(ks[6], (DT, 2 * DT), jnp.float32) * s, 'b_film_out': jnp.zeros((2 * DT,), jnp.float32), 'g_norm_in': jnp.ones((DT,), jnp.float32), 'b_norm_in': jnp.zeros((DT,), jnp.float32), 'g_norm_out': jnp.ones((DT,), jnp.float32), 'b_norm_out': jnp.zeros((DT,), jnp.float32), 'g_ffn': jnp.ones((DT,), jnp.float32), 'b_ffn': jnp.zeros((DT,), jnp.float32), 'W1': jax.random.normal(ks[7], (DT, HID), jnp.float32) * s, 'b1': jnp.zeros((HID,), jnp.float32), 'W2': jax.random.normal(ks[8], (HID, DT), jnp.float32) * s, 'b2': jnp.zeros((DT,), jnp.float32), 'log_dt': jnp.log(0.001) + jax.random.uniform(ks[9], (DT,), jnp.float32) * (jnp.log(0.1) - jnp.log(0.001)), 'A_re': -0.5 * jnp.ones((DT, N_STATE), jnp.float32), 'A_im': jnp.tile(jnp.pi * jnp.arange(N_STATE, dtype=jnp.float32), (DT, 1)), 'C_re': jax.random.normal(ks[10], (DT, N_STATE), jnp.float32) * 0.5 ** 0.5, 'C_im': jax.random.normal(ks[11], (DT, N_STATE), jnp.float32) * 0.5 ** 0.5, 'D_skip': jax.random.normal(ks[12], (DT,), jnp.float32), 'mod_gate': jnp.array(0.5, jnp.float32)}
        return inp
    _L0_xattn_all = _L0_xattn_setup()
    _L0_xattn_in = {k: v for k, v in _L0_xattn_all.items() if k in ('Wq', 'Wk', 'Wv', 'W_film_in', 'b_film_in', 'W_film_out', 'b_film_out', 'g_norm_in', 'b_norm_in', 'g_norm_out', 'b_norm_out', 'g_ffn', 'b_ffn', 'W1', 'b1', 'W2', 'b2', 'log_dt', 'A_re', 'A_im', 'C_re', 'C_im', 'D_skip', 'mod_gate')}
    del _L0_xattn_all

    def _L0_ffn_setup():
        import jax, jax.numpy as jnp
        import numpy as np
        D = 128
        H = 4
        HD = D // H
        E = 8
        FF = 512
        CAP_FACTOR = 1.0

        def _ln(x, g, b, eps=1e-05):
            mu = jnp.mean(x, -1, keepdims=True)
            v = jnp.mean((x - mu) ** 2, -1, keepdims=True)
            return (x - mu) * jax.lax.rsqrt(v + eps) * g + b

        def _mha(x, w, b, ow, ob):
            L, N, _ = x.shape
            qkv = x @ w.T + b
            q, k, v = jnp.split(qkv, 3, axis=-1)
            rh = lambda t: t.reshape(L, N, H, HD).transpose(1, 2, 0, 3)
            q, k, v = (rh(q), rh(k), rh(v))
            scores = jnp.einsum('nhld,nhmd->nhlm', q, k) / np.float32(np.sqrt(HD))
            attn = jax.nn.softmax(scores, axis=-1)
            o = jnp.einsum('nhlm,nhmd->nhld', attn, v).transpose(2, 0, 1, 3).reshape(L, N, D)
            return o @ ow.T + ob

        def _moe(x, wg, w1, b1, w2, b2):
            L, N, _ = x.shape
            S = L * N
            cap = int(CAP_FACTOR * S) // E
            xf = x.reshape(S, D)
            gates = jax.nn.softmax(xf @ wg, axis=-1)
            idx = jnp.argmax(gates, axis=-1)
            mask1 = jax.nn.one_hot(idx, E, dtype=x.dtype)
            loc = jnp.sum((jnp.cumsum(mask1, 0) - 1.0) * mask1, -1).astype(jnp.int32)
            keep = loc < cap
            gate_val = jnp.take_along_axis(gates, idx[:, None], -1)[:, 0]
            slot = jnp.where(keep, idx.astype(jnp.int32) * cap + loc, E * cap)
            disp = jnp.zeros((E * cap, D), x.dtype).at[slot].set(xf, mode='drop')
            disp = disp.reshape(E, cap, D)
            h = jnp.einsum('ecd,edf->ecf', disp, w1) + b1[:, None, :]
            y = (jnp.einsum('ecf,efd->ecd', h, w2) + b2[:, None, :]).reshape(E * cap, D)
            out = jnp.where(keep[:, None], gate_val[:, None] * y[jnp.minimum(slot, E * cap - 1)], 0.0)
            return out.reshape(L, N, D)
        key = jax.random.key(seed)
        ks = jax.random.split(key, 8)
        L, N = (128, 16)
        s = 0.02
        return {'x': jax.random.normal(ks[0], (L, N, D), jnp.float32), 'in_proj_w': jax.random.normal(ks[1], (3 * D, D), jnp.float32) * s, 'in_proj_b': jnp.zeros((3 * D,), jnp.float32), 'out_proj_w': jax.random.normal(ks[2], (D, D), jnp.float32) * s, 'out_proj_b': jnp.zeros((D,), jnp.float32), 'ln1_g': jnp.ones((D,), jnp.float32), 'ln1_b': jnp.zeros((D,), jnp.float32), 'ln2_g': jnp.ones((D,), jnp.float32), 'ln2_b': jnp.zeros((D,), jnp.float32), 'wg': jax.random.normal(ks[3], (D, E), jnp.float32) * s, 'w1': jax.random.normal(ks[4], (E, D, FF), jnp.float32) * s, 'b1': jnp.zeros((E, FF), jnp.float32), 'w2': jax.random.normal(ks[5], (E, FF, D), jnp.float32) * s, 'b2': jnp.zeros((E, D), jnp.float32)}
    _L0_ffn_all = _L0_ffn_setup()
    _L0_ffn_in = {k: v for k, v in _L0_ffn_all.items() if k in ('in_proj_w', 'in_proj_b', 'out_proj_w', 'out_proj_b', 'ln1_g', 'ln1_b', 'ln2_g', 'ln2_b', 'wg', 'w1', 'b1', 'w2', 'b2')}
    del _L0_ffn_all

    def _L1_attn_setup():
        import jax, jax.numpy as jnp
        import numpy as np
        D_K, D_MODEL, NUM_HEADS = (64, 128, 16)

        def _xavier(key, shape):
            fan_in, fan_out = (shape[-2], shape[-1])
            limit = float(np.sqrt(6.0 / (fan_in + fan_out)))
            return jax.random.uniform(key, shape, jnp.float32, -limit, limit)
        key = jax.random.key(seed)
        kx, kq, kk, kv, ko = jax.random.split(key, 5)
        x = jax.random.normal(kx, (2, 256, D_MODEL), dtype=jnp.float32)
        w_q = _xavier(kq, (NUM_HEADS, D_MODEL, D_K))
        w_k = _xavier(kk, (NUM_HEADS, D_MODEL, D_K))
        w_v = _xavier(kv, (NUM_HEADS, D_MODEL, D_K))
        w_o = _xavier(ko, (NUM_HEADS * D_K, D_MODEL))
        return {'x': x, 'w_q': w_q, 'w_k': w_k, 'w_v': w_v, 'w_o': w_o}
    _L1_attn_all = _L1_attn_setup()
    _L1_attn_in = {k: v for k, v in _L1_attn_all.items() if k in ('w_q', 'w_k', 'w_v', 'w_o')}
    del _L1_attn_all

    def _L1_xattn_setup():
        import jax, jax.numpy as jnp
        import numpy as np
        DIM_IN, DIM_LAT, DIM_HEAD = (96, 128, 64)
        INNER = max(DIM_LAT, DIM_IN)
        HEADS = INNER // DIM_HEAD
        SCALE = DIM_HEAD ** (-0.5)
        RMS_EPS = 1e-08
        LN_EPS = 1e-05

        def layernorm(x, g, b):
            mu = jnp.mean(x, axis=-1, keepdims=True)
            var = jnp.mean((x - mu) ** 2, axis=-1, keepdims=True)
            return (x - mu) * jax.lax.rsqrt(var + LN_EPS) * g + b

        def rmsnorm(x, gamma):
            norm = jnp.sqrt(jnp.sum(x * x, axis=-1, keepdims=True)) * x.shape[-1] ** (-0.5)
            return x / jnp.maximum(norm, RMS_EPS) * gamma
        key = jax.random.key(seed)
        ks = jax.random.split(key, 12)
        b, n, m = (4, 512, 64)
        x = jax.random.normal(ks[0], (b, n, DIM_IN), jnp.float32)
        latents = jax.random.normal(ks[1], (b, m, DIM_LAT), jnp.float32)
        mask = jax.random.randint(ks[2], (b, n), 0, 2).astype(bool)
        s = lambda k, sh, fan: jax.random.normal(k, sh, jnp.float32) * fan ** (-0.5)
        return {'x': x, 'latents': latents, 'mask': mask, 'ln_x_g': jnp.ones((DIM_IN,), jnp.float32), 'ln_x_b': jnp.zeros((DIM_IN,), jnp.float32), 'ln_l_g': jnp.ones((DIM_LAT,), jnp.float32), 'ln_l_b': jnp.zeros((DIM_LAT,), jnp.float32), 'qn_g': jnp.ones((DIM_HEAD,), jnp.float32), 'kn_g': jnp.ones((DIM_HEAD,), jnp.float32), 'Wq': s(ks[3], (INNER, DIM_LAT), DIM_LAT), 'Wkv': s(ks[4], (2 * INNER, DIM_IN), DIM_IN), 'Wlkv': s(ks[5], (2 * INNER, DIM_LAT), DIM_LAT), 'Wo': s(ks[6], (DIM_LAT, INNER), INNER), 'bo': jnp.zeros((DIM_LAT,), jnp.float32)}
    _L1_xattn_all = _L1_xattn_setup()
    _L1_xattn_in = {k: v for k, v in _L1_xattn_all.items() if k in ('ln_x_g', 'ln_x_b', 'ln_l_g', 'ln_l_b', 'qn_g', 'kn_g', 'Wq', 'Wkv', 'Wlkv', 'Wo', 'bo')}
    del _L1_xattn_all

    def _L1_ffn_setup():
        import jax, jax.numpy as jnp
        import numpy as np
        B, S, D = (2, 256, 128)
        E, H, K = (8, 704, 2)
        N_RESERVED = 4
        key = jax.random.key(seed)
        ks = jax.random.split(key, 5)
        scale = 0.02
        x = jax.random.normal(ks[0], (B, S, D), dtype=jnp.float32)
        gate_w = jax.random.normal(ks[1], (E, D), dtype=jnp.float32) * scale
        w1 = jax.random.normal(ks[2], (E, D, H), dtype=jnp.float32) * scale
        w3 = jax.random.normal(ks[3], (E, D, H), dtype=jnp.float32) * scale
        w2 = jax.random.normal(ks[4], (E, H, D), dtype=jnp.float32) * scale
        return {'x': x, 'gate_w': gate_w, 'w1': w1, 'w2': w2, 'w3': w3}
    _L1_ffn_all = _L1_ffn_setup()
    _L1_ffn_in = {k: v for k, v in _L1_ffn_all.items() if k in ('gate_w', 'w1', 'w2', 'w3')}
    del _L1_ffn_all
    return {'x': x, 'ctx_768': ctx_768, 'mask_BxS_bf1': mask_BxS_bf1, 'mask_BxS2_bf1': mask_BxS2_bf1, 'mask_BxS2_bk0': mask_BxS2_bk0, 'L0_attn_lower_bound': _L0_attn_in['lower_bound'], 'L0_attn_W_in': _L0_attn_in['W_in'], 'L0_attn_W_out': _L0_attn_in['W_out'], 'L0_xattn_Wq': _L0_xattn_in['Wq'], 'L0_xattn_Wk': _L0_xattn_in['Wk'], 'L0_xattn_Wv': _L0_xattn_in['Wv'], 'L0_xattn_W_film_in': _L0_xattn_in['W_film_in'], 'L0_xattn_b_film_in': _L0_xattn_in['b_film_in'], 'L0_xattn_W_film_out': _L0_xattn_in['W_film_out'], 'L0_xattn_b_film_out': _L0_xattn_in['b_film_out'], 'L0_xattn_g_norm_in': _L0_xattn_in['g_norm_in'], 'L0_xattn_b_norm_in': _L0_xattn_in['b_norm_in'], 'L0_xattn_g_norm_out': _L0_xattn_in['g_norm_out'], 'L0_xattn_b_norm_out': _L0_xattn_in['b_norm_out'], 'L0_xattn_g_ffn': _L0_xattn_in['g_ffn'], 'L0_xattn_b_ffn': _L0_xattn_in['b_ffn'], 'L0_xattn_W1': _L0_xattn_in['W1'], 'L0_xattn_b1': _L0_xattn_in['b1'], 'L0_xattn_W2': _L0_xattn_in['W2'], 'L0_xattn_b2': _L0_xattn_in['b2'], 'L0_xattn_log_dt': _L0_xattn_in['log_dt'], 'L0_xattn_A_re': _L0_xattn_in['A_re'], 'L0_xattn_A_im': _L0_xattn_in['A_im'], 'L0_xattn_C_re': _L0_xattn_in['C_re'], 'L0_xattn_C_im': _L0_xattn_in['C_im'], 'L0_xattn_D_skip': _L0_xattn_in['D_skip'], 'L0_xattn_mod_gate': _L0_xattn_in['mod_gate'], 'L0_ffn_in_proj_w': _L0_ffn_in['in_proj_w'], 'L0_ffn_in_proj_b': _L0_ffn_in['in_proj_b'], 'L0_ffn_out_proj_w': _L0_ffn_in['out_proj_w'], 'L0_ffn_out_proj_b': _L0_ffn_in['out_proj_b'], 'L0_ffn_ln1_g': _L0_ffn_in['ln1_g'], 'L0_ffn_ln1_b': _L0_ffn_in['ln1_b'], 'L0_ffn_ln2_g': _L0_ffn_in['ln2_g'], 'L0_ffn_ln2_b': _L0_ffn_in['ln2_b'], 'L0_ffn_wg': _L0_ffn_in['wg'], 'L0_ffn_w1': _L0_ffn_in['w1'], 'L0_ffn_b1': _L0_ffn_in['b1'], 'L0_ffn_w2': _L0_ffn_in['w2'], 'L0_ffn_b2': _L0_ffn_in['b2'], 'L1_attn_w_q': _L1_attn_in['w_q'], 'L1_attn_w_k': _L1_attn_in['w_k'], 'L1_attn_w_v': _L1_attn_in['w_v'], 'L1_attn_w_o': _L1_attn_in['w_o'], 'L1_xattn_ln_x_g': _L1_xattn_in['ln_x_g'], 'L1_xattn_ln_x_b': _L1_xattn_in['ln_x_b'], 'L1_xattn_ln_l_g': _L1_xattn_in['ln_l_g'], 'L1_xattn_ln_l_b': _L1_xattn_in['ln_l_b'], 'L1_xattn_qn_g': _L1_xattn_in['qn_g'], 'L1_xattn_kn_g': _L1_xattn_in['kn_g'], 'L1_xattn_Wq': _L1_xattn_in['Wq'], 'L1_xattn_Wkv': _L1_xattn_in['Wkv'], 'L1_xattn_Wlkv': _L1_xattn_in['Wlkv'], 'L1_xattn_Wo': _L1_xattn_in['Wo'], 'L1_xattn_bo': _L1_xattn_in['bo'], 'L1_ffn_gate_w': _L1_ffn_in['gate_w'], 'L1_ffn_w1': _L1_ffn_in['w1'], 'L1_ffn_w2': _L1_ffn_in['w2'], 'L1_ffn_w3': _L1_ffn_in['w3']}

def reference(x, ctx_768, mask_BxS_bf1, mask_BxS2_bf1, mask_BxS2_bk0, L0_attn_lower_bound, L0_attn_W_in, L0_attn_W_out, L0_xattn_Wq, L0_xattn_Wk, L0_xattn_Wv, L0_xattn_W_film_in, L0_xattn_b_film_in, L0_xattn_W_film_out, L0_xattn_b_film_out, L0_xattn_g_norm_in, L0_xattn_b_norm_in, L0_xattn_g_norm_out, L0_xattn_b_norm_out, L0_xattn_g_ffn, L0_xattn_b_ffn, L0_xattn_W1, L0_xattn_b1, L0_xattn_W2, L0_xattn_b2, L0_xattn_log_dt, L0_xattn_A_re, L0_xattn_A_im, L0_xattn_C_re, L0_xattn_C_im, L0_xattn_D_skip, L0_xattn_mod_gate, L0_ffn_in_proj_w, L0_ffn_in_proj_b, L0_ffn_out_proj_w, L0_ffn_out_proj_b, L0_ffn_ln1_g, L0_ffn_ln1_b, L0_ffn_ln2_g, L0_ffn_ln2_b, L0_ffn_wg, L0_ffn_w1, L0_ffn_b1, L0_ffn_w2, L0_ffn_b2, L1_attn_w_q, L1_attn_w_k, L1_attn_w_v, L1_attn_w_o, L1_xattn_ln_x_g, L1_xattn_ln_x_b, L1_xattn_ln_l_g, L1_xattn_ln_l_b, L1_xattn_qn_g, L1_xattn_kn_g, L1_xattn_Wq, L1_xattn_Wkv, L1_xattn_Wlkv, L1_xattn_Wo, L1_xattn_bo, L1_ffn_gate_w, L1_ffn_w1, L1_ffn_w2, L1_ffn_w3):
    import jax
    import jax.numpy as jnp

    def _L0_attn_ref(x, lower_bound, W_in, W_out):
        import jax, jax.numpy as jnp
        import numpy as np
        EXPAND = 2
        n, b, d = x.shape
        e = EXPAND
        h = d // e
        feat = x @ W_in
        V, Q, Fg = jnp.split(feat, 3, axis=-1)
        V = jax.nn.gelu(V, approximate=False)
        Q = jax.nn.gelu(Q, approximate=False)
        Fg = jax.nn.sigmoid(Fg)
        V = V.reshape(n, b, h, e)
        Q = Q.reshape(n, b, h, e)
        Fg = Fg.reshape(n, b, h, e)
        lb = lower_bound.reshape(h, e)
        lam = lb + (1.0 - lb) * Fg
        K = 1.0 - lam

        def step(S, inp):
            lam_t, k_t, v_t, q_t = inp
            S = lam_t[..., :, None] * S + k_t[..., :, None] * v_t[..., None, :]
            o_t = jnp.einsum('bhk,bhkv->bhv', q_t, S)
            return (S, o_t)
        S0 = jnp.zeros((b, h, e, e), dtype=x.dtype)
        _, o = jax.lax.scan(step, S0, (lam, K, V, Q))
        o = o.reshape(n, b, d)
        return o @ W_out

    def _L0_xattn_ref(x_text, x_vision, text_mask, vision_mask, Wq, Wk, Wv, W_film_in, b_film_in, W_film_out, b_film_out, g_norm_in, b_norm_in, g_norm_out, b_norm_out, g_ffn, b_ffn, W1, b1, W2, b2, log_dt, A_re, A_im, C_re, C_im, D_skip, mod_gate):
        import jax, jax.numpy as jnp
        import numpy as np
        B, T, DT, G, DV = (16, 64, 128, 72, 96)
        H, DH = (4, 32)
        INNER = H * DH
        HID = 4 * DT
        N_STATE = 64
        K_TOP = 32

        def layernorm(x, g, b, eps=1e-05):
            m = x.mean(-1, keepdims=True)
            v = x.var(-1, keepdims=True)
            return (x - m) * jax.lax.rsqrt(v + eps) * g + b

        def s4d(x, log_dt, A_re, A_im, C_re, C_im, D_skip):
            Bb, L, D = x.shape
            dt = jnp.exp(log_dt)
            A = A_re + 1j * A_im
            C = C_re + 1j * C_im
            dtA = dt[:, None] * A
            dC = C * (jnp.exp(dtA) - 1.0) / A
            powers = jnp.exp(dtA[:, :, None] * jnp.arange(L))
            K = 2.0 * jnp.einsum('dn,dnl->dl', dC, powers).real
            n = 2 * L
            Kf = jnp.fft.rfft(K, n=n, axis=-1)
            xf = jnp.fft.rfft(x, n=n, axis=1)
            y = jnp.fft.irfft(xf * Kf.T[None], n=n, axis=1)[:, :L]
            return y + x * D_skip
        Bb, Tt, D = x_text.shape
        Gg = x_vision.shape[1]
        Q = (x_text @ Wq).reshape(Bb, Tt, H, DH)
        K = (x_vision @ Wk).reshape(Bb, Gg, H, DH)
        scores = jnp.einsum('bthd,bghd->bhtg', Q, K) / np.sqrt(DH).astype(np.float32)
        scores = jnp.where(vision_mask[:, None, None, :], scores, -jnp.inf)
        topv, topi = jax.lax.top_k(scores, K_TOP)
        probs = jax.nn.softmax(topv, axis=-1)
        bi = jnp.arange(Bb)[:, None, None, None]
        hi = jnp.arange(H)[None, :, None, None]
        ti = jnp.arange(Tt)[None, None, :, None]
        attn = jnp.zeros_like(scores).at[bi, hi, ti, topi].set(probs)
        attn_mean = attn.mean(axis=1)
        V = x_vision @ Wv
        c_t = jnp.einsum('btg,bgd->btd', attn_mean, V)
        c_t = c_t * text_mask[..., None]
        x = layernorm(x_text, g_norm_in, b_norm_in)
        scale_in, shift_in = jnp.split(c_t @ W_film_in + b_film_in, 2, axis=-1)
        x = x * (1.0 + mod_gate * scale_in) + mod_gate * shift_in
        y = s4d(x, log_dt, A_re, A_im, C_re, C_im, D_skip)
        scale_out, shift_out = jnp.split(c_t @ W_film_out + b_film_out, 2, axis=-1)
        y = y * (1.0 + mod_gate * scale_out) + mod_gate * shift_out
        xt = x_text + y
        h = layernorm(xt, g_ffn, b_ffn)
        h = jax.nn.gelu(h @ W1 + b1, approximate=False) @ W2 + b2
        xt = xt + h
        return layernorm(xt, g_norm_out, b_norm_out)

    def _L0_ffn_ref(x, in_proj_w, in_proj_b, out_proj_w, out_proj_b, ln1_g, ln1_b, ln2_g, ln2_b, wg, w1, b1, w2, b2):
        import jax, jax.numpy as jnp
        import numpy as np
        D = 128
        H = 4
        HD = D // H
        E = 8
        FF = 512
        CAP_FACTOR = 1.0

        def _ln(x, g, b, eps=1e-05):
            mu = jnp.mean(x, -1, keepdims=True)
            v = jnp.mean((x - mu) ** 2, -1, keepdims=True)
            return (x - mu) * jax.lax.rsqrt(v + eps) * g + b

        def _mha(x, w, b, ow, ob):
            L, N, _ = x.shape
            qkv = x @ w.T + b
            q, k, v = jnp.split(qkv, 3, axis=-1)
            rh = lambda t: t.reshape(L, N, H, HD).transpose(1, 2, 0, 3)
            q, k, v = (rh(q), rh(k), rh(v))
            scores = jnp.einsum('nhld,nhmd->nhlm', q, k) / np.float32(np.sqrt(HD))
            attn = jax.nn.softmax(scores, axis=-1)
            o = jnp.einsum('nhlm,nhmd->nhld', attn, v).transpose(2, 0, 1, 3).reshape(L, N, D)
            return o @ ow.T + ob

        def _moe(x, wg, w1, b1, w2, b2):
            L, N, _ = x.shape
            S = L * N
            cap = int(CAP_FACTOR * S) // E
            xf = x.reshape(S, D)
            gates = jax.nn.softmax(xf @ wg, axis=-1)
            idx = jnp.argmax(gates, axis=-1)
            mask1 = jax.nn.one_hot(idx, E, dtype=x.dtype)
            loc = jnp.sum((jnp.cumsum(mask1, 0) - 1.0) * mask1, -1).astype(jnp.int32)
            keep = loc < cap
            gate_val = jnp.take_along_axis(gates, idx[:, None], -1)[:, 0]
            slot = jnp.where(keep, idx.astype(jnp.int32) * cap + loc, E * cap)
            disp = jnp.zeros((E * cap, D), x.dtype).at[slot].set(xf, mode='drop')
            disp = disp.reshape(E, cap, D)
            h = jnp.einsum('ecd,edf->ecf', disp, w1) + b1[:, None, :]
            y = (jnp.einsum('ecf,efd->ecd', h, w2) + b2[:, None, :]).reshape(E * cap, D)
            out = jnp.where(keep[:, None], gate_val[:, None] * y[jnp.minimum(slot, E * cap - 1)], 0.0)
            return out.reshape(L, N, D)
        y1 = _ln(x + _mha(x, in_proj_w, in_proj_b, out_proj_w, out_proj_b), ln1_g, ln1_b)
        y2 = _ln(y1 + _moe(y1, wg, w1, b1, w2, b2), ln2_g, ln2_b)
        return y2

    def _L1_attn_ref(x, w_q, w_k, w_v, w_o):
        import jax, jax.numpy as jnp
        import numpy as np
        D_K, D_MODEL, NUM_HEADS = (64, 128, 16)

        def _xavier(key, shape):
            fan_in, fan_out = (shape[-2], shape[-1])
            limit = float(np.sqrt(6.0 / (fan_in + fan_out)))
            return jax.random.uniform(key, shape, jnp.float32, -limit, limit)
        scale = 1.0 / jnp.sqrt(jnp.asarray(D_K, dtype=jnp.float32))
        q = jnp.einsum('bsd,hdk->bhsk', x, w_q)
        k = jnp.einsum('bsd,hdk->bhsk', x, w_k)
        v = jnp.einsum('bsd,hdk->bhsk', x, w_v)
        scores = jnp.einsum('bhqk,bhmk->bhqm', q, k) * scale
        weights = jax.nn.softmax(scores, axis=-1)
        z = jnp.einsum('bhqm,bhmk->bhqk', weights, v)
        b, h, s, dk = z.shape
        z = jnp.transpose(z, (0, 2, 1, 3)).reshape(b, s, h * dk)
        z = jnp.einsum('bse,ed->bsd', z, w_o)
        return x + z

    def _L1_xattn_ref(x, latents, mask, ln_x_g, ln_x_b, ln_l_g, ln_l_b, qn_g, kn_g, Wq, Wkv, Wlkv, Wo, bo):
        import jax, jax.numpy as jnp
        import numpy as np
        DIM_IN, DIM_LAT, DIM_HEAD = (96, 128, 64)
        INNER = max(DIM_LAT, DIM_IN)
        HEADS = INNER // DIM_HEAD
        SCALE = DIM_HEAD ** (-0.5)
        RMS_EPS = 1e-08
        LN_EPS = 1e-05

        def layernorm(x, g, b):
            mu = jnp.mean(x, axis=-1, keepdims=True)
            var = jnp.mean((x - mu) ** 2, axis=-1, keepdims=True)
            return (x - mu) * jax.lax.rsqrt(var + LN_EPS) * g + b

        def rmsnorm(x, gamma):
            norm = jnp.sqrt(jnp.sum(x * x, axis=-1, keepdims=True)) * x.shape[-1] ** (-0.5)
            return x / jnp.maximum(norm, RMS_EPS) * gamma
        b, n, _ = x.shape
        m = latents.shape[1]
        xn = layernorm(x, ln_x_g, ln_x_b)
        ln = layernorm(latents, ln_l_g, ln_l_b)
        q = ln @ Wq.T
        kv = jnp.concatenate([xn @ Wkv.T, ln @ Wlkv.T], axis=1)
        k, v = (kv[..., :INNER], kv[..., INNER:])
        split_heads = lambda t: t.reshape(t.shape[0], t.shape[1], HEADS, DIM_HEAD).transpose(0, 2, 1, 3)
        q, k, v = (split_heads(q), split_heads(k), split_heads(v))
        qn = rmsnorm(q, qn_g) * SCALE
        kn = rmsnorm(k, kn_g)
        attn = jnp.einsum('bhid,bhjd->bhij', qn, kn)
        full_mask = jnp.pad(mask, ((0, 0), (0, m)), constant_values=True)
        attn = jnp.where(full_mask[:, None, None, :], attn, -jnp.finfo(attn.dtype).max)
        attn = jax.nn.softmax(attn, axis=-1)
        out = jnp.einsum('bhij,bhjd->bhid', attn, v)
        out = out.transpose(0, 2, 1, 3).reshape(b, m, INNER)
        return out @ Wo.T + bo

    def _L1_ffn_ref(x, gate_w, w1, w2, w3):
        import jax, jax.numpy as jnp
        import numpy as np
        B, S, D = (2, 256, 128)
        E, H, K = (8, 704, 2)
        N_RESERVED = 4
        b, s, d = x.shape
        T = b * s
        xf = x.reshape(T, d)
        logits = xf @ gate_w.T
        expert_ids = jnp.arange(E)
        logits = jnp.where(expert_ids[None, :] >= E - N_RESERVED, -jnp.inf, logits)
        weights = jax.nn.softmax(logits, axis=-1)
        top_w, top_idx = jax.lax.top_k(weights, K)
        top_w = top_w / jnp.sum(top_w, axis=-1, keepdims=True)
        cw = jnp.zeros((T, E), dtype=x.dtype).at[jnp.arange(T)[:, None], top_idx].add(top_w)
        h = jax.nn.silu(jnp.einsum('td,edh->teh', xf, w1)) * jnp.einsum('td,edh->teh', xf, w3)
        y = jnp.einsum('teh,ehd->ted', h, w2)
        out = jnp.einsum('te,ted->td', cw, y)
        return out.reshape(b, s, d)
    x = _layernorm(x + _L0_attn_ref(x, L0_attn_lower_bound, L0_attn_W_in, L0_attn_W_out), axis=-1)
    x = _layernorm(x + _L0_xattn_ref(x, ctx_768, mask_BxS_bf1, mask_BxS2_bf1, L0_xattn_Wq, L0_xattn_Wk, L0_xattn_Wv, L0_xattn_W_film_in, L0_xattn_b_film_in, L0_xattn_W_film_out, L0_xattn_b_film_out, L0_xattn_g_norm_in, L0_xattn_b_norm_in, L0_xattn_g_norm_out, L0_xattn_b_norm_out, L0_xattn_g_ffn, L0_xattn_b_ffn, L0_xattn_W1, L0_xattn_b1, L0_xattn_W2, L0_xattn_b2, L0_xattn_log_dt, L0_xattn_A_re, L0_xattn_A_im, L0_xattn_C_re, L0_xattn_C_im, L0_xattn_D_skip, L0_xattn_mod_gate), axis=-1)
    x = _layernorm(x + _L0_ffn_ref(x, L0_ffn_in_proj_w, L0_ffn_in_proj_b, L0_ffn_out_proj_w, L0_ffn_out_proj_b, L0_ffn_ln1_g, L0_ffn_ln1_b, L0_ffn_ln2_g, L0_ffn_ln2_b, L0_ffn_wg, L0_ffn_w1, L0_ffn_b1, L0_ffn_w2, L0_ffn_b2), axis=-1)
    x = _layernorm(x + _L1_attn_ref(x, L1_attn_w_q, L1_attn_w_k, L1_attn_w_v, L1_attn_w_o), axis=-1)
    x = _layernorm(x + _L1_xattn_ref(ctx_768, x, mask_BxS2_bk0, L1_xattn_ln_x_g, L1_xattn_ln_x_b, L1_xattn_ln_l_g, L1_xattn_ln_l_b, L1_xattn_qn_g, L1_xattn_kn_g, L1_xattn_Wq, L1_xattn_Wkv, L1_xattn_Wlkv, L1_xattn_Wo, L1_xattn_bo), axis=-1)
    x = _layernorm(x + _L1_ffn_ref(x, L1_ffn_gate_w, L1_ffn_w1, L1_ffn_w2, L1_ffn_w3), axis=-1)
    return x

_drawn_inputs = setup_inputs


def setup_inputs(seed=0):
    import zlib

    import numpy as np

    out = dict(_drawn_inputs(seed))
    spreads = {'L0_attn_lower_bound': (0.0, 0.268),
     'L0_xattn_b_film_in': (0.0, 0.1),
     'L0_xattn_b_film_out': (0.0, 0.1),
     'L0_xattn_g_norm_in': (1.0, 0.2),
     'L0_xattn_b_norm_in': (0.0, 0.1),
     'L0_xattn_g_norm_out': (1.0, 0.2),
     'L0_xattn_b_norm_out': (0.0, 0.1),
     'L0_xattn_g_ffn': (1.0, 0.6),
     'L0_xattn_b_ffn': (0.0, 0.8),
     'L0_xattn_b1': (0.0, 0.8),
     'L0_xattn_b2': (0.0, 0.1),
     'L0_xattn_A_re': (-0.5, 0.2),
     'L0_ffn_in_proj_b': (0.0, 0.403),
     'L0_ffn_out_proj_b': (0.0, 0.1),
     'L0_ffn_ln1_g': (1.0, 0.2),
     'L0_ffn_ln1_b': (0.0, 0.1),
     'L0_ffn_ln2_g': (1.0, 0.2),
     'L0_ffn_ln2_b': (0.0, 0.1),
     'L0_ffn_b1': (0.0, 0.8),
     'L0_ffn_b2': (0.0, 0.8),
     'L1_xattn_ln_x_g': (1.0, 0.6),
     'L1_xattn_ln_x_b': (0.0, 0.729),
     'L1_xattn_ln_l_g': (1.0, 0.2),
     'L1_xattn_ln_l_b': (0.0, 0.1),
     'L1_xattn_qn_g': (1.0, 0.543),
     'L1_xattn_kn_g': (1.0, 0.2),
     'L1_xattn_bo': (0.0, 0.1)}
    factors = {'L0_xattn_Wq': 8.0,
     'L0_xattn_Wk': 8.0,
     'L0_xattn_Wv': 3.518,
     'L0_xattn_W_film_in': 4.238,
     'L0_xattn_W_film_out': 7.175,
     'L0_xattn_W1': 3.262,
     'L0_xattn_W2': 2.706,
     'L0_ffn_in_proj_w': 2.885,
     'L0_ffn_wg': 5.154,
     'L0_ffn_w1': 6.838,
     'L0_ffn_w2': 6.198,
     'L1_ffn_gate_w': 8.0,
     'L1_ffn_w1': 5.862,
     'L1_ffn_w2': 5.822,
     'L1_ffn_w3': 5.827}
    for name, (base, spread) in spreads.items():
        noise = np.random.default_rng([zlib.crc32(name.encode()), seed]).standard_normal(out[name].shape)
        drawn = base * np.exp(spread * noise) if base else spread * noise
        out[name] = jnp.asarray(drawn.astype(out[name].dtype))
    for name, factor in factors.items():
        out[name] = (out[name] * factor).astype(out[name].dtype)
    return out
```

```python
from contextlib import ExitStack

import concourse.bass as bass
import numpy as np
from concourse import mybir

F32 = mybir.dt.float32
BF16 = mybir.dt.bfloat16
U8 = mybir.dt.uint8
ALU = mybir.AluOpType
ACT = mybir.ActivationFunctionType
AX_X = mybir.AxisListType.X

P = 128
B, S, D = 2, 512, 128
T = B * S
NT = T // P
S2, DC = 154, 96
REST = S2 - P
EPS = 1e-5
NEG = -1.0e30
GONE = -3.0e38
MAGIC = 12582912.0
TWO_PI = 6.2831845
H_X, DH_X, TOP = 4, 32, 32
N_ST, LOW, HIGH = 64, 32, 16
FF0, E0, CAP = 512, 8, 128
H_L, DK = 16, 64
PAIRS = H_L // 2
H_C = 2
KEYS = S2 + S
E1, E1_LIVE, FF1 = 8, 4, 704
FCH = 6

PACK_MIX = [("xT", T), ("W_in", 384), ("lower", 1), ("ident", 128), ("pair_sum", 128), ("x", T), ("W_out", 128)]
PACK_SSM = [("A_re", N_ST), ("A_im", N_ST), ("C_re", N_ST), ("C_im", N_ST), ("log_dt", 1), ("low_lags", LOW),
            ("high_lags", HIGH), ("quarter", 1), ("quarter_angle", 1), ("bin_weight", 4), ("Wq_T", 128), ("Wk", 128),
            ("Wv", 128), ("ctx_T", B * S2), ("W_film", 512)]
PACK_DFT = [("dft_cos", 2048), ("dft_sin", 2048), ("inv_sin0", 512)]
PACK_FFN = [("W1", 512), ("W2", 512), ("ffn_b1", 4), ("ffn_g", 1), ("ffn_b", 1)]
PACK_MOE = [("m_w1T", 4096), ("m_w2", 4096)]
PACK_MHA = [("m_b1", 256), ("qkv_T", 384), ("ow_T", 128), ("m_wg", 8), ("b_q", 1), ("b_v", 1), ("ln1_g", 1),
            ("ln1_b", 1), ("head_sum", 128), ("earlier", 128), ("m_b2", 128)]
PACK_ATT = [("w_q", 1024), ("w_k", 1024), ("w_v", 1024), ("w_o", 1024), ("head_pick", 256)]
PACK_LAT = [("expert_rank", 8), ("l_WkvT", 256), ("l_WqT", 128), ("l_WlkvT", 256), ("l_WoT", 128), ("ctx", 4 * DC), ("lx_g", 1),
            ("lx_b", 1), ("ll_g", 1), ("ll_b", 1), ("qn_g", 1), ("kn_g", 1), ("gate_T", E1_LIVE)]
PACK_EXP = [("e_w1", E1_LIVE * FF1), ("e_w3", E1_LIVE * FF1), ("e_w2", E1_LIVE * FCH * 128)]
ROWS = ["g_in", "b_in", "g_out", "b_out", "n1_g", "n1_b", "n2_g", "n2_b"]
LINES = [("ffn_b2", 128), ("m_ob", 128), ("l_bo", 128), ("b_film", 512)]


def width(pack):
    return sum(n for _, n in pack)


def views(pack, ap):
    out, at = {}, 0
    for name, n in pack:
        out[name] = ap[:, at:at + n]
        at += n
    return out


PACKS = {"mix": PACK_MIX, "ssm": PACK_SSM, "dft": PACK_DFT, "ffn": PACK_FFN, "moe": PACK_MOE, "mha": PACK_MHA,
         "att": PACK_ATT, "lat": PACK_LAT, "exp": PACK_EXP}


def build(nc, dram):
    with ExitStack() as ctx:
        _build(nc, dram, ctx)


def _build(nc, dram, ctx):
    semaphores = {}

    def sem(name):
        if name not in semaphores:
            semaphores[name] = ctx.enter_context(nc.semaphore(name))
        return semaphores[name]

    SB = ctx.enter_context(nc.sbuf_tensor("SB", [P, 53200], F32))
    PS = ctx.enter_context(nc.psum_tensor("PS", [P, 4096], F32))

    def bank(i, n=1):
        return PS[:, 512 * i:512 * (i + n)]

    class Space:

        def __init__(self, at, end):
            self.at, self.end = at, end

        def __call__(self, n, dtype=F32):
            a = SB[:, self.at:self.at + n]
            self.at += n
            assert self.at <= self.end, (self.at, self.end)
            return a if dtype == F32 else a.bitcast(dtype)

    def tiled(a, n=NT):
        return a.rearrange("p (t d) -> p t d", t=n)

    keep = Space(0, 7200)
    mix = views(PACK_MIX, keep(width(PACK_MIX)))
    lat = views(PACK_LAT, keep(width(PACK_LAT)))
    rows = {name: keep(128) for name in ROWS}
    lines = views(LINES, keep(sum(n for _, n in LINES)))
    mod_gate, text_mask = keep(1), keep(NT)
    ones, minus_half, stats, moments = keep(128), keep(40), keep(NT * 6), keep(NT * 2)
    variance, rstd = keep(NT), keep(NT)
    bytes_in = keep(1000).bitcast(U8)
    text_bytes, ctx_bytes, key_bytes = bytes_in[:, 0:NT], bytes_in[0:1, 1024:1024 + B * S2], bytes_in[0:1, 2048:2048 + B * S2]
    stream = Space(keep.at, keep.at + 4096)
    xs, xsT, xn, xsum = (stream(T) for _ in range(4))
    W = Space(stream.at, stream.at + 8792)
    ssm, dft, ffn = (views(pk, W(width(pk))) for pk in (PACK_SSM, PACK_DFT, PACK_FFN))
    exp_w = views(PACK_EXP, Space(stream.at, stream.at + 8792)(width(PACK_EXP)))
    W2 = Space(W.end, W.end + width(PACK_ATT))
    att = views(PACK_ATT, W2(width(PACK_ATT)))
    free_at = W2.end
    END = 53200
    ident = mix["ident"]

    def chain(engine, name):
        done = sem(name)
        count = [0]

        def follow(ins):
            count[0] += 1
            ins.then_inc(done, 1)
            engine.wait_ge(done, count[0])
        return follow

    norms = [0, 0]

    def norm_stats(dve, follow, src, n=NT):
        norms[0] += 1
        k = norms[0]
        for t in range(n):
            ins = dve.bn_stats(tiled(stats)[:, t, :], src[:, t, :])
        follow(ins)
        for t in range(n):
            ins = dve.bn_aggr(moments.rearrange("p (t m) -> p t m", m=2)[:, t, :], tiled(stats)[:, t, :])
        follow(ins)
        dve.tensor_scalar(variance[:, 0:n], moments.rearrange("p (t m) -> p m t", m=2)[:, 1, 0:n], EPS, None,
                          ALU.add).then_inc(sem("norm_variance"), 1)
        dve.wait_ge(sem("norm_rstd"), k)

    def norm_apply(dve, src, out, n=NT):
        for t in range(n):
            ins = dve.tensor_scalar(out[:, t, :], src[:, t, :], moments[:, 2 * t:2 * t + 1], rstd[:, t:t + 1],
                                    ALU.subtract, ALU.mult)
        return ins

    def pool_rstd(pool):
        norms[1] += 1
        pool.wait_ge(sem("norm_variance"), norms[1])
        pool.tensor_tensor(rstd, variance, minus_half[:, 0:NT], ALU.pow).then_inc(sem("norm_rstd"), 1)

    turns = [0, 0, 0]

    def turn_pe(pe, src, b0, wait):
        turns[0] += 1
        if wait is not None:
            pe.wait_ge(*wait)
        for t in range(NT):
            ins = pe.transpose(PS[:, 512 * b0 + 128 * t:512 * b0 + 128 * t + 128], src[:, t, :], ident)
        ins.then_inc(sem("turned"), 1)

    A = Space(END - 7 * T - 1, END)
    gate_v, gate_q, forget, keys, qk, carried, mixed = (A(T) for _ in range(7))
    one_less = A(1)

    def a_sp(sp):
        sp.dma_start(SB[:, 0:T + 384 + 129], dram["mix"][:, 0:T + 384 + 129]).then_inc(sem("mix_in"), 16)
        sp.dma_start(SB[:, T + 513:width(PACK_MIX)], dram["mix"][:, T + 513:]).then_inc(sem("mix_in2"), 16)
        a0 = W.end - 8792
        sp.dma_start(SB[:, a0:a0 + width(PACK_SSM)], dram["ssm"]).then_inc(sem("ssm_in"), 16)
        r0 = width(PACK_MIX) + width(PACK_LAT)
        sp.dma_start(SB[:, r0:r0 + 1024], dram["rows"].to_broadcast([P, 8 * D])).then_inc(sem("small_in"), 16)
        sp.dma_start(SB[0:1, r0 + 1024:r0 + 1024 + 896], dram["lines"]).then_inc(sem("small_in"), 16)
        sp.dma_start(mod_gate, dram["mod_gate"].to_broadcast([P, 1])).then_inc(sem("small_in"), 16)
        sp.dma_start(text_bytes, dram["text_mask"]).then_inc(sem("small_in"), 16)
        sp.dma_start(ctx_bytes, dram["ctx_mask"]).then_inc(sem("small_in"), 16)
        sp.dma_start(key_bytes, dram["key_mask"]).then_inc(sem("small_in"), 16)
        sp.dma_start(film_line, dram["lines"][:, 384:896]).then_inc(sem("small_in"), 16)
        sp.dma_start(skip_line, dram["d_skip"]).then_inc(sem("small_in"), 16)
        a1 = a0 + width(PACK_SSM)
        sp.dma_start(SB[:, a1:a1 + width(PACK_DFT)], dram["dft"]).then_inc(sem("dft_in"), 16)
        a2 = a1 + width(PACK_DFT)
        sp.dma_start(SB[:, a2:a2 + width(PACK_FFN)], dram["ffn"]).then_inc(sem("ffn_in"), 16)
        sp.dma_start(SB[:, W2.end - width(PACK_ATT):W2.end], dram["att"]).then_inc(sem("att_in"), 16)
        l0 = width(PACK_MIX)
        sp.dma_start(SB[:, l0:l0 + width(PACK_LAT)], dram["lat"]).then_inc(sem("lat_in"), 16)

    SMALL = 16 * 8

    def a_pe(pe):
        pe.wait_ge(sem("mix_in"), 16)
        for m in range(3):
            for n in range(2):
                pe.matmul(bank(2 * m + n), mix["W_in"][:, 128 * m:128 * m + 128], mix["xT"][:, 512 * n:512 * n + 512],
                          start=True, stop=True).then_inc(sem("a_features"), 1)
        pe.wait_ge(sem("mix_in2"), 16)
        pe.wait_ge(sem("a_products"), 1)
        for n in range(2):
            pe.matmul(bank(6 + n), mix["pair_sum"], qk[:, 512 * n:512 * n + 512], start=True, stop=True)
        pe.wait_ge(sem("a_products"), 2)
        pe.matmul(bank(0), mix["pair_sum"], carried[:, 512:1024], start=True, stop=True).then_inc(sem("a_sums"), 1)
        pe.wait_ge(sem("a_mixed"), 1)
        for t in range(NT):
            ins = pe.matmul(PS[:, 1024 + 128 * t:1024 + 128 * t + 128], mixed[:, 128 * t:128 * t + 128], mix["W_out"],
                            start=True, stop=True)
        ins.then_inc(sem("a_out"), 1)

    def a_act(act):
        act.wait_ge(sem("a_features"), 2)
        act.activation(gate_v, bank(0, 2), ACT.Gelu).then_inc(sem("a_gates"), 1)
        act.wait_ge(sem("a_features"), 4)
        act.activation(gate_q, bank(2, 2), ACT.Gelu).then_inc(sem("a_gates"), 1)
        act.wait_ge(sem("a_features"), 6)
        act.activation(forget, bank(4, 2), ACT.Sigmoid, scale=-1.0).then_inc(sem("a_gates"), 1)

    def a_dve(dve, follow):
        dve.memset(ones, 1.0).then_inc(sem("ones_set"), 1)
        dve.memset(minus_half, -0.5).then_inc(sem("ones_set"), 1)
        dve.wait_ge(sem("mix_in"), 16)
        follow(dve.tensor_scalar(one_less, mix["lower"], -1.0, 1.0, ALU.mult, ALU.add))
        dve.wait_ge(sem("a_gates"), 3)
        follow(dve.tensor_scalar(keys, forget, one_less, None, ALU.mult))
        dve.tensor_tensor(qk, gate_q, keys, ALU.mult).then_inc(sem("a_products"), 1)
        follow(dve.scalar_tensor_tensor(carried[:, 0:512], keys[:, 512:], 1.0, keys[:, 0:512], ALU.subtract, ALU.mult))
        dve.tensor_tensor(carried[:, 512:], gate_q[:, 512:], carried[:, 0:512], ALU.mult).then_inc(sem("a_products"), 1)
        dve.wait_ge(sem("a_sums"), 1)
        dve.tensor_tensor(mixed[:, 0:512], gate_v[:, 0:512], bank(6), ALU.mult)
        dve.tensor_tensor(carried[:, 0:512], gate_v[:, 0:512], bank(0), ALU.mult)
        follow(dve.tensor_tensor(qk[:, 0:512], gate_v[:, 512:], bank(7), ALU.mult))
        dve.tensor_tensor(mixed[:, 512:], qk[:, 0:512], carried[:, 0:512], ALU.subtract).then_inc(sem("a_mixed"), 1)
        dve.wait_ge(sem("a_out"), 1)
        dve.wait_ge(sem("mix_in2"), 16)
        dve.tensor_tensor(xsum, mix["x"], bank(2, 2), ALU.add).then_inc(sem("a_out_read"), 1)
        dve.wait_ge(sem("a_out_read"), 1)
        norm_stats(dve, follow, tiled(xsum))
        norm_apply(dve, tiled(xsum), tiled(xs)).then_inc(sem("stage_done"), 1)

    Bf = Space(free_at, END)
    film_line = Bf(512)[32:33, :]
    skip_line = Bf(128)[0:1, :]
    K_T, V_T, score_w, mask_line = Bf(B * S2), Bf(B * S2), Bf(B * H_X * S2), Bf(2 * B * S2)[0:1, :]
    film_w, vf0, vf1 = Bf(512), Bf(1024), Bf(1024)
    taps_re, taps_im, taps_re2, taps_im2 = (Bf(512) for _ in range(4))
    u_n = Bf(T)
    after_small = Bf.at
    Tb = Space(after_small, END)
    d_tab = Tb(20 * N_ST)
    stack, stack_T = Tb(512), Tb(512)
    d_dt = Tb(1)
    low_k, low_e, high_k, low_r = (Tb(4096) for _ in range(4))
    high_r, high_e = low_r[:, 0:2048], low_r[:, 2048:]
    taps = Tb(512)
    best = Bf(NT * H_X * TOP)
    minus_max, total, share = Bf(NT * H_X), Bf(NT * H_X), Bf(NT * H_X)
    all_exp, rest_exp, probs, left = ([Bf(S2) for _ in range(2)] for _ in range(4))
    best_exp = Bf(TOP)
    scored = [Bf(H_X * S2) for _ in range(2)]
    diag = [Bf(128) for _ in range(2)]
    attn0, attn1 = Bf(T), Bf(T)
    film = Bf(NT * 512)
    after_attn = Bf.at

    def dt_(i):
        return d_tab[:, N_ST * i:N_ST * i + N_ST]

    def lag(a, n):
        return a.rearrange("p (d l) -> p d l", l=n)

    def b_dve_tables(dve, follow):
        tt = lambda o, a, b, op: follow(dve.tensor_tensor(o, a, b, op))
        dve.wait_ge(sem("ssm_in"), 16)
        dve.wait_ge(sem("s_dt"), 1)
        a_re, a_im = dt_(0), dt_(1)
        follow(dve.tensor_scalar(a_re, ssm["A_re"], d_dt, None, ALU.mult))
        dve.tensor_scalar(a_im, ssm["A_im"], d_dt, float(1.0 / (2.0 * np.pi)), ALU.mult, ALU.mult).then_inc(sem("s_dta"), 1)
        dve.wait_ge(sem("s_dta"), 1)
        dve.tensor_scalar(dt_(2), a_im, 0.25, None, ALU.add)
        follow(dve.tensor_copy(dt_(3), a_im))
        follow(dve.tensor_scalar(d_tab[:, 4 * N_ST:6 * N_ST], d_tab[:, 2 * N_ST:4 * N_ST], MAGIC, None, ALU.add))
        dve.scalar_tensor_tensor(d_tab[:, 4 * N_ST:6 * N_ST], d_tab[:, 4 * N_ST:6 * N_ST], MAGIC,
                                 d_tab[:, 2 * N_ST:4 * N_ST], ALU.subtract, ALU.subtract).then_inc(sem("s_turns"), 1)
        dve.wait_ge(sem("s_trig"), 2)
        cos, sin, er = dt_(6), dt_(7), dt_(8)
        tt(dt_(9), er, cos, ALU.mult)
        tt(dt_(10), er, sin, ALU.mult)
        follow(dve.tensor_scalar(dt_(9), dt_(9), -1.0, None, ALU.add))
        Ar, Ai, Cr, Ci = ssm["A_re"], ssm["A_im"], ssm["C_re"], ssm["C_im"]
        tt(dt_(11), dt_(9), Ar, ALU.mult)
        tt(dt_(12), dt_(10), Ai, ALU.mult)
        tt(dt_(11), dt_(11), dt_(12), ALU.add)
        tt(dt_(12), dt_(10), Ar, ALU.mult)
        tt(dt_(13), dt_(9), Ai, ALU.mult)
        tt(dt_(12), dt_(12), dt_(13), ALU.subtract)
        tt(dt_(13), Ar, Ar, ALU.mult)
        tt(dt_(14), Ai, Ai, ALU.mult)
        tt(dt_(13), dt_(13), dt_(14), ALU.add)
        follow(dve.reciprocal(dt_(13), dt_(13)))
        tt(dt_(11), dt_(11), dt_(13), ALU.mult)
        tt(dt_(12), dt_(12), dt_(13), ALU.mult)
        tt(dt_(14), Cr, dt_(11), ALU.mult)
        tt(dt_(15), Ci, dt_(12), ALU.mult)
        tt(dt_(16), Cr, dt_(12), ALU.mult)
        tt(dt_(17), Ci, dt_(11), ALU.mult)
        s = stack.rearrange("p (k n) -> p k n", n=N_ST)
        tt(s[:, 4, :], dt_(14), dt_(15), ALU.subtract)
        tt(dt_(18), dt_(16), dt_(17), ALU.add)
        for k, src, f in ((0, a_im, 1.0), (1, a_im, 1.0), (2, a_re, 1.0), (3, a_re, 1.0), (5, dt_(18), -1.0),
                          (6, dt_(18), -1.0), (7, s[:, 4, :], -1.0)):
            ins = dve.tensor_scalar(s[:, k, :], src, f, None, ALU.mult)
        ins.then_inc(sem("s_stack"), 1)
        dve.wait_ge(sem("s_stack_turned"), 1)
        follow(dve.tensor_copy(stack_T, bank(7)))
        turn_T, rate_T, u_T, v_T = (stack_T[:, 128 * i:128 * i + 128] for i in range(4))
        every = lambda a, n: a[:, :, None].to_broadcast([P, 128, n])
        lags = lambda a, n: a[:, None, :].to_broadcast([P, 128, n])
        dve.tensor_tensor(lag(low_e, LOW), every(rate_T, LOW), lags(ssm["low_lags"], LOW), ALU.mult).then_inc(sem("s_rates"), 1)
        tt(lag(low_r, LOW), every(turn_T, LOW), lags(ssm["low_lags"], LOW), ALU.mult)
        follow(dve.tensor_scalar(low_k, low_r, ssm["quarter"], MAGIC, ALU.add, ALU.add))
        dve.scalar_tensor_tensor(low_k, low_k, MAGIC, low_r, ALU.subtract, ALU.subtract).then_inc(sem("s_angles"), 1)
        dve.wait_ge(sem("s_angles"), 1)
        dve.tensor_tensor(lag(high_e, HIGH), every(rate_T, HIGH), lags(ssm["high_lags"], HIGH), ALU.mult).then_inc(sem("s_rates"), 1)
        tt(lag(high_r, HIGH), every(turn_T, HIGH), lags(ssm["high_lags"], HIGH), ALU.mult)
        dve.tensor_scalar(high_k[:, 0:2048], high_r, 0.25, MAGIC, ALU.add, ALU.add)
        follow(dve.tensor_scalar(high_k[:, 2048:], high_r, MAGIC, None, ALU.add))
        for h in range(2):
            ins = dve.scalar_tensor_tensor(high_k[:, 2048 * h:2048 * h + 2048], high_k[:, 2048 * h:2048 * h + 2048],
                                           MAGIC, high_r, ALU.subtract, ALU.subtract)
        ins.then_inc(sem("s_angles"), 1)
        dve.wait_ge(sem("s_tables"), 4)
        tt(low_k, low_k, low_e, ALU.mult)
        dve.wait_ge(sem("s_tables"), 5)
        dve.tensor_tensor(lag(high_k[:, 0:2048], HIGH), lag(high_k[:, 0:2048], HIGH), every(u_T, HIGH), ALU.mult)
        follow(dve.tensor_tensor(lag(high_k[:, 2048:], HIGH), lag(high_k[:, 2048:], HIGH), every(v_T, HIGH), ALU.mult))
        tt(high_r, high_k[:, 0:2048], high_k[:, 2048:], ALU.add)
        dve.tensor_tensor(high_r, high_r, high_e, ALU.mult).then_inc(sem("s_factors"), 1)
        dve.wait_ge(sem("s_taps"), 1)
        tp = PS[:, 0:2048].rearrange("p (d c q) -> p c d q", c=4, q=4)
        for q in range(4):
            ins = dve.tensor_copy(taps.rearrange("p (c d) -> p c d", c=4)[32 * q:32 * q + 32], tp[0:32, :, :, q])
        follow(ins)
        dve.wait_ge(sem("small_in"), SMALL)
        follow(dve.tensor_scalar(skip_line, skip_line, 0.5, None, ALU.mult))
        dve.tensor_tensor(taps[0:1, 0:128], taps[0:1, 0:128], skip_line, ALU.add).then_inc(sem("s_taps_in"), 1)
        dve.wait_ge(sem("s_taps_dft"), 1)
        for j in range(4):
            dve.tensor_scalar(taps_re[:, 128 * j:128 * j + 128], PS[:, 128 * j:128 * j + 128],
                              ssm["bin_weight"][:, j:j + 1], None, ALU.mult)
            ins = dve.tensor_scalar(taps_im[:, 128 * j:128 * j + 128], PS[:, 512 + 128 * j:512 + 128 * j + 128],
                                    ssm["bin_weight"][:, j:j + 1], None, ALU.mult)
        follow(ins)
        follow(dve.tensor_copy(taps_re2, taps_re))
        dve.tensor_copy(taps_re2[0:1, 0:128], taps_im[0:1, 0:128])
        follow(dve.tensor_copy(taps_im2, taps_im))
        dve.memset(taps_im2[0:1, 0:128], 0.0).then_inc(sem("s_spectrum"), 1)

    def b_act_tables(act):
        act.wait_ge(sem("ssm_in"), 16)
        act.activation(d_dt, ssm["log_dt"], ACT.Exp).then_inc(sem("s_dt"), 1)
        act.wait_ge(sem("s_dta"), 1)
        act.activation(dt_(8), dt_(0), ACT.Exp).then_inc(sem("s_trig"), 1)
        act.wait_ge(sem("s_turns"), 1)
        act.activation(d_tab[:, 6 * N_ST:8 * N_ST], d_tab[:, 4 * N_ST:6 * N_ST], ACT.Sin, scale=-TWO_PI).then_inc(sem("s_trig"), 1)
        act.wait_ge(sem("s_angles"), 1)
        act.activation(low_k, low_k, ACT.Sin, scale=-TWO_PI, bias=ssm["quarter_angle"]).then_inc(sem("s_tables"), 1)
        act.wait_ge(sem("s_angles"), 2)
        act.activation(high_k[:, 0:2048], high_k[:, 0:2048], ACT.Sin, scale=-TWO_PI, bias=0.25 * TWO_PI).then_inc(sem("s_tables"), 1)
        act.activation(high_k[:, 2048:], high_k[:, 2048:], ACT.Sin, scale=-TWO_PI).then_inc(sem("s_tables"), 1)
        act.wait_ge(sem("s_rates"), 2)
        act.activation(low_e, low_e, ACT.Exp).then_inc(sem("s_tables"), 1)
        act.activation(high_e, high_e, ACT.Exp).then_inc(sem("s_tables"), 1)

    def b_pe_pre(pe):
        pe.wait_ge(sem("ssm_in"), 16)
        pe.wait_ge(sem("a_out_read"), 1)
        pe.matmul(bank(0)[:, 0:308], ssm["Wk"], ssm["ctx_T"], start=True, stop=True).then_inc(sem("x_kv"), 1)
        pe.matmul(bank(1)[:, 0:308], ssm["Wv"], ssm["ctx_T"], start=True, stop=True).then_inc(sem("x_kv"), 1)
        pe.wait_ge(sem("x_kv_in"), 2)
        pe.wait_ge(sem("film_w_in"), 1)
        for h in range(H_X):
            r = slice(DH_X * h, DH_X * h + DH_X)
            pe.matmul(bank(2 + h)[:, 0:308], ssm["Wq_T"][r, :], K_T[r, :], start=True, stop=True).then_inc(sem("x_scorer"), 1)
        pe.wait_ge(sem("x_kv_in"), 2)
        for b in range(B):
            pe.matmul(bank(b), V_T[:, S2 * b:S2 * b + 128], film_w, start=True, stop=True).then_inc(sem("x_vf"), 1)
        for b in range(B):
            pe.matmul(bank(6 + b)[0:REST, :], V_T[:, S2 * b + 128:S2 * b + S2], film_w, start=True, stop=True).then_inc(sem("x_vf"), 1)
        pe.wait_ge(sem("x_small_in"), 8)
        turn_pe(pe, tiled(xs), 4, (sem("stage_done"), 1))
        pe.wait_ge(sem("s_stack"), 1)
        for i in range(4):
            ins = pe.transpose(bank(7)[:, 128 * i:128 * i + 128], stack[:, 128 * i:128 * i + 128], ident)
        ins.then_inc(sem("s_stack_turned"), 1)
        pe.wait_ge(sem("s_factors"), 1)
        for d in range(D):
            ins = pe.matmul(PS[0:LOW, HIGH * d:HIGH * d + HIGH], low_k[:, LOW * d:LOW * d + LOW],
                            high_r[:, HIGH * d:HIGH * d + HIGH], start=True, stop=True)
        ins.then_inc(sem("s_taps"), 1)
        pe.wait_ge(sem("s_taps_in"), 1)
        pe.wait_ge(sem("dft_in"), 16)
        for part, mat in ((0, dft["dft_cos"]), (1, dft["dft_sin"])):
            for j in range(4):
                for c in range(4):
                    ins = pe.matmul(bank(part)[:, 128 * j:128 * j + 128], mat[:, 512 * c + 128 * j:512 * c + 128 * j + 128],
                                    taps[:, 128 * c:128 * c + 128], start=(c == 0), stop=(c == 3))
        ins.then_inc(sem("s_taps_dft"), 1)

    def b_act_pre(act):
        act.wait_ge(sem("x_kv"), 1)
        act.activation(K_T, bank(0)[:, 0:308], ACT.Copy, scale=float(1.0 / np.sqrt(DH_X))).then_inc(sem("x_kv_in"), 1)
        act.wait_ge(sem("x_kv"), 2)
        act.activation(V_T, bank(1)[:, 0:308], ACT.Copy).then_inc(sem("x_kv_in"), 1)
        for h in range(H_X):
            act.wait_ge(sem("x_scorer"), h + 1)
            act.activation(score_w.rearrange("p (b h g) -> p b h g", b=B, h=H_X)[:, :, h, :],
                           bank(2 + h)[:, 0:308].rearrange("p (b g) -> p b g", b=B), ACT.Copy).then_inc(sem("x_small_in"), 1)
        for b in range(B):
            act.wait_ge(sem("x_vf"), b + 1)
            act.activation(vf0[:, 512 * b:512 * b + 512], bank(b), ACT.Copy).then_inc(sem("x_small_in"), 1)
        act.wait_ge(sem("x_rest_clear"), 1)
        for b in range(B):
            act.wait_ge(sem("x_vf"), b + 3)
            act.activation(vf1[0:REST, 512 * b:512 * b + 512], bank(6 + b)[0:REST, :], ACT.Copy).then_inc(sem("x_small_in"), 1)
        act.wait_ge(sem("turned"), 1)
        act.activation(xsT, bank(4, 2), ACT.Copy).then_inc(sem("turned_in"), 1)

    def b_pool_pre(pool, follow):
        pool.wait_ge(sem("small_in"), SMALL)
        pool.wait_ge(sem("ssm_in"), 16)
        pool.tensor_scalar(film_w, ssm["W_film"], mod_gate, None, ALU.mult).then_inc(sem("film_w_in"), 1)
        pool.wait_ge(sem("film_w_in"), 1)
        pool.memset(vf1[0:32, :], 0.0).then_inc(sem("x_rest_clear"), 1)
        pool.wait_ge(sem("x_rest_clear"), 1)
        follow(pool.tensor_scalar(film_line, film_line, mod_gate[32:33, :], None, ALU.mult))
        fl = film_line.rearrange("p (f s d) -> p f s d", f=2, s=2)
        follow(pool.tensor_scalar(fl[:, :, 0, :], fl[:, :, 0, :], 1.0, None, ALU.add))
        for b in range(B):
            follow(pool.tensor_copy(vf1[32:33, 512 * b:512 * b + 512], film_line))
        follow(pool.tensor_copy(mask_line[:, 0:308], ctx_bytes))
        follow(pool.tensor_scalar(mask_line[:, 0:308], mask_line[:, 0:308], 1.0, None, ALU.subtract))
        follow(pool.tensor_scalar(mask_line[:, 0:308], mask_line[:, 0:308], -NEG, None, ALU.mult))
        m2 = mask_line.rearrange("p (b h g) -> p b h g", b=2, h=2)
        follow(pool.tensor_copy(m2[:, 1, 1, :], mask_line[:, S2:2 * S2]))
        follow(pool.tensor_copy(m2[:, 1, 0, :], m2[:, 1, 1, :]))
        follow(pool.tensor_copy(m2[:, 0, 1, :], m2[:, 0, 0, :]))
        follow(pool.tensor_copy(text_mask, text_bytes))
        pool.tensor_scalar(text_mask, text_mask, 1.0 / H_X, None, ALU.mult).then_inc(sem("masks_in"), 1)
        pool.wait_ge(sem("masks_in"), 1)

    STEPS = NT * H_X

    def scores(i):
        t, h = divmod(i, H_X)
        return scored[t % 2][:, S2 * h:S2 * h + S2]

    def b_pe_attention(pe):
        pe.wait_ge(sem("turned_in"), 1)
        pe.wait_ge(sem("masks_in"), 1)
        pe.wait_ge(sem("s_spectrum"), 1)
        pe.wait_ge(sem("ones_set"), 2)

        def score(t):
            if t >= 2:
                pe.wait_ge(sem("x_scores_in"), t - 1)
            b = t // (NT // B)
            for g in range(2):
                o = bank(2 * (t % 2) + g)[:, 0:2 * S2]
                pe.matmul(o, xsT[:, 128 * t:128 * t + 128], score_w[:, 4 * S2 * b + 2 * S2 * g:4 * S2 * b + 2 * S2 * g + 2 * S2],
                          start=True, stop=False)
                pe.matmul(o, ones[0:1, :], mask_line[:, 2 * S2 * b:2 * S2 * b + 2 * S2], start=False, stop=True)\
                  .then_inc(sem("x_scores"), 1)

        def gather(t):
            if t >= 2:
                pe.wait_ge(sem("x_attn_in"), 2 * (t - 1))
            for h in range(H_X):
                i = H_X * t + h
                pe.wait_ge(sem("x_diag"), i + 1)
                pe.matmul(bank(4 + t % 2)[:, 0:128], probs[i % 2][:, 0:128], diag[i % 2], start=(h == 0), stop=(h == 3))
                pe.matmul(bank(6 + t % 2)[0:REST, 0:128], probs[i % 2][:, 128:S2], diag[i % 2], start=(h == 0),
                          stop=(h == 3)).then_inc(sem("x_gathered"), 1)

        score(0)
        score(1)
        for t in range(NT):
            gather(t)
            if t + 2 < NT:
                score(t + 2)

    def b_dve_attention(dve, follow):
        for t in range(NT):
            dve.wait_ge(sem("x_scores_in"), t + 1)
            for h in range(H_X):
                i = H_X * t + h
                m8 = best[:, TOP * i:TOP * i + TOP]
                if i >= 2:
                    dve.wait_ge(sem("x_exp"), 3 * (i - 1))
                src = scores(i)
                for r in range(TOP // 8):
                    ins = dve.max(m8[:, 8 * r:8 * r + 8], src)
                    if r == 0:
                        ins.then_inc(sem("x_max"), 1)
                        dve.wait_ge(sem("x_max"), i + 1)
                    else:
                        follow(ins)
                    ins = dve.match_replace(left[i % 2], m8[:, 8 * r:8 * r + 8], src, GONE)
                    if r < TOP // 8 - 1:
                        follow(ins)
                    else:
                        ins.then_inc(sem("x_selected"), 1)
                    src = left[i % 2]
                if i >= 1:
                    dve.wait_ge(sem("x_exp"), 3 * i)
                    dve.reciprocal(share[:, i - 1:i], total[:, i - 1:i]).then_inc(sem("x_share"), 1)
        dve.wait_ge(sem("x_exp"), 3 * STEPS)
        dve.reciprocal(share[:, STEPS - 1:STEPS], total[:, STEPS - 1:STEPS]).then_inc(sem("x_share"), 1)

    def b_act_attention(act):
        def scores_in(t):
            if t >= 2:
                act.wait_ge(sem("x_selected"), H_X * (t - 1))
                act.wait_ge(sem("x_exp"), 3 * H_X * (t - 1))
            act.wait_ge(sem("x_scores"), 2 * t + 2)
            act.activation(scored[t % 2].rearrange("p (g k) -> p g k", g=2),
                           bank(2 * (t % 2), 2).rearrange("p (g k) -> p g k", g=2)[:, :, 0:2 * S2], ACT.Copy)\
               .then_inc(sem("x_scores_in"), 1)

        act.wait_ge(sem("s_spectrum"), 1)
        scores_in(0)
        for t in range(NT):
            if t + 1 < NT:
                scores_in(t + 1)
            for h in range(H_X):
                i = H_X * t + h
                act.wait_ge(sem("x_minus_max"), i + 1)
                if i >= 2:
                    act.wait_ge(sem("x_probs"), i - 1)
                bias = minus_max[:, i:i + 1]
                act.activation(all_exp[i % 2], scores(i), ACT.Exp, bias=bias).then_inc(sem("x_exp"), 1)
                act.wait_ge(sem("x_selected"), i + 1)
                act.activation(rest_exp[i % 2], left[i % 2], ACT.Exp, bias=bias).then_inc(sem("x_exp"), 1)
                if i >= 1:
                    act.wait_ge(sem("x_exp"), 3 * i)
                act.activation(best_exp, best[:, TOP * i:TOP * i + TOP], ACT.Exp, bias=bias,
                               accum_out=total[:, i:i + 1]).then_inc(sem("x_exp"), 1)
            if t >= 1:
                attn_in(act, t - 1)
        attn_in(act, NT - 1)

    def attn_in(act, t):
        act.wait_ge(sem("x_gathered"), H_X * (t + 1))
        if t == 0:
            act.wait_ge(sem("x_attn_clear"), 1)
        act.activation(attn0[:, 128 * t:128 * t + 128], bank(4 + t % 2)[:, 0:128], ACT.Copy).then_inc(sem("x_attn_in"), 1)
        act.activation(attn1[0:REST, 128 * t:128 * t + 128], bank(6 + t % 2)[0:REST, 0:128], ACT.Copy).then_inc(sem("x_attn_in"), 1)

    def b_pool_attention(pool, follow):
        pool.wait_ge(sem("s_spectrum"), 1)
        follow(pool.memset(attn1[0:32, :], 0.0))
        pool.memset(attn1[32:33, :], 1.0).then_inc(sem("x_attn_clear"), 1)
        pool.wait_ge(sem("x_attn_clear"), 1)

        def negate(i):
            pool.wait_ge(sem("x_max"), i + 1)
            pool.tensor_scalar(minus_max[:, i:i + 1], best[:, TOP * i:TOP * i + 1], -1.0, None, ALU.mult)\
                .then_inc(sem("x_minus_max"), 1)

        negate(0)
        for i in range(STEPS):
            if i + 1 < STEPS:
                negate(i + 1)
            pool.wait_ge(sem("x_exp"), 3 * i + 2)
            if i >= 2:
                pool.wait_ge(sem("x_gathered"), i - 1)
            pool.tensor_tensor(probs[i % 2], all_exp[i % 2], rest_exp[i % 2], ALU.subtract).then_inc(sem("x_probs"), 1)
            pool.wait_ge(sem("x_share"), i + 1)
            t = i // H_X
            pool.tensor_scalar(share[:, i:i + 1], share[:, i:i + 1], text_mask[:, t:t + 1], None, ALU.mult).then_inc(sem("x_share_p"), 1)
            pool.wait_ge(sem("x_share_p"), i + 1)
            pool.wait_ge(sem("x_probs"), i + 1)
            pool.tensor_scalar(diag[i % 2], ident, share[:, i:i + 1], None, ALU.mult).then_inc(sem("x_diag"), 1)

    Bc = Space(after_attn, END)
    W.at = W.end - 8792
    Y_re, Y_im = best, None
    spec = Space(after_small, after_small + 1024 + 96 + 1232 + 32 + 256 + 2048)
    Y_re, Y_im, prod_a, prod_b = spec(1024), spec(1024), spec(1024), spec(1024)
    u = Bc(T)
    inner = Bc(T)
    inner_n = u
    hT = inner
    gelu = film

    def b_dve_norm(dve, follow):
        dve.wait_ge(sem("stage_done"), 1)
        norm_stats(dve, follow, tiled(xs))
        follow(norm_apply(dve, tiled(xs), tiled(u_n)))
        every = lambda a: a[:, None, :].to_broadcast([P, NT, 128])
        follow(dve.tensor_tensor(tiled(u_n), tiled(u_n), every(rows["g_in"]), ALU.mult))
        follow(dve.tensor_tensor(tiled(u_n), tiled(u_n), every(rows["b_in"]), ALU.add))

    def b_pe_ssm(pe):
        for t in range(NT):
            pe.wait_ge(sem("x_attn_in"), 2 * NT if t == NT - 1 else 2 * t + 2)
            if t == 0:
                pe.wait_ge(sem("x_selected"), STEPS)
                pe.wait_ge(sem("x_exp"), 3 * STEPS)
            if t >= 2:
                pe.wait_ge(sem("x_film_in"), t - 1)
            b = t // (NT // B)
            pe.matmul(bank(t % 2), attn0[:, 128 * t:128 * t + 128], vf0[:, 512 * b:512 * b + 512], start=True, stop=False)
            pe.matmul(bank(t % 2), attn1[0:33, 128 * t:128 * t + 128], vf1[0:33, 512 * b:512 * b + 512], start=False,
                      stop=True).then_inc(sem("x_film"), 1)
        pe.wait_ge(sem("s_u"), 1)
        pe.wait_ge(sem("x_film_in"), NT)
        uv = u.rearrange("p (b c d) -> p c b d", b=B, c=4)
        for j in range(4):
            for part, mat in ((0, dft["dft_cos"]), (1, dft["dft_sin"])):
                for c in range(4):
                    ins = pe.matmul(bank(4 * part + j)[:, 0:256], mat[:, 512 * c + 128 * j:512 * c + 128 * j + 128],
                                    uv[:, c], start=(c == 0), stop=(c == 3))
            ins.then_inc(sem("s_spectra"), 1)
        pe.wait_ge(sem("s_product"), 5)
        for c in range(4):
            o = bank(c)[:, 0:256]
            for j in range(4):
                pe.matmul(o, dft["dft_cos"][:, 512 * j + 128 * c:512 * j + 128 * c + 128], Y_re[:, 256 * j:256 * j + 256],
                          start=(j == 0), stop=False)
            for j in range(4):
                sin = dft["inv_sin0"][:, 128 * c:128 * c + 128] if j == 0 else \
                    dft["dft_sin"][:, 512 * j + 128 * c:512 * j + 128 * c + 128]
                ins = pe.matmul(o, sin, Y_im[:, 256 * j:256 * j + 256], start=False, stop=(j == 3))
            ins.then_inc(sem("s_conv"), 1)
        turn_pe(pe, tiled(inner_n), 4, (sem("f_normed"), 1))
        pe.wait_ge(sem("turned_in"), 2)
        pe.wait_ge(sem("ffn_in"), 16)
        for k in range(4):
            if k >= 2:
                pe.wait_ge(sem("f_gelu"), k - 1)
            for n in range(2):
                ins = pe.matmul(bank(2 * (k % 2) + n), ffn["W1"][:, 128 * k:128 * k + 128], hT[:, 512 * n:512 * n + 512],
                                start=True, stop=True)
            ins.then_inc(sem("f_hidden"), 1)
        pe.wait_ge(sem("f_gelu"), 4)
        for t in range(NT):
            pe.matmul(PS[:, 3072 + 128 * t:3072 + 128 * t + 128], ones[0:1, :], lines["ffn_b2"][0:1, :], start=True, stop=False)
            for k in range(4):
                ins = pe.matmul(PS[:, 3072 + 128 * t:3072 + 128 * t + 128], gelu[:, T * k + 128 * t:T * k + 128 * t + 128],
                                ffn["W2"][:, 128 * k:128 * k + 128], start=False, stop=(k == 3))
        ins.then_inc(sem("f_out"), 1)

    def b_act_ssm(act):
        for t in range(NT):
            act.wait_ge(sem("x_film"), t + 1)
            act.activation(film[:, 512 * t:512 * t + 512], bank(t % 2), ACT.Copy).then_inc(sem("x_film_in"), 1)
        act.wait_ge(sem("turned"), 2)
        act.wait_ge(sem("ffn_in"), 16)
        act.wait_ge(sem("f_inner_kept"), 1)
        act.activation(hT, bank(4, 2), ACT.Identity, scale=ffn["ffn_g"], bias=ffn["ffn_b"]).then_inc(sem("turned_in"), 1)
        for k in range(4):
            act.wait_ge(sem("f_hidden"), k + 1)
            act.activation(gelu[:, T * k:T * k + T], bank(2 * (k % 2), 2), ACT.Gelu, bias=ffn["ffn_b1"][:, k:k + 1])\
               .then_inc(sem("f_gelu"), 1)

    def b_dve_ssm(dve, follow):
        fv = film.rearrange("p (t k d) -> p t k d", t=NT, k=4)
        dve.wait_ge(sem("x_film_in"), NT)
        follow(dve.tensor_tensor(tiled(u), tiled(u_n), fv[:, :, 0], ALU.mult))
        dve.tensor_tensor(tiled(u), tiled(u), fv[:, :, 1], ALU.add).then_inc(sem("s_u"), 1)
        two = lambda a, j: a[:, None, 128 * j:128 * j + 128].to_broadcast([P, 2, 128])
        bd = lambda a: a.rearrange("p (b d) -> p b d", b=2)
        for j in range(4):
            dve.wait_ge(sem("s_spectra"), j + 1)
            re, im = bd(bank(j)[:, 0:256]), bd(bank(4 + j)[:, 0:256])
            at = slice(256 * j, 256 * j + 256)
            dve.tensor_tensor(bd(Y_re[:, at]), re, two(taps_re, j), ALU.mult)
            dve.tensor_tensor(bd(prod_a[:, at]), im, two(taps_im2, j), ALU.mult)
            dve.tensor_tensor(bd(Y_im[:, at]), im, two(taps_re2, j), ALU.mult)
            follow(dve.tensor_tensor(bd(prod_b[:, at]), re, two(taps_im2, j), ALU.mult))
            dve.tensor_tensor(Y_re[:, at], Y_re[:, at], prod_a[:, at], ALU.subtract)
            dve.tensor_tensor(Y_im[:, at], Y_im[:, at], prod_b[:, at], ALU.add).then_inc(sem("s_product"), 1)
        dve.memset(dft["dft_sin"].rearrange("p (c l) -> p c l", c=4)[:, 1:4, 0:1], 0.0).then_inc(sem("s_product"), 1)
        dve.wait_ge(sem("s_conv"), 4)
        y = PS[:, 0:2048].rearrange("p (c b d) -> p c b d", c=4, b=4)
        i4 = inner.rearrange("p (b c d) -> p b c d", b=B, c=4)
        f4 = film.rearrange("p (b c k d) -> p b c k d", b=B, c=4, k=4)
        for b in range(B):
            ins = dve.tensor_tensor(i4[:, b], y[:, :, b], f4[:, b, :, 2], ALU.mult)
        follow(ins)
        follow(dve.tensor_tensor(tiled(inner), tiled(inner), fv[:, :, 3], ALU.add))
        follow(dve.tensor_tensor(inner, inner, xs, ALU.add))
        norm_stats(dve, follow, tiled(inner))
        norm_apply(dve, tiled(inner), tiled(inner_n)).then_inc(sem("f_normed"), 1)
        dve.tensor_copy(xsum, inner).then_inc(sem("f_inner_kept"), 1)
        every = lambda a: a[:, None, :].to_broadcast([P, NT, 128])
        follow(dve.tensor_tensor(tiled(u_n), tiled(xs), every(rows["b_out"]), ALU.add))
        dve.wait_ge(sem("f_out"), 1)
        follow(dve.tensor_tensor(xsum, xsum, bank(6, 2), ALU.add))
        norm_stats(dve, follow, tiled(xsum))
        follow(norm_apply(dve, tiled(xsum), tiled(xn)))
        follow(dve.tensor_tensor(tiled(xn), tiled(xn), every(rows["g_out"]), ALU.mult))
        follow(dve.tensor_tensor(xsum, xn, u_n, ALU.add))
        norm_stats(dve, follow, tiled(xsum))
        norm_apply(dve, tiled(xsum), tiled(xs)).then_inc(sem("stage_done"), 1)

    W3 = Space(after_small, END)
    moe = views(PACK_MOE, Space(END - 8192, END)(8192))
    mha_at = W3.at
    mha = views(PACK_MHA, W3(width(PACK_MHA)))
    C = Space(W3.at, END - 8192)
    C0 = Space(stream.at, stream.at + 8792)
    merged, merged_bias = C0(E0 * 128), C0(128)
    d_x, d_k, d_v, v_1 = C0(512), C0(512), C0(512), C0(512)
    q_dk, attended = C(T), C(T)
    y1, y1T, y1_bias = C(T), C(T), C(T)
    g_logit, g_cand, g_hot, g_pos, g_coef = (C(NT * E0) for _ in range(5))
    g_max, g_sum = C(NT), C(NT)
    coef_T = C(T)
    moe_sum = C(T)
    by_tile = C(NT * E0)

    def c_sp(sp):
        sp.wait_ge(sem("s_product"), 5)
        sp.wait_ge(sem("f_normed"), 1)
        sp.dma_start(SB[:, mha_at:mha_at + width(PACK_MHA)], dram["mha"]).then_inc(sem("mha_in"), 16)
        sp.wait_ge(sem("stage_done"), 2)
        sp.dma_start(SB[:, END - 8192:END], dram["moe"]).then_inc(sem("moe_in"), 16)

    def c_pe(pe):
        turn_pe(pe, tiled(xs), 0, (sem("stage_done"), 2))
        pe.wait_ge(sem("mha_in"), 16)
        pe.wait_ge(sem("turned_in"), 3)
        pe.wait_ge(sem("c_dx"), 1)
        for n in range(2):
            ins = pe.matmul(bank(2 + n), mha["qkv_T"][:, 0:128], xsT[:, 512 * n:512 * n + 512], start=True, stop=True)
        ins.then_inc(sem("c_qkv"), 1)
        pe.matmul(bank(4), mha["qkv_T"][:, 128:256], d_x, start=True, stop=True).then_inc(sem("c_qkv"), 1)
        pe.matmul(bank(5), mha["qkv_T"][:, 256:384], d_x, start=True, stop=True).then_inc(sem("c_qkv"), 1)
        pe.matmul(bank(6), mha["qkv_T"][:, 256:384], xsT[:, 512:], start=True, stop=True).then_inc(sem("c_qkv"), 1)
        pe.wait_ge(sem("c_qdk"), 1)
        for n in range(2):
            ins = pe.matmul(bank(n), mha["head_sum"], q_dk[:, 512 * n:512 * n + 512], start=True, stop=True)
        ins.then_inc(sem("c_scores"), 1)
        pe.wait_ge(sem("c_attended"), 1)
        for t in range(NT):
            o = PS[:, 3072 + 128 * t:3072 + 128 * t + 128]
            if t == 0:
                pe.wait_ge(sem("c_v_in"), 4)
            pe.matmul(o, ones[0:1, :], lines["m_ob"][0:1, :], start=True, stop=False)
            ins = pe.matmul(o, attended[:, 128 * t:128 * t + 128], mha["ow_T"], start=False, stop=True)
        ins.then_inc(sem("c_out"), 1)
        pe.wait_ge(sem("moe_in"), 16)
        for e in range(E0):
            o = bank(2 + e // 4)[:, 128 * (e % 4):128 * (e % 4) + 128]
            for k in range(4):
                i = 4 * e + k
                ins = pe.matmul(o, moe["m_w1T"][:, 128 * i:128 * i + 128], moe["m_w2"][:, 128 * i:128 * i + 128],
                                start=(k == 0), stop=(k == 3))
        ins.then_inc(sem("c_merged"), 1)
        for e in range(E0):
            for k in range(4):
                ins = pe.matmul(bank(4)[0:E0, 0:128], mha["m_b1"][:, 64 * k + 8 * e:64 * k + 8 * e + 8],
                                moe["m_w2"][:, 128 * (4 * e + k):128 * (4 * e + k) + 128], start=(e + k == 0), stop=(e == 7 and k == 3))
        ins.then_inc(sem("c_merged"), 1)
        turn_pe(pe, tiled(xn), 0, (sem("c_normed"), 1))
        pe.wait_ge(sem("turned_in"), 4)
        for t in range(NT):
            ins = pe.matmul(bank(5)[:, E0 * t:E0 * t + E0], y1T[:, 128 * t:128 * t + 128], mha["m_wg"], start=True, stop=True)
        ins.then_inc(sem("g_logits"), 1)
        pe.wait_ge(sem("g_hot"), 1)
        pe.matmul(bank(6)[:, 0:NT * E0], mha["earlier"], g_hot, start=True, stop=False)
        pe.matmul(bank(6)[:, 0:NT * E0], ones, by_tile, start=False, stop=True).then_inc(sem("g_counted"), 1)
        pe.wait_ge(sem("g_coef"), 1)
        for t in range(NT):
            ins = pe.transpose(PS[0:E0, 128 * t:128 * t + 128], g_coef[:, E0 * t:E0 * t + E0], ident)
        ins.then_inc(sem("g_coef_turned"), 1)
        pe.wait_ge(sem("g_coef_in"), 1)
        for t in range(NT):
            ins = pe.matmul(PS[:, 3072 + 128 * t:3072 + 128 * t + 128], coef_T[0:E0, 128 * t:128 * t + 128],
                            merged_bias[0:E0, :], start=True, stop=True)
        ins.then_inc(sem("c_bias"), 1)
        pe.wait_ge(sem("c_merged_in"), 2)
        for t in range(NT):
            if t >= 3:
                pe.wait_ge(sem("c_combined"), t - 2)
            for n in range(2):
                ins = pe.matmul(bank(2 * (t % 3) + n), y1T[:, 128 * t:128 * t + 128], merged[:, 512 * n:512 * n + 512],
                                start=True, stop=True)
            ins.then_inc(sem("c_expert"), 1)

    def c_act(act):
        act.wait_ge(sem("turned"), 3)
        act.activation(xsT, bank(0, 2), ACT.Copy).then_inc(sem("turned_in"), 1)
        act.wait_ge(sem("c_qkv"), 2)
        act.activation(d_k, bank(4), ACT.Copy).then_inc(sem("c_v_in"), 1)
        act.wait_ge(sem("c_qkv"), 3)
        act.activation(d_v, bank(5), ACT.Copy).then_inc(sem("c_v_in"), 1)
        act.wait_ge(sem("c_qkv"), 4)
        act.activation(v_1, bank(6), ACT.Identity, bias=mha["b_v"]).then_inc(sem("c_v_in"), 1)
        act.wait_ge(sem("c_scores"), 1)
        act.activation(attended, bank(0, 2), ACT.Sigmoid, scale=float(1.0 / np.sqrt(DH_X))).then_inc(sem("c_v_in"), 1)
        act.wait_ge(sem("c_merged"), 1)
        act.activation(merged, bank(2, 2), ACT.Copy).then_inc(sem("c_merged_in"), 1)
        act.wait_ge(sem("turned"), 4)
        act.activation(y1T, bank(0, 2), ACT.Identity, scale=mha["ln1_g"], bias=mha["ln1_b"]).then_inc(sem("turned_in"), 1)
        act.wait_ge(sem("g_hot"), 1)
        act.activation(g_cand, g_logit, ACT.Exp).then_inc(sem("g_exp"), 1)
        act.wait_ge(sem("g_coef_turned"), 1)
        act.activation(coef_T[0:E0, :], PS[0:E0, 0:1024], ACT.Copy).then_inc(sem("g_coef_in"), 1)

    def c_dve(dve, follow):
        every = lambda a: a[:, None, :].to_broadcast([P, NT, 128])
        dve.wait_ge(sem("turned_in"), 3)
        dve.tensor_tensor(d_x, xsT[:, 0:512], xsT[:, 512:], ALU.subtract).then_inc(sem("c_dx"), 1)
        dve.wait_ge(sem("c_qkv"), 1)
        dve.wait_ge(sem("c_v_in"), 1)
        for n in range(2):
            ins = dve.scalar_tensor_tensor(q_dk[:, 512 * n:512 * n + 512], bank(2 + n), mha["b_q"], d_k, ALU.add, ALU.mult)
        ins.then_inc(sem("c_qdk"), 1)
        dve.wait_ge(sem("c_v_in"), 4)
        two = lambda a: a[:, None, :].to_broadcast([P, 2, 512])
        a2 = attended.rearrange("p (l n) -> p l n", l=2)
        follow(dve.tensor_tensor(a2, a2, two(d_v), ALU.mult))
        dve.tensor_tensor(a2, a2, two(v_1), ALU.add).then_inc(sem("c_attended"), 1)
        dve.wait_ge(sem("c_out"), 1)
        follow(dve.tensor_tensor(xsum, xs, bank(6, 2), ALU.add))
        norm_stats(dve, follow, tiled(xsum))
        norm_apply(dve, tiled(xsum), tiled(xn)).then_inc(sem("c_normed"), 1)
        dve.wait_ge(sem("c_normed"), 1)
        follow(dve.tensor_tensor(tiled(y1), tiled(xn), every(rows["n1_g"]), ALU.mult))
        follow(dve.tensor_tensor(tiled(y1), tiled(y1), every(rows["n1_b"]), ALU.add))
        follow(dve.tensor_tensor(tiled(y1_bias), tiled(xs), every(rows["n2_b"]), ALU.add))
        dve.wait_ge(sem("c_merged"), 2)
        dve.tensor_tensor(merged_bias[0:E0, :], bank(4)[0:E0, 0:128], mha["m_b2"][0:E0, :], ALU.add).then_inc(sem("c_merged_in"), 1)
        dve.wait_ge(sem("lat_in"), 16)
        dve.wait_ge(sem("g_logits"), 1)
        te = lambda a: a.rearrange("p (t e) -> p t e", t=NT)
        eight = lambda a: a[:, :, None].to_broadcast([P, NT, E0])
        follow(dve.tensor_copy(g_logit, bank(5)[:, 0:NT * E0]))
        follow(dve.tensor_reduce(g_max, te(g_logit), AX_X, ALU.max))
        follow(dve.tensor_tensor(te(g_logit), te(g_logit), eight(g_max), ALU.subtract))
        follow(dve.tensor_scalar(g_cand, g_logit, 0.0, None, ALU.is_equal))
        follow(dve.tensor_tensor(te(g_cand), te(g_cand), lat["expert_rank"][:, None, :].to_broadcast([P, NT, E0]), ALU.mult))
        follow(dve.tensor_reduce(g_max, te(g_cand), AX_X, ALU.max))
        follow(dve.tensor_tensor(te(g_hot), te(g_cand), eight(g_max), ALU.is_equal))
        follow(dve.memset(by_tile[:, 0:E0], 0.0))
        for t in range(1, NT):
            ins = dve.tensor_tensor(te(by_tile)[:, t], te(by_tile)[:, t - 1], te(g_hot)[:, t - 1], ALU.add)
            if t < NT - 1:
                follow(ins)
        ins.then_inc(sem("g_hot"), 1)
        dve.wait_ge(sem("g_hot"), 1)
        dve.wait_ge(sem("g_exp"), 1)
        follow(dve.tensor_reduce(g_sum, te(g_cand), AX_X, ALU.add))
        follow(dve.reciprocal(g_sum, g_sum))
        dve.wait_ge(sem("g_counted"), 1)
        follow(dve.scalar_tensor_tensor(g_coef, bank(6)[:, 0:NT * E0], float(CAP), g_hot, ALU.is_lt, ALU.mult))
        dve.tensor_tensor(te(g_coef), te(g_coef), eight(g_sum), ALU.mult).then_inc(sem("g_coef"), 1)
        dve.wait_ge(sem("c_bias"), 1)
        follow(dve.tensor_tensor(moe_sum, y1, bank(6, 2), ALU.add))
        for t in range(NT):
            dve.wait_ge(sem("c_expert"), t + 1)
            dve.wait_ge(sem("g_coef"), 1)
            for e in range(E0):
                o = tiled(moe_sum)[:, t]
                ins = dve.scalar_tensor_tensor(o, PS[:, 1024 * (t % 3) + 128 * e:1024 * (t % 3) + 128 * e + 128],
                                               g_coef[:, E0 * t + e:E0 * t + e + 1], o, ALU.mult, ALU.add)
                if e < E0 - 1:
                    follow(ins)
            ins.then_inc(sem("c_combined"), 1)
        dve.wait_ge(sem("c_combined"), NT)
        norm_stats(dve, follow, tiled(moe_sum))
        follow(norm_apply(dve, tiled(moe_sum), tiled(xn)))
        follow(dve.tensor_tensor(tiled(xn), tiled(xn), every(rows["n2_g"]), ALU.mult))
        follow(dve.tensor_tensor(xsum, xn, y1_bias, ALU.add))
        norm_stats(dve, follow, tiled(xsum))
        norm_apply(dve, tiled(xsum), tiled(xs)).then_inc(sem("stage_done"), 1)

    D1 = Space(stream.at, stream.at + 8792)
    value = D1(8192)
    D2 = Space(W2.end, END)
    headed = D2(8192)
    expd = [D2(4096) for _ in range(2)]
    q_ring, k_ring = [D2(1024) for _ in range(3)], [D2(1024) for _ in range(3)]
    qb_ring, kb_ring = [D2(512, BF16) for _ in range(3)], [D2(512, BF16) for _ in range(3)]
    half_sum, key_sum, unit = D2(1024), D2(1024), D2(512)
    shift = [D2(8) for _ in range(2)]
    NP_ = B * PAIRS

    def two_heads(a):
        return a.rearrange("p (h n) -> p h n", h=2)

    def d_pe(pe):
        turn_pe(pe, tiled(xs), 0, (sem("stage_done"), 3))
        pe.wait_ge(sem("turned_in"), 5)
        pe.wait_ge(sem("att_in"), 16)

        def project(i, which):
            b, pair = divmod(i, PAIRS)
            if which:
                pe.wait_ge(sem("d_qk_in"), 4 * i + 2)
            elif i == 1:
                pe.wait_ge(sem("d_qk_in"), 4)
            elif i >= 2:
                pe.wait_ge(sem("d_shift_q"), i - 1)
                pe.wait_ge(sem("d_shift_k"), i - 1)
            w = att["w_k"] if which else att["w_q"]
            pe.matmul(bank(7), w[:, 128 * pair:128 * pair + 128], xsT[:, 512 * b:512 * b + 512], start=True, stop=True)\
              .then_inc(sem("d_qk"), 1)

        def maxima(i, qt):
            n = 4 * i + qt
            if qt == 0:
                pe.wait_ge(sem("d_bf16"), 2 * i + 2)
            if n >= 1:
                pe.wait_ge(sem("d_max"), n)
            for h in range(2):
                ins = pe.matmul(bank(4 + h), two_heads(qb_ring[i % 3])[0:DK, h, 128 * qt:128 * qt + 128],
                                two_heads(kb_ring[i % 3])[0:DK, h, :], start=True, stop=True)
            ins.then_inc(sem("d_rough"), 1)

        def shifts(i):
            pe.wait_ge(sem("d_max"), 4 * i + 4)
            if i < 2:
                pe.wait_ge(sem("d_qk_in"), 4 * (i + 2))
            else:
                pe.wait_ge(sem("d_unit"), i - 1)
            for qt in range(4):
                for h in range(2):
                    c = 2 * qt + h
                    ins = pe.matmul(bank(7)[32 * h:32 * h + 1, 128 * qt:128 * qt + 128], shift[i % 2][:, c:c + 1], ident,
                                    start=True, stop=True)
            ins.then_inc(sem("d_shifts"), 1)

        def score(i, u):
            h, half = divmod(u, 2)
            n = 4 * i + u
            if u == 0:
                pe.wait_ge(sem("d_shift_q"), i + 1)
                pe.wait_ge(sem("d_shift_k"), i + 1)
            if n >= 2:
                pe.wait_ge(sem("d_exp"), n - 1)
            for k in range(2):
                kt = 2 * half + k
                ins = pe.matmul(bank(2 * (n % 2) + k), two_heads(k_ring[i % 3])[0:DK + 1, h, 128 * kt:128 * kt + 128],
                                two_heads(q_ring[i % 3])[0:DK + 1, h, :], start=True, stop=True)
            ins.then_inc(sem("d_scores"), 1)

        def weigh(i, kt):
            b, pair = divmod(i, PAIRS)
            if kt == 0:
                pe.wait_ge(sem("d_exp"), 4 * i + 4)
                if i >= 1:
                    pe.wait_ge(sem("d_headed"), i)
            for h in range(2):
                v = value[:, 1024 * (4 * b + kt) + 128 * pair + DK * h:1024 * (4 * b + kt) + 128 * pair + DK * h + DK]
                ins = pe.matmul(bank(6)[DK * h:DK * h + DK, :], v, expd[i % 2][:, 2048 * h + 512 * kt:2048 * h + 512 * kt + 512],
                                start=(kt == 0), stop=(kt == 3))
            if kt == 3:
                ins.then_inc(sem("d_weighed"), 1)

        def sums(i):
            pe.wait_ge(sem("d_key_sum"), i + 1)
            if i + 3 < NP_:
                pe.wait_ge(sem("d_qk_in"), 4 * (i + 4))
            elif i + 1 < NP_:
                pe.wait_ge(sem("d_shift_q"), i + 2)
                pe.wait_ge(sem("d_shift_k"), i + 2)
            else:
                pe.wait_ge(sem("d_unit"), i)
            for h in range(2):
                ins = pe.matmul(bank(7)[DK * h:DK * h + DK, :], ones[:, 0:DK], two_heads(key_sum)[:, h, :], start=True, stop=True)
            ins.then_inc(sem("d_sums"), 1)

        for t in range(NT):
            if t >= 4:
                pe.wait_ge(sem(("d_v_even", "d_v_odd")[t % 2]), (t - 4) // 2 + 1)
            for n in range(2):
                ins = pe.matmul(bank(2 * (t % 4) + n), xsT[:, 128 * t:128 * t + 128], att["w_v"][:, 512 * n:512 * n + 512],
                                start=True, stop=True)
            ins.then_inc(sem("d_v"), 1)
        pe.wait_ge(sem("d_v_even"), NT // 2)
        pe.wait_ge(sem("d_v_odd"), NT // 2)
        pe.wait_ge(sem("d_ones"), 1)
        for i in range(2):
            project(i, 0)
            project(i, 1)
        for qt in range(4):
            maxima(0, qt)
        shifts(0)
        for i in range(NP_ + 1):
            now, ahead, before = i < NP_, i + 1 < NP_, i >= 1
            for u in range(4):
                if ahead and u < 3:
                    maxima(i + 1, (0, 2, 3)[u])
                if ahead and u == 3:
                    shifts(i + 1)
                if now:
                    score(i, u)
                if ahead and u == 0:
                    maxima(i + 1, 1)
                if before:
                    weigh(i - 1, u)
                if i + 2 < NP_ and u < 2:
                    project(i + 2, u)
                if before and u == 2:
                    sums(i - 1)
        for t in range(NT):
            b, c = divmod(t, 4)
            if t == 0:
                pe.wait_ge(sem("d_headed"), NP_)
            for pair in range(PAIRS):
                ins = pe.matmul(PS[:, 128 * t:128 * t + 128], headed[:, 512 * (PAIRS * b + pair) + 128 * c:512 * (PAIRS * b + pair) + 128 * c + 128],
                                att["w_o"][:, 128 * pair:128 * pair + 128], start=(pair == 0), stop=(pair == PAIRS - 1))
        ins.then_inc(sem("d_out"), 1)

    def d_act(act):
        act.wait_ge(sem("turned"), 5)
        act.activation(xsT, bank(0, 2), ACT.Copy).then_inc(sem("turned_in"), 1)
        for t in range(0, NT, 2):
            act.wait_ge(sem("d_v"), t + 1)
            act.activation(value[:, 1024 * t:1024 * t + 1024], bank(2 * (t % 4), 2), ACT.Copy).then_inc(sem("d_v_even"), 1)

        def rows_in(i, which):
            ring, low, s = (k_ring, kb_ring, 1.0) if which else (q_ring, qb_ring, DK ** -0.5)
            if i >= 3:
                act.wait_ge(sem("d_scores"), 4 * (i - 2))
            act.wait_ge(sem("d_qk"), 2 * i + which + 1)
            for h in range(2):
                act.activation(two_heads(ring[i % 3])[0:DK, h, :], bank(7)[DK * h:DK * h + DK, :], ACT.Copy, scale=s)\
                   .then_inc(sem("d_qk_in"), 1)
            act.wait_ge(sem("d_qk_in"), 4 * i + 2 * which + 2)
            act.activation(low[i % 3][0:DK, :], ring[i % 3][0:DK, :], ACT.Copy).then_inc(sem("d_bf16"), 1)

        def shift_in(i):
            act.wait_ge(sem("d_shifts"), i + 1)
            act.activation(two_heads(q_ring[i % 3])[DK:DK + 1, 0, :], bank(7)[0:1, :], ACT.Copy).then_inc(sem("d_shift_q"), 1)

        def exp(i, u):
            if i >= 2 and u == 0:
                act.wait_ge(sem("d_weighed"), i - 1)
                act.wait_ge(sem("d_key_sum"), i - 1)
            act.wait_ge(sem("d_scores"), 4 * i + u + 1)
            act.activation(expd[i % 2][:, 1024 * u:1024 * u + 1024], bank(2 * (u % 2), 2), ACT.Exp).then_inc(sem("d_exp"), 1)

        for i in range(2):
            rows_in(i, 0)
            rows_in(i, 1)
        shift_in(0)
        for i in range(NP_):
            for u in range(4):
                if u == 3 and i + 1 < NP_:
                    shift_in(i + 1)
                exp(i, u)
                if u < 2 and i + 2 < NP_:
                    rows_in(i + 2, u)

    def d_dve(dve, follow):
        for t in range(1, NT, 2):
            dve.wait_ge(sem("d_v"), t + 1)
            dve.tensor_copy(value[:, 1024 * t:1024 * t + 1024], bank(2 * (t % 4), 2)).then_inc(sem("d_v_odd"), 1)
        for r in k_ring:
            ins = dve.memset(r[DK:DK + 1, :], 1.0)
        ins.then_inc(sem("d_ones"), 1)

        def maximum(i, qt):
            n = 4 * i + qt
            dve.wait_ge(sem("d_rough"), n + 1)
            if qt == 0 and i >= 2:
                dve.wait_ge(sem("d_shifts"), i - 1)
            dve.tensor_reduce(shift[i % 2][:, 2 * qt:2 * qt + 2], two_heads(bank(4, 2)), AX_X, ALU.max, negate=True)\
               .then_inc(sem("d_max"), 1)

        def shift_in(i):
            dve.wait_ge(sem("d_shifts"), i + 1)
            if i >= 3:
                dve.wait_ge(sem("d_scores"), 4 * (i - 2))
            dve.tensor_copy(two_heads(q_ring[i % 3])[DK:DK + 1, 1, :], bank(7)[32:33, :]).then_inc(sem("d_shift_k"), 1)

        def key_sums(i, h):
            dve.wait_ge(sem("d_exp"), 4 * i + 2 * h + 2)
            if h == 0 and i >= 1:
                dve.wait_ge(sem("d_sums"), i)
            e = expd[i % 2][:, 2048 * h:2048 * h + 2048]
            follow(dve.tensor_tensor(half_sum, e[:, 0:1024], e[:, 1024:], ALU.add))
            ins = dve.tensor_tensor(two_heads(key_sum)[:, h, :], half_sum[:, 0:512], half_sum[:, 512:], ALU.add)
            if h:
                ins.then_inc(sem("d_key_sum"), 1)
            else:
                follow(ins)

        for qt in range(4):
            maximum(0, qt)
        shift_in(0)
        for i in range(NP_ + 1):
            ahead, before = i + 1 < NP_, i >= 1
            if ahead:
                maximum(i + 1, 0)
                maximum(i + 1, 1)
            if before:
                key_sums(i - 1, 0)
            if ahead:
                maximum(i + 1, 2)
            if before:
                key_sums(i - 1, 1)
            if ahead:
                maximum(i + 1, 3)
            if before:
                dve.wait_ge(sem("d_sums"), i)
                dve.reciprocal(unit, bank(7)).then_inc(sem("d_unit"), 1)
            if ahead:
                shift_in(i + 1)
            if before:
                dve.wait_ge(sem("d_weighed"), i)
                dve.wait_ge(sem("d_unit"), i)
                dve.tensor_tensor(headed[:, 512 * (i - 1):512 * i], bank(6), unit, ALU.mult).then_inc(sem("d_headed"), 1)
        dve.wait_ge(sem("d_out"), 1)
        follow(dve.scalar_tensor_tensor(xsum, xs, 2.0, bank(0, 2), ALU.mult, ALU.add))
        norm_stats(dve, follow, tiled(xsum))
        norm_apply(dve, tiled(xsum), tiled(xs)).then_inc(sem("stage_done"), 1)

    E_ = Space(W2.end, END)
    ctx_n, ctx_T = E_(4 * DC), E_(512)
    qkv, ctx_kv = E_(NT * 384), E_(4 * 256)
    squares, ctx_squares = E_(NT * 256), E_(512)
    norm2, rnorm = E_(40), E_(40)
    latT = E_(T)
    q_T, k_T = E_(T), E_(B * KEYS)
    weights = [E_(KEYS) for _ in range(2)]
    neg_max, w_sum, w_unit = E_(16), E_(16), E_(16)
    turned_w = [E_(768) for _ in range(2)]
    heads_T = E_(T)
    q_gain = E_(1)
    mask_row = E_(B * 333)[0:1, :]
    HALF = KEYS // 2
    EI = B * 4 * H_C

    lat_at = width(PACK_MIX)

    def e_sp(sp):
        sp.wait_ge(sem("stage_done"), 4)
        sp.dma_start(SB[:, stream.at:stream.at + width(PACK_EXP)], dram["exp"]).then_inc(sem("exp_in"), 16)

    def e_pool(pool, follow):
        pool.wait_ge(sem("stage_done"), 4)
        follow(pool.memset(mask_row, 0.0))
        m = mask_row.rearrange("p (b k) -> p b k", b=B)[:, :, 0:S2]
        follow(pool.tensor_copy(m, key_bytes.rearrange("p (b k) -> p b k", b=B)))
        follow(pool.tensor_scalar(m, m, 1.0, None, ALU.subtract))
        pool.tensor_scalar(m, m, -NEG, None, ALU.mult).then_inc(sem("e_mask"), 1)
        pool.wait_ge(sem("e_mask"), 1)
        pool_rstd(pool)
        pool_rstd(pool)
        pool.wait_ge(sem("e_norm2"), 1)
        pool.tensor_tensor(rnorm, norm2, minus_half[:, 0:40], ALU.pow).then_inc(sem("e_rnorm"), 1)

    def e_pe(pe):
        pe.wait_ge(sem("e_ctx_n"), 1)
        for i in range(4):
            ins = pe.transpose(bank(2)[0:DC, 128 * i:128 * i + 128], ctx_n[:, DC * i:DC * i + DC], ident)
        ins.then_inc(sem("e_ctx_turned"), 1)
        turn_pe(pe, tiled(xn), 0, (sem("e_normed"), 1))
        pe.wait_ge(sem("e_ctx_T"), 1)
        for i in range(4):
            ins = pe.matmul(bank(4 + i // 2)[:, 256 * (i % 2):256 * (i % 2) + 256], ctx_T[0:DC, 128 * i:128 * i + 128],
                            lat["l_WkvT"][0:DC, :], start=True, stop=True)
        ins.then_inc(sem("e_ctx_kv"), 1)
        pe.wait_ge(sem("turned_in"), 6)
        wide = SB[:, lat_at + 264:lat_at + 264 + 384]
        for t in range(NT):
            if t >= 2:
                pe.wait_ge(sem("e_qkv_in"), t - 1)
            pe.matmul(bank(6 + t % 2)[:, 0:384], latT[:, 128 * t:128 * t + 128], wide, start=True, stop=True)\
              .then_inc(sem("e_qkv"), 1)
        pe.wait_ge(sem("e_scaled"), 1)
        for t in range(NT):
            pe.transpose(PS[:, 128 * t:128 * t + 128], qkv[:, 384 * t:384 * t + 128], ident)
            ins = pe.transpose(PS[:, 1024 + 128 * t:1024 + 128 * t + 128], qkv[:, 384 * t + 128:384 * t + 256], ident)
        for i in range(4):
            ins = pe.transpose(bank(4)[:, 128 * i:128 * i + 128], ctx_kv[:, 256 * i:256 * i + 128], ident)
        ins.then_inc(sem("e_qk_turned"), 1)
        pe.wait_ge(sem("e_qk_T"), 4)
        pe.wait_ge(sem("e_mask"), 1)

        def score(i):
            b, qt, h = i // 8, i // 2 % 4, i % 2
            r = slice(DK * h, DK * h + DK)
            if i >= 2:
                pe.wait_ge(sem("e_exp"), i - 1)
            pe.matmul(bank(2 * (i % 2))[:, 0:HALF], ones[0:1, :], mask_row[:, HALF * b:HALF * b + HALF], start=True, stop=False)
            for n in range(2):
                ins = pe.matmul(bank(2 * (i % 2) + n)[:, 0:HALF], q_T[r, 512 * b + 128 * qt:512 * b + 128 * qt + 128],
                                k_T[r, KEYS * b + HALF * n:KEYS * b + HALF * n + HALF], start=(n == 1), stop=True)
            ins.then_inc(sem("e_scores"), 1)

        def turn(i):
            pe.wait_ge(sem("e_weights"), i + 1)
            if i >= 1:
                pe.wait_ge(sem("e_weights_T"), 2 * i)
            w = weights[i % 2]
            for c in range(5):
                at = 0 if c == 0 else S2 + 128 * (c - 1)
                pe.transpose(PS[:, 2048 + 128 * c:2048 + 128 * c + 128], w[:, at:at + 128], ident)
            pe.transpose(PS[0:REST, 2048 + 640:2048 + 768], w[:, 128:S2], ident).then_inc(sem("e_turned"), 1)

        def weigh(i):
            b, qt, h = i // 8, i // 2 % 4, i % 2
            pe.wait_ge(sem("e_weights_T"), 2 * i + 2)
            o = bank(6 + b)[DK * h:DK * h + DK, 128 * qt:128 * qt + 128]
            w = turned_w[i % 2]
            c0 = 512 * b + 128 + DK * h
            pe.matmul(o, ctx_kv[:, c0:c0 + DK], w[:, 0:128], start=True, stop=False)
            pe.matmul(o, ctx_kv[0:REST, c0 + 256:c0 + 256 + DK], w[0:REST, 640:768], start=False, stop=False)
            for c in range(4):
                v0 = 384 * (4 * b + c) + 256 + DK * h
                ins = pe.matmul(o, qkv[:, v0:v0 + DK], w[:, 128 * (c + 1):128 * (c + 2)], start=False, stop=(c == 3))
            ins.then_inc(sem("e_weighed"), 1)

        for i in range(EI + 2):
            if i < EI:
                score(i)
            if 1 <= i <= EI:
                turn(i - 1)
            if i >= 2:
                weigh(i - 2)
        pe.wait_ge(sem("e_heads"), 1)
        for t in range(NT):
            o = PS[:, 128 * t:128 * t + 128]
            pe.matmul(o, ones[0:1, :], lines["l_bo"][0:1, :], start=True, stop=False)
            ins = pe.matmul(o, heads_T[:, 128 * t:128 * t + 128], lat["l_WoT"], start=False, stop=True)
        ins.then_inc(sem("e_out"), 1)

    def e_act(act):
        act.wait_ge(sem("e_ctx_turned"), 1)
        act.activation(ctx_T[0:DC, :], bank(2)[0:DC, :], ACT.Identity, scale=lat["lx_g"][0:DC, :], bias=lat["lx_b"][0:DC, :])\
           .then_inc(sem("e_ctx_T"), 1)
        act.wait_ge(sem("turned"), 6)
        act.activation(latT, bank(0, 2), ACT.Identity, scale=lat["ll_g"], bias=lat["ll_b"]).then_inc(sem("turned_in"), 1)
        act.wait_ge(sem("e_ctx_kv"), 1)
        act.activation(ctx_kv, bank(4, 2), ACT.Copy).then_inc(sem("e_ctx_kv_raw"), 1)
        for t in range(NT):
            act.wait_ge(sem("e_qkv"), t + 1)
            act.activation(qkv[:, 384 * t:384 * t + 384], bank(6 + t % 2)[:, 0:384], ACT.Copy).then_inc(sem("e_qkv_in"), 1)
        act.wait_ge(sem("e_qk_turned"), 1)
        act.wait_ge(sem("e_gain"), 1)
        act.activation(q_T, bank(0, 2), ACT.Copy, scale=q_gain).then_inc(sem("e_qk_T"), 1)
        k3 = k_T.rearrange("p (b k) -> p b k", b=B)
        act.activation(k3[:, :, S2:], bank(2, 2).rearrange("p (b k) -> p b k", b=B), ACT.Copy, scale=lat["kn_g"])\
           .then_inc(sem("e_qk_T"), 1)
        c4 = bank(4).rearrange("p (b k) -> p b k", b=B)
        act.activation(k3[:, :, 0:S2], c4[:, :, 0:S2], ACT.Copy, scale=lat["kn_g"]).then_inc(sem("e_qk_T"), 2)

        def turned_in(i):
            act.wait_ge(sem("e_turned"), i + 1)
            if i >= 2:
                act.wait_ge(sem("e_weighed"), i - 1)
            w = turned_w[i % 2]
            act.activation(w[:, 0:640], PS[:, 2048:2688], ACT.Copy).then_inc(sem("e_weights_T"), 1)
            act.activation(w[0:REST, 640:768], PS[0:REST, 2688:2816], ACT.Copy).then_inc(sem("e_weights_T"), 1)

        for i in range(EI + 1):
            if i < EI:
                act.wait_ge(sem("e_max"), i + 1)
                if i >= 2:
                    act.wait_ge(sem("e_turned"), i - 1)
                s = bank(2 * (i % 2), 2).rearrange("p (n k) -> p n k", n=2)[:, :, 0:HALF]
                act.activation(weights[i % 2].rearrange("p (n k) -> p n k", n=2), s, ACT.Exp, bias=neg_max[:, i:i + 1],
                               accum_out=w_sum[:, i:i + 1]).then_inc(sem("e_exp"), 1)
            if i >= 1:
                turned_in(i - 1)
        act.wait_ge(sem("e_weighed"), EI)
        act.activation(heads_T, bank(6, 2), ACT.Copy).then_inc(sem("e_heads"), 1)

    def e_dve(dve, follow):
        dve.wait_ge(sem("stage_done"), 4)
        dve.tensor_scalar(q_gain, lat["qn_g"], DK ** -0.5, None, ALU.mult).then_inc(sem("e_gain"), 1)
        c4 = lat["ctx"].rearrange("p (i d) -> p i d", d=DC)
        norm_stats(dve, follow, c4, 4)
        norm_apply(dve, c4, ctx_n.rearrange("p (i d) -> p i d", d=DC), 4).then_inc(sem("e_ctx_n"), 1)
        dve.wait_ge(sem("e_ctx_n"), 1)
        norm_stats(dve, follow, tiled(xs))
        norm_apply(dve, tiled(xs), tiled(xn)).then_inc(sem("e_normed"), 1)
        g = lambda a, n: a.rearrange("p (t g k) -> p t g k", g=n, k=DK)
        dve.wait_ge(sem("e_ctx_kv_raw"), 1)
        ck = ctx_kv.rearrange("p (i w) -> p i w", w=256)[:, :, 0:128]
        csq = ctx_squares.rearrange("p (i w) -> p i w", w=128)
        follow(dve.tensor_tensor(csq, ck, ck, ALU.mult))
        follow(dve.tensor_reduce(norm2[:, 32:40], ctx_squares.rearrange("p (g k) -> p g k", k=DK), AX_X, ALU.add))
        dve.wait_ge(sem("e_qkv_in"), NT)
        qk = qkv.rearrange("p (t w) -> p t w", w=384)[:, :, 0:256]
        follow(dve.tensor_tensor(squares.rearrange("p (t w) -> p t w", w=256), qk, qk, ALU.mult))
        follow(dve.tensor_reduce(norm2[:, 0:32], squares.rearrange("p (g k) -> p g k", k=DK), AX_X, ALU.add))
        dve.tensor_scalar(norm2, norm2, 1.0 / DK, 1e-16, ALU.mult, ALU.max).then_inc(sem("e_norm2"), 1)
        dve.wait_ge(sem("e_rnorm"), 1)
        for t in range(NT):
            q4 = qkv[:, 384 * t:384 * t + 256].rearrange("p (g k) -> p g k", k=DK)
            dve.tensor_tensor(q4, q4, rnorm[:, 4 * t:4 * t + 4][:, :, None].to_broadcast([P, 4, DK]), ALU.mult)
        for i in range(4):
            k2 = ctx_kv[:, 256 * i:256 * i + 128].rearrange("p (g k) -> p g k", k=DK)
            ins = dve.tensor_tensor(k2, k2, rnorm[:, 32 + 2 * i:34 + 2 * i][:, :, None].to_broadcast([P, 2, DK]), ALU.mult)
        ins.then_inc(sem("e_scaled"), 1)
        for i in range(EI + 1):
            if i < EI:
                dve.wait_ge(sem("e_scores"), i + 1)
                s = bank(2 * (i % 2), 2).rearrange("p (n k) -> p n k", n=2)[:, :, 0:HALF]
                dve.tensor_reduce(neg_max[:, i:i + 1], s, mybir.AxisListType.XY, ALU.max, negate=True)\
                   .then_inc(sem("e_max"), 1)
            if i >= 1:
                j = i - 1
                dve.wait_ge(sem("e_exp"), j + 1)
                follow(dve.reciprocal(w_unit[:, j:j + 1], w_sum[:, j:j + 1]))
                dve.tensor_scalar(weights[j % 2], weights[j % 2], w_unit[:, j:j + 1], None, ALU.mult).then_inc(sem("e_weights"), 1)
        dve.wait_ge(sem("e_out"), 1)
        follow(dve.tensor_tensor(xsum, xs, bank(0, 2), ALU.add))
        norm_stats(dve, follow, tiled(xsum))
        norm_apply(dve, tiled(xsum), tiled(xs)).then_inc(sem("stage_done"), 1)

    F_ = Space(W2.end, END)
    hidden = [F_(FCH * T) for _ in range(2)]
    silu = [F_(512) for _ in range(3)]
    logits, marks, hot1, hot2, e_logits, weight = (F_(NT * E1_LIVE) for _ in range(6))
    peak, w_total = F_(NT), F_(NT)
    HIDES = FCH * 2

    def f_rows(k):
        return min(128, FF1 - 128 * k)

    def f_pe(pe):
        turn_pe(pe, tiled(xs), 0, (sem("stage_done"), 5))
        pe.wait_ge(sem("turned_in"), 7)
        for t in range(NT):
            ins = pe.matmul(bank(6)[:, 4 * t:4 * t + 4], xsT[:, 128 * t:128 * t + 128], lat["gate_T"], start=True, stop=True)
        ins.then_inc(sem("top2_logits"), 1)
        pe.wait_ge(sem("exp_in"), 16)

        def hide(i):
            e, k, n = i // HIDES, i % HIDES // 2, i % 2
            if i >= 3:
                pe.wait_ge(sem("top2_hidden"), i - 2)
            m, c = f_rows(k), FF1 * e + 128 * k
            for w, side in (("e_w1", 0), ("e_w3", 1)):
                ins = pe.matmul(bank(2 * (i % 3) + side)[0:m, :], exp_w[w][:, c:c + m], xsT[:, 512 * n:512 * n + 512],
                                start=True, stop=True)
                if side == 0:
                    ins.then_inc(sem("top2_w1"), 1)
            ins.then_inc(sem("top2_w3"), 1)

        def output(e, t):
            j = NT * e + t
            if t == 0:
                pe.wait_ge(sem("top2_hidden"), HIDES * (e + 1))
            if j == 0:
                pe.wait_ge(sem("top2_logits_in"), 1)
            if j >= 2:
                pe.wait_ge(sem("top2_added"), j - 1)
            for k in range(FCH):
                m = f_rows(k)
                w2 = exp_w["e_w2"][0:m, 128 * (FCH * e + k):128 * (FCH * e + k) + 128]
                ins = pe.matmul(bank(6 + j % 2)[:, 0:128], hidden[e % 2][0:m, T * k + 128 * t:T * k + 128 * t + 128], w2,
                                start=(k == 0), stop=(k == FCH - 1))
            ins.then_inc(sem("top2_output"), 1)

        for i in range(HIDES):
            hide(i)
        for e in range(E1_LIVE):
            for s in range(HIDES):
                if e + 1 < E1_LIVE:
                    hide(HIDES * (e + 1) + s)
                if s < NT:
                    output(e, s)

    def f_act(act):
        act.wait_ge(sem("turned"), 7)
        act.activation(xsT, bank(0, 2), ACT.Copy).then_inc(sem("turned_in"), 1)
        act.wait_ge(sem("top2_shifted"), 1)
        act.activation(e_logits, logits, ACT.Exp).then_inc(sem("top2_exp"), 1)
        for i in range(E1_LIVE * HIDES):
            m = f_rows(i % HIDES // 2)
            act.wait_ge(sem("top2_w1"), i + 1)
            if i >= 3:
                act.wait_ge(sem("top2_hidden"), i - 2)
            act.activation(silu[i % 3][0:m, :], bank(2 * (i % 3))[0:m, :], ACT.Silu).then_inc(sem("top2_silu"), 1)

    def f_dve(dve, follow):
        by_token = lambda a: a.rearrange("p (t e) -> p t e", e=E1_LIVE)
        each = lambda a: a[:, :, None].to_broadcast([P, NT, E1_LIVE])
        rank = lat["expert_rank"][:, None, 0:E1_LIVE].to_broadcast([P, NT, E1_LIVE])
        tt = lambda o, a, b, op: follow(dve.tensor_tensor(by_token(o), a, b, op))

        def largest(a, out):
            follow(dve.tensor_reduce(peak, by_token(a), AX_X, ALU.max))
            tt(marks, by_token(a), each(peak), ALU.is_equal)
            tt(marks, by_token(marks), rank, ALU.mult)
            follow(dve.tensor_reduce(peak, by_token(marks), AX_X, ALU.max))
            tt(out, by_token(marks), each(peak), ALU.is_equal)

        dve.wait_ge(sem("top2_logits"), 1)
        dve.tensor_copy(logits, bank(6)[:, 0:NT * E1_LIVE]).then_inc(sem("top2_logits_in"), 1)
        dve.wait_ge(sem("top2_logits_in"), 1)
        follow(dve.tensor_reduce(peak, by_token(logits), AX_X, ALU.max))
        dve.tensor_tensor(by_token(logits), by_token(logits), each(peak), ALU.subtract).then_inc(sem("top2_shifted"), 1)
        dve.wait_ge(sem("top2_shifted"), 1)
        largest(logits, hot1)
        follow(dve.scalar_tensor_tensor(hot2, hot1, NEG, logits, ALU.mult, ALU.add))
        follow(dve.tensor_copy(weight, hot2))
        largest(weight, hot2)
        tt(hot1, by_token(hot1), by_token(hot2), ALU.add)
        dve.wait_ge(sem("top2_exp"), 1)
        tt(weight, by_token(hot1), by_token(e_logits), ALU.mult)
        follow(dve.tensor_reduce(peak, by_token(weight), AX_X, ALU.add))
        follow(dve.reciprocal(w_total, peak))
        tt(weight, by_token(weight), each(w_total), ALU.mult)

        def multiply(i):
            e, k, n = i // HIDES, i % HIDES // 2, i % 2
            m = f_rows(k)
            dve.wait_ge(sem("top2_w3"), i + 1)
            dve.wait_ge(sem("top2_silu"), i + 1)
            if e >= 2 and i % HIDES == 0:
                dve.wait_ge(sem("top2_output"), NT * (e - 1))
            dve.tensor_tensor(hidden[e % 2][0:m, T * k + 512 * n:T * k + 512 * n + 512], silu[i % 3][0:m, :],
                              bank(2 * (i % 3) + 1)[0:m, :], ALU.mult).then_inc(sem("top2_hidden"), 1)

        def add(e, t):
            j = NT * e + t
            dve.wait_ge(sem("top2_output"), j + 1)
            if e:
                dve.wait_ge(sem("top2_added"), j - NT + 1)
            dve.scalar_tensor_tensor(tiled(xsum)[:, t, :], bank(6 + j % 2)[:, 0:128], weight[:, 4 * t + e:4 * t + e + 1],
                                     tiled(xsum if e else xs)[:, t, :], ALU.mult, ALU.add).then_inc(sem("top2_added"), 1)

        for i in range(HIDES):
            multiply(i)
        for e in range(E1_LIVE):
            for s in range(HIDES):
                if e + 1 < E1_LIVE:
                    multiply(HIDES * (e + 1) + s)
                if s < NT:
                    add(e, s)
        dve.wait_ge(sem("top2_added"), NT * E1_LIVE)
        norm_stats(dve, follow, tiled(xsum))
        norm_apply(dve, tiled(xsum), tiled(xs)).then_inc(sem("stage_done"), 1)

    block = ctx.enter_context(nc.Block())

    @block.sync
    def _(sp):
        a_sp(sp)
        c_sp(sp)
        e_sp(sp)
        sp.wait_ge(sem("stage_done"), 6)
        sp.dma_start(dram["out"].rearrange("b (c p) d -> p (b c) d", p=P), tiled(xs)).then_inc(sem("out_written"), 16)
        sp.wait_ge(sem("out_written"), 16)

    @block.tensor
    def _(pe):
        a_pe(pe)
        b_pe_pre(pe)
        b_pe_attention(pe)
        b_pe_ssm(pe)
        c_pe(pe)
        d_pe(pe)
        e_pe(pe)
        f_pe(pe)

    @block.scalar
    def _(act):
        a_act(act)
        b_act_pre(act)
        b_act_tables(act)
        b_act_attention(act)
        b_act_ssm(act)
        c_act(act)
        d_act(act)
        e_act(act)
        f_act(act)

    @block.gpsimd
    def _(pool):
        follow = chain(pool, "pool_step")
        pool.wait_ge(sem("ones_set"), 2)
        pool_rstd(pool)
        b_pool_pre(pool, follow)
        pool_rstd(pool)
        b_pool_attention(pool, follow)
        for _ in range(3):
            pool_rstd(pool)
        for _ in range(3):
            pool_rstd(pool)
        pool_rstd(pool)
        e_pool(pool, follow)
        pool_rstd(pool)
        pool_rstd(pool)

    @block.vector
    def _(dve):
        follow = chain(dve, "dve_step")
        a_dve(dve, follow)
        b_dve_norm(dve, follow)
        b_dve_tables(dve, follow)
        b_dve_attention(dve, follow)
        b_dve_ssm(dve, follow)
        c_dve(dve, follow)
        d_dve(dve, follow)
        e_dve(dve, follow)
        f_dve(dve, follow)


def _constants():
    n = np.arange(512)
    turn = 2.0 * np.pi * ((n[:, None] * n[None, :]) % 1024) / 1024.0
    cos, sin = np.cos(turn), -np.sin(turn)
    nyquist = 1.0 - 2.0 * (n % 2)
    fwd, inv = sin.copy(), sin.copy()
    fwd[:, 0] = nyquist
    inv[0, :] = nyquist
    rows = lambda a: a.reshape(4, 128, 512).transpose(1, 0, 2).reshape(128, 2048)
    p = np.arange(128)
    weight = np.full((128, 4), 4.0 / 1024)
    weight[0, 0] = 2.0 / 1024
    pick = np.zeros((128, 2, 128))
    pick[0, 0] = pick[1, 1] = 1.0
    return {
        "dft_cos": rows(cos), "dft_sin": rows(fwd), "inv_sin0": inv[:128], "ident": np.eye(128),
        "pair_sum": p[:, None] // 2 == p[None, :] // 2, "head_sum": p[:, None] // 32 == p[None, :] // 32,
        "earlier": p[:, None] < p[None, :], "low_lags": np.tile(np.arange(LOW), (128, 1)),
        "high_lags": np.tile(LOW * np.arange(HIGH), (128, 1)), "quarter": 0.25 * (p < 64)[:, None],
        "quarter_angle": 0.25 * TWO_PI * (p < 64)[:, None], "bin_weight": weight,
        "expert_rank": np.tile(8.0 - np.arange(8), (128, 1)), "head_pick": pick.reshape(128, 256),
    }


def _layout(i):
    f = lambda a: np.asarray(a, np.float32)
    col = lambda a: a.reshape(-1, 1)
    tiles = lambda a, n: a.reshape(-1, 128, n).transpose(1, 0, 2).reshape(128, -1)
    x = i["x"].reshape(T, D)
    ctx = i["ctx_768"]
    ctx_tm = np.zeros((2, 2, 128, DC), np.float32)
    ctx_tm[:, 0] = ctx[:, :128]
    ctx_tm[:, 1, :REST] = ctx[:, 128:]
    b1 = np.zeros((4, 128, E0, E0), np.float32)
    for e in range(E0):
        b1[:, :, e, e] = i["L0_ffn_b1"][e].reshape(4, 128)
    w2 = np.zeros((E1_LIVE, FCH * 128, 128), np.float32)
    w2[:, :FF1] = i["L1_ffn_w2"][:E1_LIVE]
    qkv = i["L0_ffn_in_proj_b"]
    names = {
        "xT": x.T, "x": tiles(x, D), "W_in": i["L0_attn_W_in"], "W_out": i["L0_attn_W_out"],
        "lower": col(i["L0_attn_lower_bound"]),
        "A_re": i["L0_xattn_A_re"], "A_im": i["L0_xattn_A_im"], "C_re": i["L0_xattn_C_re"],
        "C_im": i["L0_xattn_C_im"], "log_dt": col(i["L0_xattn_log_dt"]),
        "Wq_T": i["L0_xattn_Wq"].T, "Wk": i["L0_xattn_Wk"], "Wv": i["L0_xattn_Wv"],
        "ctx_T": ctx.reshape(B * S2, DC).T,
        "W_film": np.concatenate([i["L0_xattn_W_film_in"], i["L0_xattn_W_film_out"]], 1),
        "W1": i["L0_xattn_W1"], "W2": tiles(i["L0_xattn_W2"], 128), "ffn_b1": i["L0_xattn_b1"].reshape(4, 128).T,
        "ffn_g": col(i["L0_xattn_g_ffn"]), "ffn_b": col(i["L0_xattn_b_ffn"]),
        "m_w1T": tiles(i["L0_ffn_w1"].transpose(0, 2, 1).reshape(E0 * FF0, D), D),
        "m_w2": tiles(i["L0_ffn_w2"].reshape(E0 * FF0, D), D),
        "m_b1": b1.transpose(1, 0, 2, 3).reshape(128, 256),
        "qkv_T": i["L0_ffn_in_proj_w"].T, "ow_T": i["L0_ffn_out_proj_w"].T, "m_wg": i["L0_ffn_wg"],
        "b_q": col(qkv[:128]), "b_v": col(qkv[256:]), "ln1_g": col(i["L0_ffn_ln1_g"]),
        "ln1_b": col(i["L0_ffn_ln1_b"]), "m_b2": i["L0_ffn_b2"],
        "w_q": i["L1_attn_w_q"].transpose(1, 0, 2).reshape(D, -1),
        "w_k": i["L1_attn_w_k"].transpose(1, 0, 2).reshape(D, -1),
        "w_v": i["L1_attn_w_v"].transpose(1, 0, 2).reshape(D, -1), "w_o": tiles(i["L1_attn_w_o"], D),
        "l_WqT": i["L1_xattn_Wq"].T, "l_WkvT": i["L1_xattn_Wkv"].T, "l_WlkvT": i["L1_xattn_Wlkv"].T,
        "l_WoT": i["L1_xattn_Wo"].T, "ctx": ctx_tm.transpose(2, 0, 1, 3).reshape(128, -1),
        "lx_g": col(i["L1_xattn_ln_x_g"]), "lx_b": col(i["L1_xattn_ln_x_b"]),
        "ll_g": col(i["L1_xattn_ln_l_g"]), "ll_b": col(i["L1_xattn_ln_l_b"]),
        "qn_g": col(np.tile(i["L1_xattn_qn_g"], 2)), "kn_g": col(np.tile(i["L1_xattn_kn_g"], 2)),
        "gate_T": i["L1_ffn_gate_w"][:E1_LIVE].T,
        "e_w1": i["L1_ffn_w1"][:E1_LIVE].transpose(1, 0, 2).reshape(D, -1),
        "e_w3": i["L1_ffn_w3"][:E1_LIVE].transpose(1, 0, 2).reshape(D, -1),
        "e_w2": tiles(w2.reshape(-1, D), D),
    }
    names.update(_constants())
    packed = {}
    for key, pack in PACKS.items():
        a = np.zeros((128, width(pack)), np.float32)
        at = 0
        for name, n in pack:
            v = f(names[name])
            a[:v.shape[0], at:at + n] = v
            at += n
        packed[key] = a
    rows = {"g_in": "L0_xattn_g_norm_in", "b_in": "L0_xattn_b_norm_in", "g_out": "L0_xattn_g_norm_out",
            "b_out": "L0_xattn_b_norm_out", "n1_g": "L0_ffn_ln1_g", "n1_b": "L0_ffn_ln1_b", "n2_g": "L0_ffn_ln2_g",
            "n2_b": "L0_ffn_ln2_b"}
    packed["rows"] = np.concatenate([f(i[rows[r]]) for r in ROWS]).reshape(1, -1)
    packed["lines"] = np.concatenate([f(i["L0_xattn_b2"]), f(i["L0_ffn_out_proj_b"]), f(i["L1_xattn_bo"]),
                                      f(i["L0_xattn_b_film_in"]), f(i["L0_xattn_b_film_out"])]).reshape(1, -1)
    packed["mod_gate"] = f(i["L0_xattn_mod_gate"]).reshape(1, 1)
    packed["d_skip"] = f(i["L0_xattn_D_skip"]).reshape(1, 128)
    packed["text_mask"] = np.ascontiguousarray(i["mask_BxS_bf1"].reshape(NT, 128).T)
    packed["ctx_mask"] = i["mask_BxS2_bf1"].reshape(1, B * S2)
    packed["key_mask"] = i["mask_BxS2_bk0"].reshape(1, B * S2)
    return packed


def kernel(**inputs):
    import concourse.bacc as bacc
    from concourse.bass_utils import run_bass_kernel_spmd

    inputs = {k: np.asarray(v) for k, v in inputs.items()}
    arrays = _layout(inputs)
    nc = bacc.Bacc("TRN2", target_bir_lowering=False, num_devices=1)
    aps = {k: nc.dram_tensor(k, a.shape, mybir.dt.from_np(a.dtype), kind="ExternalInput").ap()
           for k, a in arrays.items()}
    aps["out"] = nc.dram_tensor("out", (B, S, D), F32, kind="ExternalOutput").ap()
    build(nc, aps)
    r = run_bass_kernel_spmd(nc, [arrays], core_ids=[0])
    return r.results[0]["out"]
```

```python
from contextlib import ExitStack

import concourse.bass as bass
import numpy as np
from concourse import mybir

F32 = mybir.dt.float32
BF16 = mybir.dt.bfloat16
U8 = mybir.dt.uint8
ALU = mybir.AluOpType
ACT = mybir.ActivationFunctionType
AX_X = mybir.AxisListType.X

P = 128
B, S, D = 2, 512, 128
T = B * S
NT = T // P
S2, DC = 154, 96
REST = S2 - P
EPS = 1e-5
NEG = -1.0e30
GONE = -3.0e38
MAGIC = 12582912.0
TWO_PI = 6.2831845
H_X, DH_X, TOP = 4, 32, 32
N_ST, LOW, HIGH = 64, 32, 16
FF0, E0, CAP = 512, 8, 128
H_L, DK = 16, 64
PAIRS = H_L // 2
H_C = 2
KEYS = S2 + S
E1, E1_LIVE, FF1 = 8, 4, 704
FCH = 6

PACK_MIX = [("xT", T), ("W_in", 384), ("lower", 1), ("ident", 128), ("pair_sum", 128), ("x", T), ("W_out", 128)]
PACK_SSM = [("A_re", N_ST), ("A_im", N_ST), ("C_re", N_ST), ("C_im", N_ST), ("log_dt", 1), ("low_lags", LOW),
            ("high_lags", HIGH), ("quarter", 1), ("quarter_angle", 1), ("bin_weight", 4), ("Wq_T", 128), ("Wk", 128),
            ("Wv", 128), ("ctx_T", B * S2), ("W_film", 512)]
PACK_DFT = [("dft_cos", 2048), ("dft_sin", 2048), ("inv_sin0", 512)]
PACK_FFN = [("W1", 512), ("W2", 512), ("ffn_b1", 4), ("ffn_g", 1), ("ffn_b", 1)]
PACK_MOE = [("m_w1T", 4096), ("m_w2", 4096)]
PACK_MHA = [("m_b1", 256), ("qkv_T", 384), ("ow_T", 128), ("m_wg", 8), ("b_q", 1), ("b_v", 1), ("ln1_g", 1),
            ("ln1_b", 1), ("head_sum", 128), ("earlier", 128), ("m_b2", 128)]
PACK_ATT = [("w_q", 1024), ("w_k", 1024), ("w_v", 1024), ("w_o", 1024), ("head_pick", 256)]
PACK_LAT = [("expert_rank", 8), ("l_WkvT", 256), ("l_WqT", 128), ("l_WlkvT", 256), ("l_WoT", 128), ("ctx", 4 * DC), ("lx_g", 1),
            ("lx_b", 1), ("ll_g", 1), ("ll_b", 1), ("qn_g", 1), ("kn_g", 1), ("gate_T", E1_LIVE)]
PACK_EXP = [("e_w1", E1_LIVE * FF1), ("e_w3", E1_LIVE * FF1), ("e_w2", E1_LIVE * FCH * 128)]
ROWS = ["g_in", "b_in", "g_out", "b_out", "n1_g", "n1_b", "n2_g", "n2_b"]
LINES = [("ffn_b2", 128), ("m_ob", 128), ("l_bo", 128), ("b_film", 512)]


def width(pack):
    return sum(n for _, n in pack)


def views(pack, ap):
    out, at = {}, 0
    for name, n in pack:
        out[name] = ap[:, at:at + n]
        at += n
    return out


PACKS = {"mix": PACK_MIX, "ssm": PACK_SSM, "dft": PACK_DFT, "ffn": PACK_FFN, "moe": PACK_MOE, "mha": PACK_MHA,
         "att": PACK_ATT, "lat": PACK_LAT, "exp": PACK_EXP}


def build(nc, dram):
    with ExitStack() as ctx:
        _build(nc, dram, ctx)


def _build(nc, dram, ctx):
    semaphores = {}

    def sem(name):
        if name not in semaphores:
            semaphores[name] = ctx.enter_context(nc.semaphore(name))
        return semaphores[name]

    SB = ctx.enter_context(nc.sbuf_tensor("SB", [P, 53200], F32))
    PS = ctx.enter_context(nc.psum_tensor("PS", [P, 4096], F32))

    def bank(i, n=1):
        return PS[:, 512 * i:512 * (i + n)]

    class Space:

        def __init__(self, at, end):
            self.at, self.end = at, end

        def __call__(self, n, dtype=F32):
            a = SB[:, self.at:self.at + n]
            self.at += n
            assert self.at <= self.end, (self.at, self.end)
            return a if dtype == F32 else a.bitcast(dtype)

    def tiled(a, n=NT):
        return a.rearrange("p (t d) -> p t d", t=n)

    keep = Space(0, 7200)
    mix = views(PACK_MIX, keep(width(PACK_MIX)))
    lat = views(PACK_LAT, keep(width(PACK_LAT)))
    rows = {name: keep(128) for name in ROWS}
    lines = views(LINES, keep(sum(n for _, n in LINES)))
    mod_gate, text_mask = keep(1), keep(NT)
    ones, minus_half, stats, moments = keep(128), keep(40), keep(NT * 6), keep(NT * 2)
    variance, rstd = keep(NT), keep(NT)
    bytes_in = keep(1000).bitcast(U8)
    text_bytes, ctx_bytes, key_bytes = bytes_in[:, 0:NT], bytes_in[0:1, 1024:1024 + B * S2], bytes_in[0:1, 2048:2048 + B * S2]
    stream = Space(keep.at, keep.at + 4096)
    xs, xsT, xn, xsum = (stream(T) for _ in range(4))
    W = Space(stream.at, stream.at + 8792)
    ssm, dft, ffn = (views(pk, W(width(pk))) for pk in (PACK_SSM, PACK_DFT, PACK_FFN))
    exp_w = views(PACK_EXP, Space(stream.at, stream.at + 8792)(width(PACK_EXP)))
    W2 = Space(W.end, W.end + width(PACK_ATT))
    att = views(PACK_ATT, W2(width(PACK_ATT)))
    free_at = W2.end
    END = 53200
    ident = mix["ident"]

    def chain(engine, name):
        done = sem(name)
        count = [0]

        def follow(ins):
            count[0] += 1
            ins.then_inc(done, 1)
            engine.wait_ge(done, count[0])
        return follow

    norms = [0, 0]

    def norm(dve, follow, src, out, n=NT, first_half=None):
        halves = [(0, n // 2), (n // 2, n)]
        for a, z in halves:
            for t in range(a, z):
                ins = dve.bn_stats(tiled(stats)[:, t, :], src[:, t, :])
            follow(ins)
            for t in range(a, z):
                ins = dve.bn_aggr(moments.rearrange("p (t m) -> p t m", m=2)[:, t, :], tiled(stats)[:, t, :])
            follow(ins)
            dve.tensor_scalar(variance[:, a:z], moments.rearrange("p (t m) -> p m t", m=2)[:, 1, a:z], EPS, None,
                              ALU.add).then_inc(sem("norm_variance"), 1)
        for k, (a, z) in enumerate(halves):
            norms[0] += 1
            dve.wait_ge(sem("norm_rstd"), norms[0])
            for t in range(a, z):
                ins = dve.tensor_scalar(out[:, t, :], src[:, t, :], moments[:, 2 * t:2 * t + 1], rstd[:, t:t + 1],
                                        ALU.subtract, ALU.mult)
            if k == 0 and first_half is not None:
                ins.then_inc(sem(first_half), 1)
        return ins

    def pool_rstd(pool, n=NT):
        for a, z in ((0, n // 2), (n // 2, n)):
            norms[1] += 1
            pool.wait_ge(sem("norm_variance"), norms[1])
            pool.tensor_tensor(rstd[:, a:z], variance[:, a:z], minus_half[:, a:z], ALU.pow).then_inc(sem("norm_rstd"), 1)

    turns = [0, 0, 0]

    def turn_pe(pe, src, b0, wait, first_half=None):
        turns[0] += 1
        for t in range(NT):
            if t == 0:
                pe.wait_ge(*(first_half or wait))
            if t == NT // 2 and first_half:
                pe.wait_ge(*wait)
            ins = pe.transpose(PS[:, 512 * b0 + 128 * t:512 * b0 + 128 * t + 128], src[:, t, :], ident)
        ins.then_inc(sem("turned"), 1)

    A = Space(END - 7 * T - 1, END)
    gate_v, gate_q, forget, keys, qk, carried, mixed = (A(T) for _ in range(7))
    one_less = A(1)

    def a_sp(sp):
        a0 = W.end - 8792
        n_table = 4 * N_ST + 1 + LOW + HIGH + 6
        sp.dma_start(SB[:, a0:a0 + n_table], dram["ssm"][:, 0:n_table]).then_inc(sem("table_in"), 16)
        sp.dma_start(SB[:, 0:T + 384 + 129], dram["mix"][:, 0:T + 384 + 129]).then_inc(sem("mix_in"), 16)
        sp.dma_start(SB[:, T + 513:width(PACK_MIX)], dram["mix"][:, T + 513:]).then_inc(sem("mix_in2"), 16)
        sp.dma_start(SB[:, a0 + n_table:a0 + width(PACK_SSM)], dram["ssm"][:, n_table:]).then_inc(sem("ssm_in"), 16)
        r0 = width(PACK_MIX) + width(PACK_LAT)
        sp.dma_start(SB[:, r0:r0 + 1024], dram["rows"].to_broadcast([P, 8 * D])).then_inc(sem("small_in"), 16)
        sp.dma_start(SB[0:1, r0 + 1024:r0 + 1024 + 896], dram["lines"]).then_inc(sem("small_in"), 16)
        sp.dma_start(mod_gate, dram["mod_gate"].to_broadcast([P, 1])).then_inc(sem("small_in"), 16)
        sp.dma_start(text_bytes, dram["text_mask"]).then_inc(sem("small_in"), 16)
        sp.dma_start(ctx_bytes, dram["ctx_mask"]).then_inc(sem("small_in"), 16)
        sp.dma_start(key_bytes, dram["key_mask"]).then_inc(sem("small_in"), 16)
        sp.dma_start(film_line, dram["lines"][:, 384:896]).then_inc(sem("small_in"), 16)
        sp.dma_start(skip_line, dram["d_skip"]).then_inc(sem("small_in"), 16)
        a1 = a0 + width(PACK_SSM)
        sp.dma_start(SB[:, a1:a1 + width(PACK_DFT)], dram["dft"]).then_inc(sem("dft_in"), 16)
        a2 = a1 + width(PACK_DFT)
        sp.dma_start(SB[:, a2:a2 + width(PACK_FFN)], dram["ffn"]).then_inc(sem("ffn_in"), 16)
        sp.dma_start(SB[:, W2.end - width(PACK_ATT):W2.end], dram["att"]).then_inc(sem("att_in"), 16)
        l0 = width(PACK_MIX)
        sp.dma_start(SB[:, l0:l0 + width(PACK_LAT)], dram["lat"]).then_inc(sem("lat_in"), 16)

    SMALL = 16 * 8

    def a_pe(pe):
        pe.wait_ge(sem("mix_in"), 16)
        for m in range(3):
            for n in range(2):
                pe.matmul(bank(2 * m + n), mix["W_in"][:, 128 * m:128 * m + 128], mix["xT"][:, 512 * n:512 * n + 512],
                          start=True, stop=True).then_inc(sem("a_features"), 1)
        pe.wait_ge(sem("s_stack"), 1)
        for i in range(4):
            ins = pe.transpose(bank(7)[:, 128 * i:128 * i + 128], stack[:, 128 * i:128 * i + 128], ident)
        ins.then_inc(sem("s_stack_turned"), 1)
        pe.wait_ge(sem("mix_in2"), 16)
        pe.wait_ge(sem("s_stack_in"), 1)
        pe.wait_ge(sem("a_products"), 1)
        for n in range(2):
            pe.matmul(bank(6 + n), mix["pair_sum"], qk[:, 512 * n:512 * n + 512], start=True, stop=True)
        pe.wait_ge(sem("a_products"), 2)
        pe.matmul(bank(0), mix["pair_sum"], carried[:, 512:1024], start=True, stop=True).then_inc(sem("a_sums"), 1)
        pe.wait_ge(sem("a_mixed"), 1)
        for t in range(NT):
            ins = pe.matmul(PS[:, 1024 + 128 * t:1024 + 128 * t + 128], mixed[:, 128 * t:128 * t + 128], mix["W_out"],
                            start=True, stop=True)
        ins.then_inc(sem("a_out"), 1)

    def a_act(act):
        b_act_stack(act)
        act.wait_ge(sem("a_features"), 2)
        act.activation(gate_v, bank(0, 2), ACT.Gelu).then_inc(sem("a_gates"), 1)
        act.wait_ge(sem("a_features"), 4)
        act.activation(gate_q, bank(2, 2), ACT.Gelu).then_inc(sem("a_gates"), 1)
        act.wait_ge(sem("a_features"), 6)
        act.activation(forget, bank(4, 2), ACT.Sigmoid, scale=-1.0).then_inc(sem("a_gates"), 1)

    def a_dve(dve, follow):
        dve.memset(ones, 1.0).then_inc(sem("ones_set"), 1)
        dve.memset(minus_half, -0.5).then_inc(sem("ones_set"), 1)
        dve.wait_ge(sem("mix_in"), 16)
        follow(dve.tensor_scalar(one_less, mix["lower"], -1.0, 1.0, ALU.mult, ALU.add))
        b_dve_stack(dve, follow)
        dve.wait_ge(sem("a_gates"), 3)
        follow(dve.tensor_scalar(keys, forget, one_less, None, ALU.mult))
        dve.tensor_tensor(qk, gate_q, keys, ALU.mult).then_inc(sem("a_products"), 1)
        follow(dve.scalar_tensor_tensor(carried[:, 0:512], keys[:, 512:], 1.0, keys[:, 0:512], ALU.subtract, ALU.mult))
        dve.tensor_tensor(carried[:, 512:], gate_q[:, 512:], carried[:, 0:512], ALU.mult).then_inc(sem("a_products"), 1)
        dve.wait_ge(sem("a_sums"), 1)
        dve.tensor_tensor(mixed[:, 0:512], gate_v[:, 0:512], bank(6), ALU.mult)
        dve.tensor_tensor(carried[:, 0:512], gate_v[:, 0:512], bank(0), ALU.mult)
        follow(dve.tensor_tensor(qk[:, 0:512], gate_v[:, 512:], bank(7), ALU.mult))
        dve.tensor_tensor(mixed[:, 512:], qk[:, 0:512], carried[:, 0:512], ALU.subtract).then_inc(sem("a_mixed"), 1)
        dve.wait_ge(sem("a_out"), 1)
        dve.wait_ge(sem("mix_in2"), 16)
        dve.tensor_tensor(xsum, mix["x"], bank(2, 2), ALU.add).then_inc(sem("a_out_read"), 1)
        dve.wait_ge(sem("a_out_read"), 1)
        norm(dve, follow, tiled(xsum), tiled(xs), first_half="stage_half").then_inc(sem("stage_done"), 1)

    Bf = Space(free_at, END)
    film_line = Bf(512)[32:33, :]
    skip_line = Bf(128)[0:1, :]
    K_T, V_T, score_w, mask_line = Bf(B * S2), Bf(B * S2), Bf(B * H_X * S2), Bf(2 * B * S2)[0:1, :]
    film_w, vf0, vf1 = Bf(512), Bf(1024), Bf(1024)
    taps_re, taps_im, taps_re2, taps_im2 = (Bf(512) for _ in range(4))
    u_n = Bf(T)
    after_small = Bf.at
    Tb = Space(after_small, END)
    d_tab = Tb(20 * N_ST)
    stack, stack_T = Tb(512), Tb(512)
    d_dt = Tb(1)
    taps = Tb(512)
    selection_at = Tb.at
    low_e, high_k, low_k, low_r = (Tb(4096) for _ in range(4))
    high_r, high_e = low_r[:, 0:2048], low_r[:, 2048:]
    Sel = Space(selection_at, selection_at + 8192)
    best, best_exp = Sel(NT * H_X * TOP), Sel(NT * H_X * TOP)
    minus_max, total, share = Sel(NT * H_X), Sel(NT * H_X), Sel(NT * H_X)
    all_exp, rest_exp, left = ([Sel(S2) for _ in range(4)] for _ in range(3))
    probs, diag = [Sel(S2) for _ in range(8)], [Sel(128) for _ in range(4)]
    scored = [d_tab[:, 0:H_X * S2], d_tab[:, H_X * S2:2 * H_X * S2]]
    attn0 = Sel(T)
    Late = Space(selection_at + 8192, END)
    film = Late(NT * 512)
    attn1 = Late(T)
    Bf.at = Late.at
    after_attn = Bf.at

    def dt_(i):
        return d_tab[:, N_ST * i:N_ST * i + N_ST]

    def lag(a, n):
        return a.rearrange("p (d l) -> p d l", l=n)

    def b_dve_stack(dve, follow):
        tt = lambda o, a, b, op: follow(dve.tensor_tensor(o, a, b, op))
        dve.wait_ge(sem("table_in"), 16)
        dve.wait_ge(sem("s_dt"), 1)
        a_re, a_im = dt_(0), dt_(1)
        follow(dve.tensor_scalar(a_re, ssm["A_re"], d_dt, None, ALU.mult))
        dve.tensor_scalar(a_im, ssm["A_im"], d_dt, float(1.0 / (2.0 * np.pi)), ALU.mult, ALU.mult).then_inc(sem("s_dta"), 1)
        dve.wait_ge(sem("s_dta"), 1)
        dve.tensor_scalar(dt_(2), a_im, 0.25, None, ALU.add)
        follow(dve.tensor_copy(dt_(3), a_im))
        follow(dve.tensor_scalar(d_tab[:, 4 * N_ST:6 * N_ST], d_tab[:, 2 * N_ST:4 * N_ST], MAGIC, None, ALU.add))
        dve.scalar_tensor_tensor(d_tab[:, 4 * N_ST:6 * N_ST], d_tab[:, 4 * N_ST:6 * N_ST], MAGIC,
                                 d_tab[:, 2 * N_ST:4 * N_ST], ALU.subtract, ALU.subtract).then_inc(sem("s_turns"), 1)
        dve.wait_ge(sem("s_trig"), 2)
        cos, sin, er = dt_(6), dt_(7), dt_(8)
        tt(dt_(9), er, cos, ALU.mult)
        tt(dt_(10), er, sin, ALU.mult)
        follow(dve.tensor_scalar(dt_(9), dt_(9), -1.0, None, ALU.add))
        Ar, Ai, Cr, Ci = ssm["A_re"], ssm["A_im"], ssm["C_re"], ssm["C_im"]
        tt(dt_(11), dt_(9), Ar, ALU.mult)
        tt(dt_(12), dt_(10), Ai, ALU.mult)
        tt(dt_(11), dt_(11), dt_(12), ALU.add)
        tt(dt_(12), dt_(10), Ar, ALU.mult)
        tt(dt_(13), dt_(9), Ai, ALU.mult)
        tt(dt_(12), dt_(12), dt_(13), ALU.subtract)
        tt(dt_(13), Ar, Ar, ALU.mult)
        tt(dt_(14), Ai, Ai, ALU.mult)
        tt(dt_(13), dt_(13), dt_(14), ALU.add)
        follow(dve.reciprocal(dt_(13), dt_(13)))
        tt(dt_(11), dt_(11), dt_(13), ALU.mult)
        tt(dt_(12), dt_(12), dt_(13), ALU.mult)
        tt(dt_(14), Cr, dt_(11), ALU.mult)
        tt(dt_(15), Ci, dt_(12), ALU.mult)
        tt(dt_(16), Cr, dt_(12), ALU.mult)
        tt(dt_(17), Ci, dt_(11), ALU.mult)
        s = stack.rearrange("p (k n) -> p k n", n=N_ST)
        tt(s[:, 4, :], dt_(14), dt_(15), ALU.subtract)
        tt(dt_(18), dt_(16), dt_(17), ALU.add)
        for k, src, f in ((0, a_im, 1.0), (1, a_im, 1.0), (2, a_re, 1.0), (3, a_re, 1.0), (5, dt_(18), -1.0),
                          (6, dt_(18), -1.0), (7, s[:, 4, :], -1.0)):
            ins = dve.tensor_scalar(s[:, k, :], src, f, None, ALU.mult)
        ins.then_inc(sem("s_stack"), 1)
        dve.wait_ge(sem("s_stack_turned"), 1)
        dve.tensor_copy(stack_T, bank(7)).then_inc(sem("s_stack_in"), 1)

    turn_T, rate_T, u_T, v_T = (stack_T[:, 128 * i:128 * i + 128] for i in range(4))

    def b_dve_tables(dve, follow):
        tt = lambda o, a, b, op: follow(dve.tensor_tensor(o, a, b, op))
        every = lambda a, n: a[:, :, None].to_broadcast([P, 128, n])
        lags = lambda a, n: a[:, None, :].to_broadcast([P, 128, n])
        dve.wait_ge(sem("a_mixed"), 1)
        dve.tensor_tensor(lag(low_e, LOW), every(rate_T, LOW), lags(ssm["low_lags"], LOW), ALU.mult).then_inc(sem("s_rates"), 1)
        tt(lag(low_r, LOW), every(turn_T, LOW), lags(ssm["low_lags"], LOW), ALU.mult)
        follow(dve.tensor_scalar(low_k, low_r, ssm["quarter"], MAGIC, ALU.add, ALU.add))
        dve.scalar_tensor_tensor(low_k, low_k, MAGIC, low_r, ALU.subtract, ALU.subtract).then_inc(sem("s_angles"), 1)
        dve.wait_ge(sem("s_angles"), 1)
        dve.tensor_tensor(lag(high_e, HIGH), every(rate_T, HIGH), lags(ssm["high_lags"], HIGH), ALU.mult).then_inc(sem("s_rates"), 1)
        tt(lag(high_r, HIGH), every(turn_T, HIGH), lags(ssm["high_lags"], HIGH), ALU.mult)
        dve.tensor_scalar(high_k[:, 0:2048], high_r, 0.25, MAGIC, ALU.add, ALU.add)
        follow(dve.tensor_scalar(high_k[:, 2048:], high_r, MAGIC, None, ALU.add))
        for h in range(2):
            ins = dve.scalar_tensor_tensor(high_k[:, 2048 * h:2048 * h + 2048], high_k[:, 2048 * h:2048 * h + 2048],
                                           MAGIC, high_r, ALU.subtract, ALU.subtract)
        ins.then_inc(sem("s_angles"), 1)

    def b_dve_factors(dve, follow):
        tt = lambda o, a, b, op: follow(dve.tensor_tensor(o, a, b, op))
        every = lambda a, n: a[:, :, None].to_broadcast([P, 128, n])
        dve.wait_ge(sem("s_tables"), 3)
        tt(low_k, low_k, low_e, ALU.mult)
        dve.wait_ge(sem("s_tables"), 5)
        dve.tensor_tensor(lag(high_k[:, 0:2048], HIGH), lag(high_k[:, 0:2048], HIGH), every(u_T, HIGH), ALU.mult)
        follow(dve.tensor_tensor(lag(high_k[:, 2048:], HIGH), lag(high_k[:, 2048:], HIGH), every(v_T, HIGH), ALU.mult))
        tt(high_r, high_k[:, 0:2048], high_k[:, 2048:], ALU.add)
        dve.tensor_tensor(high_r, high_r, high_e, ALU.mult).then_inc(sem("s_factors"), 1)

    def b_dve_skip(dve, follow):
        dve.wait_ge(sem("s_taps_copied"), 4)
        dve.wait_ge(sem("small_in"), SMALL)
        follow(dve.tensor_scalar(skip_line, skip_line, 0.5, None, ALU.mult))
        dve.tensor_tensor(taps[0:1, 0:128], taps[0:1, 0:128], skip_line, ALU.add).then_inc(sem("s_taps_in"), 1)

    def b_dve_spectrum(dve, follow):
        dve.wait_ge(sem("s_taps_dft"), 1)
        for j in range(4):
            dve.tensor_scalar(taps_re[:, 128 * j:128 * j + 128], bank(6)[:, 128 * j:128 * j + 128],
                              ssm["bin_weight"][:, j:j + 1], None, ALU.mult)
            ins = dve.tensor_scalar(taps_im[:, 128 * j:128 * j + 128], bank(7)[:, 128 * j:128 * j + 128],
                                    ssm["bin_weight"][:, j:j + 1], None, ALU.mult)
        follow(ins)
        follow(dve.tensor_copy(taps_re2, taps_re))
        dve.tensor_copy(taps_re2[0:1, 0:128], taps_im[0:1, 0:128])
        follow(dve.tensor_copy(taps_im2, taps_im))
        dve.memset(taps_im2[0:1, 0:128], 0.0).then_inc(sem("s_spectrum"), 1)

    def b_act_stack(act):
        act.wait_ge(sem("table_in"), 16)
        act.activation(d_dt, ssm["log_dt"], ACT.Exp).then_inc(sem("s_dt"), 1)
        act.wait_ge(sem("s_dta"), 1)
        act.activation(dt_(8), dt_(0), ACT.Exp).then_inc(sem("s_trig"), 1)
        act.wait_ge(sem("s_turns"), 1)
        act.activation(d_tab[:, 6 * N_ST:8 * N_ST], d_tab[:, 4 * N_ST:6 * N_ST], ACT.Sin, scale=-TWO_PI).then_inc(sem("s_trig"), 1)

    def b_act_tables(act):
        act.wait_ge(sem("s_rates"), 1)
        act.activation(low_e, low_e, ACT.Exp).then_inc(sem("s_tables"), 1)
        act.wait_ge(sem("s_rates"), 2)
        act.activation(high_e, high_e, ACT.Exp).then_inc(sem("s_tables"), 1)
        act.wait_ge(sem("s_angles"), 1)
        act.activation(low_k, low_k, ACT.Sin, scale=-TWO_PI, bias=ssm["quarter_angle"]).then_inc(sem("s_tables"), 1)
        act.wait_ge(sem("s_angles"), 2)
        act.activation(high_k[:, 0:2048], high_k[:, 0:2048], ACT.Sin, scale=-TWO_PI, bias=0.25 * TWO_PI).then_inc(sem("s_tables"), 1)
        act.activation(high_k[:, 2048:], high_k[:, 2048:], ACT.Sin, scale=-TWO_PI).then_inc(sem("s_tables"), 1)

    def b_act_taps(act):
        act.wait_ge(sem("s_taps"), 1)
        tp = PS[:, 2048:4096].rearrange("p (d c q) -> p c d q", c=4, q=4)
        for q in range(4):
            act.activation(taps.rearrange("p (c d) -> p c d", c=4)[32 * q:32 * q + 32], tp[0:32, :, :, q], ACT.Copy)\
               .then_inc(sem("s_taps_copied"), 1)

    def b_pe_pre(pe):
        pe.wait_ge(sem("ssm_in"), 16)
        pe.wait_ge(sem("a_out_read"), 1)
        pe.matmul(bank(0)[:, 0:308], ssm["Wk"], ssm["ctx_T"], start=True, stop=True).then_inc(sem("x_kv"), 1)
        pe.matmul(bank(1)[:, 0:308], ssm["Wv"], ssm["ctx_T"], start=True, stop=True).then_inc(sem("x_kv"), 1)
        pe.wait_ge(sem("x_kv_in"), 2)
        pe.wait_ge(sem("film_w_in"), 1)
        for h in range(H_X):
            r = slice(DH_X * h, DH_X * h + DH_X)
            pe.matmul(bank(2 + h)[:, 0:308], ssm["Wq_T"][r, :], K_T[r, :], start=True, stop=True).then_inc(sem("x_scorer"), 1)
        pe.wait_ge(sem("x_kv_in"), 2)
        for b in range(B):
            pe.matmul(bank(b), V_T[:, S2 * b:S2 * b + 128], film_w, start=True, stop=True).then_inc(sem("x_vf"), 1)
        for b in range(B):
            pe.matmul(bank(6 + b)[0:REST, :], V_T[:, S2 * b + 128:S2 * b + S2], film_w, start=True, stop=True).then_inc(sem("x_vf"), 1)
        pe.wait_ge(sem("x_small_in"), 8)
        turn_pe(pe, tiled(xs), 4, (sem("stage_done"), 1), (sem("stage_half"), 1))

    def b_act_pre(act):
        act.wait_ge(sem("x_kv"), 1)
        act.activation(K_T, bank(0)[:, 0:308], ACT.Copy, scale=float(1.0 / np.sqrt(DH_X))).then_inc(sem("x_kv_in"), 1)
        act.wait_ge(sem("x_kv"), 2)
        act.activation(V_T, bank(1)[:, 0:308], ACT.Copy).then_inc(sem("x_kv_in"), 1)
        for h in range(H_X):
            act.wait_ge(sem("x_scorer"), h + 1)
            act.activation(score_w.rearrange("p (b h g) -> p b h g", b=B, h=H_X)[:, :, h, :],
                           bank(2 + h)[:, 0:308].rearrange("p (b g) -> p b g", b=B), ACT.Copy).then_inc(sem("x_small_in"), 1)
        for b in range(B):
            act.wait_ge(sem("x_vf"), b + 1)
            act.activation(vf0[:, 512 * b:512 * b + 512], bank(b), ACT.Copy).then_inc(sem("x_small_in"), 1)
        act.wait_ge(sem("x_rest_clear"), 1)
        for b in range(B):
            act.wait_ge(sem("x_vf"), b + 3)
            act.activation(vf1[0:REST, 512 * b:512 * b + 512], bank(6 + b)[0:REST, :], ACT.Copy).then_inc(sem("x_small_in"), 1)
        act.wait_ge(sem("turned"), 1)
        act.activation(xsT, bank(4, 2), ACT.Copy).then_inc(sem("turned_in"), 1)

    def b_pool_pre(pool, follow):
        pool.wait_ge(sem("small_in"), SMALL)
        pool.wait_ge(sem("ssm_in"), 16)
        pool.tensor_scalar(film_w, ssm["W_film"], mod_gate, None, ALU.mult).then_inc(sem("film_w_in"), 1)
        pool.wait_ge(sem("film_w_in"), 1)
        pool.memset(vf1[0:32, :], 0.0).then_inc(sem("x_rest_clear"), 1)
        pool.wait_ge(sem("x_rest_clear"), 1)
        follow(pool.tensor_scalar(film_line, film_line, mod_gate[32:33, :], None, ALU.mult))
        fl = film_line.rearrange("p (f s d) -> p f s d", f=2, s=2)
        follow(pool.tensor_scalar(fl[:, :, 0, :], fl[:, :, 0, :], 1.0, None, ALU.add))
        for b in range(B):
            follow(pool.tensor_copy(vf1[32:33, 512 * b:512 * b + 512], film_line))
        follow(pool.tensor_copy(mask_line[:, 0:308], ctx_bytes))
        follow(pool.tensor_scalar(mask_line[:, 0:308], mask_line[:, 0:308], 1.0, None, ALU.subtract))
        follow(pool.tensor_scalar(mask_line[:, 0:308], mask_line[:, 0:308], -NEG, None, ALU.mult))
        m2 = mask_line.rearrange("p (b h g) -> p b h g", b=2, h=2)
        follow(pool.tensor_copy(m2[:, 1, 1, :], mask_line[:, S2:2 * S2]))
        follow(pool.tensor_copy(m2[:, 1, 0, :], m2[:, 1, 1, :]))
        follow(pool.tensor_copy(m2[:, 0, 1, :], m2[:, 0, 0, :]))
        follow(pool.tensor_copy(text_mask, text_bytes))
        pool.tensor_scalar(text_mask, text_mask, 1.0 / H_X, None, ALU.mult).then_inc(sem("masks_in"), 1)
        pool.wait_ge(sem("masks_in"), 1)

    STEPS = NT * H_X

    def scores(i):
        t, h = divmod(i, H_X)
        return scored[t % 2][:, S2 * h:S2 * h + S2]

    def b_pe_attention(pe):
        pe.wait_ge(sem("turned_in"), 1)
        pe.wait_ge(sem("masks_in"), 1)
        pe.wait_ge(sem("ones_set"), 2)

        def score(t):
            if t >= 2:
                pe.wait_ge(sem("x_scores_in"), t - 1)
            b = t // (NT // B)
            for g in range(2):
                o = bank(2 * (t % 2) + g)[:, 0:2 * S2]
                pe.matmul(o, xsT[:, 128 * t:128 * t + 128], score_w[:, 4 * S2 * b + 2 * S2 * g:4 * S2 * b + 2 * S2 * g + 2 * S2],
                          start=True, stop=False)
                pe.matmul(o, ones[0:1, :], mask_line[:, 2 * S2 * b:2 * S2 * b + 2 * S2], start=False, stop=True)\
                  .then_inc(sem("x_scores"), 1)

        def gather(t):
            pe.wait_ge(sem("x_probs"), H_X * t + H_X)
            pe.wait_ge(sem("x_diag"), H_X * t + H_X)
            if t >= 2:
                pe.wait_ge(sem("x_attn_in"), 2 * (t - 1))
            o = bank(4 + t % 2)
            for h in range(H_X):
                i = H_X * t + h
                pe.matmul(o[:, 0:128], probs[i % 8][:, 0:128], diag[h], start=(h == 0), stop=(h == 3))
            for h in range(H_X):
                i = H_X * t + h
                ins = pe.matmul(o[0:REST, 128:256], probs[i % 8][:, 128:S2], diag[h], start=(h == 0), stop=(h == 3))
            ins.then_inc(sem("x_gathered"), 1)

        score(0)
        score(1)
        pe.wait_ge(sem("s_factors"), 1)
        for d in range(D):
            ins = pe.matmul(PS[0:LOW, 2048 + HIGH * d:2048 + HIGH * d + HIGH], low_k[:, LOW * d:LOW * d + LOW],
                            high_r[:, HIGH * d:HIGH * d + HIGH], start=True, stop=True)
        ins.then_inc(sem("s_taps"), 1)
        for t in range(NT):
            if t + 2 < NT:
                score(t + 2)
            if t == 0:
                pe.wait_ge(sem("s_taps_copied"), 4)
            gather(t)
            if t == 2:
                pe.wait_ge(sem("s_taps_in"), 1)
                pe.wait_ge(sem("dft_in"), 16)
                for part, mat in ((0, dft["dft_cos"]), (1, dft["dft_sin"])):
                    for j in range(4):
                        for c in range(4):
                            ins = pe.matmul(bank(6 + part)[:, 128 * j:128 * j + 128],
                                            mat[:, 512 * c + 128 * j:512 * c + 128 * j + 128],
                                            taps[:, 128 * c:128 * c + 128], start=(c == 0), stop=(c == 3))
                ins.then_inc(sem("s_taps_dft"), 1)

    def b_dve_attention(dve, follow):
        for t in range(NT):
            dve.wait_ge(sem("x_scores_in"), t + 1)
            for pair in range(2):
                j = 2 * t + pair
                two = (2 * j, 2 * j + 1)
                m8 = [best[:, TOP * i:TOP * i + TOP] for i in two]
                src = [scores(i) for i in two]
                base = 14 * j
                for r in range(TOP // 8):
                    for k in range(2):
                        if r:
                            dve.wait_ge(sem("x_best"), base + 4 * r + k - 1)
                        dve.max(m8[k][:, 8 * r:8 * r + 8], src[k]).then_inc(sem("x_best"), 1)
                    for k in range(2):
                        dve.wait_ge(sem("x_best"), base + 4 * r + k + 1)
                        if r == 0 and k == 0 and j >= 2:
                            dve.wait_ge(sem("x_exp"), 6 * (j - 1))
                        rest = left[two[k] % 4]
                        ins = dve.match_replace(rest, m8[k][:, 8 * r:8 * r + 8], src[k], GONE)
                        ins.then_inc(sem("x_selected" if r == 3 else "x_best"), 1)
                        src[k] = rest
                    if r == 0:
                        b3 = best.rearrange("p (i m) -> p i m", m=TOP)
                        dve.tensor_scalar(minus_max[:, 2 * j:2 * j + 2], b3[:, 2 * j:2 * j + 2, 0], -1.0, None, ALU.mult)\
                           .then_inc(sem("x_minus_max"), 1)
                if pair == 0 and t >= 1:
                    shares(dve, follow, t - 1)
            if t == 0:
                b_dve_skip(dve, follow)
            if t == 5:
                b_dve_spectrum(dve, follow)
        shares(dve, follow, NT - 1)

    def shares(dve, follow, t):
        dve.wait_ge(sem("x_exp"), 3 * H_X * (t + 1))
        a = share[:, H_X * t:H_X * t + H_X]
        follow(dve.reciprocal(a, total[:, H_X * t:H_X * t + H_X]))
        dve.tensor_scalar(a, a, text_mask[:, t:t + 1], None, ALU.mult).then_inc(sem("x_share"), 1)

    def b_act_attention(act):
        def scores_in(t):
            if t >= 2:
                act.wait_ge(sem("x_selected"), H_X * (t - 1))
                act.wait_ge(sem("x_exp"), 3 * H_X * (t - 1))
            act.wait_ge(sem("x_scores"), 2 * t + 2)
            act.activation(scored[t % 2].rearrange("p (g k) -> p g k", g=2),
                           bank(2 * (t % 2), 2).rearrange("p (g k) -> p g k", g=2)[:, :, 0:2 * S2], ACT.Copy)\
               .then_inc(sem("x_scores_in"), 1)

        def exponentials(i):
            act.wait_ge(sem("x_minus_max"), i // 2 + 1)
            if i >= 4:
                act.wait_ge(sem("x_probs"), i - 3)
            bias = minus_max[:, i:i + 1]
            act.activation(all_exp[i % 4], scores(i), ACT.Exp, bias=bias).then_inc(sem("x_exp"), 1)
            act.wait_ge(sem("x_selected"), i + 1)
            act.activation(rest_exp[i % 4], left[i % 4], ACT.Exp, bias=bias).then_inc(sem("x_exp"), 1)
            at = slice(TOP * i, TOP * i + TOP)
            act.activation(best_exp[:, at], best[:, at], ACT.Exp, bias=bias, accum_out=total[:, i:i + 1]).then_inc(sem("x_exp"), 1)

        def diagonals(t):
            act.wait_ge(sem("x_share"), t + 1)
            if t >= 1:
                act.wait_ge(sem("x_gathered"), t)
            for h in range(H_X):
                i = H_X * t + h
                act.activation(diag[h], ident, ACT.Copy, scale=share[:, i:i + 1]).then_inc(sem("x_diag"), 1)

        act.wait_ge(sem("s_stack_in"), 1)
        scores_in(0)
        for t in range(NT):
            exponentials(H_X * t)
            exponentials(H_X * t + 1)
            if t == 0:
                b_act_taps(act)
            if t + 1 < NT:
                scores_in(t + 1)
            if t >= 1:
                diagonals(t - 1)
            exponentials(H_X * t + 2)
            exponentials(H_X * t + 3)
            if t >= 1:
                attn_in(act, t - 1)
        diagonals(NT - 1)
        attn_in(act, NT - 1)

    def attn_in(act, t):
        act.wait_ge(sem("x_gathered"), t + 1)
        if t == 0:
            act.wait_ge(sem("x_attn_clear"), 1)
        act.activation(attn0[:, 128 * t:128 * t + 128], bank(4 + t % 2)[:, 0:128], ACT.Copy).then_inc(sem("x_attn_in"), 1)
        act.activation(attn1[0:REST, 128 * t:128 * t + 128], bank(4 + t % 2)[0:REST, 128:256], ACT.Copy).then_inc(sem("x_attn_in"), 1)

    def b_pool_attention(pool, follow):
        pool.wait_ge(sem("s_taps"), 1)
        follow(pool.memset(attn1[0:32, :], 0.0))
        pool.memset(attn1[32:33, :], 1.0).then_inc(sem("x_attn_clear"), 1)
        pool.wait_ge(sem("x_attn_clear"), 1)
        for i in range(STEPS):
            pool.wait_ge(sem("x_exp"), 3 * i + 2)
            if i >= 8:
                pool.wait_ge(sem("x_gathered"), i // 4 - 1)
            pool.tensor_tensor(probs[i % 8], all_exp[i % 4], rest_exp[i % 4], ALU.subtract).then_inc(sem("x_probs"), 1)

    Bc = Space(after_attn, END)
    W.at = W.end - 8792
    spec = Space(after_small, after_small + 4096)
    Y_re, Y_im, prod_a, prod_b = spec(1024), spec(1024), spec(1024), spec(1024)
    u = Bc(T)
    inner = Bc(T)
    inner_n = u
    hT = inner
    gelu = film

    def b_dve_norm(dve, follow):
        dve.wait_ge(sem("stage_done"), 1)
        norm(dve, follow, tiled(xs), tiled(u_n)).then_inc(sem("u_normed"), 1)

    def b_pool_norm(pool, follow):
        every = lambda a: a[:, None, :].to_broadcast([P, NT, 128])
        pool.wait_ge(sem("u_normed"), 1)
        follow(pool.tensor_tensor(tiled(u_n), tiled(u_n), every(rows["g_in"]), ALU.mult))
        pool.tensor_tensor(tiled(u_n), tiled(u_n), every(rows["b_in"]), ALU.add).then_inc(sem("u_affine"), 1)

    def b_pe_ssm(pe):
        for t in range(NT):
            pe.wait_ge(sem("x_attn_in"), 2 * NT if t == NT - 1 else 2 * t + 2)
            if t == 0:
                pe.wait_ge(sem("x_selected"), STEPS)
                pe.wait_ge(sem("x_exp"), 3 * STEPS)
            if t >= 2:
                pe.wait_ge(sem("x_film_in"), t - 1)
            b = t // (NT // B)
            pe.matmul(bank(t % 2), attn0[:, 128 * t:128 * t + 128], vf0[:, 512 * b:512 * b + 512], start=True, stop=False)
            pe.matmul(bank(t % 2), attn1[0:33, 128 * t:128 * t + 128], vf1[0:33, 512 * b:512 * b + 512], start=False,
                      stop=True).then_inc(sem("x_film"), 1)
        pe.wait_ge(sem("s_u"), 1)
        pe.wait_ge(sem("x_film_in"), NT)
        uv = u.rearrange("p (b c d) -> p c b d", b=B, c=4)
        for j in range(4):
            for part, mat in ((0, dft["dft_cos"]), (1, dft["dft_sin"])):
                for c in range(4):
                    ins = pe.matmul(bank(4 * part + j)[:, 0:256], mat[:, 512 * c + 128 * j:512 * c + 128 * j + 128],
                                    uv[:, c], start=(c == 0), stop=(c == 3))
            ins.then_inc(sem("s_spectra"), 1)
        pe.wait_ge(sem("s_product"), 5)
        for c in range(4):
            o = bank(c)[:, 0:256]
            for j in range(4):
                pe.matmul(o, dft["dft_cos"][:, 512 * j + 128 * c:512 * j + 128 * c + 128], Y_re[:, 256 * j:256 * j + 256],
                          start=(j == 0), stop=False)
            for j in range(4):
                sin = dft["inv_sin0"][:, 128 * c:128 * c + 128] if j == 0 else \
                    dft["dft_sin"][:, 512 * j + 128 * c:512 * j + 128 * c + 128]
                ins = pe.matmul(o, sin, Y_im[:, 256 * j:256 * j + 256], start=False, stop=(j == 3))
            ins.then_inc(sem("s_conv"), 1)
        turn_pe(pe, tiled(inner_n), 4, (sem("f_normed"), 1), (sem("f_half"), 1))
        pe.wait_ge(sem("turned_in"), 2)
        pe.wait_ge(sem("ffn_in"), 16)
        for k in range(4):
            if k >= 2:
                pe.wait_ge(sem("f_gelu"), k - 1)
            for n in range(2):
                ins = pe.matmul(bank(2 * (k % 2) + n), ffn["W1"][:, 128 * k:128 * k + 128], hT[:, 512 * n:512 * n + 512],
                                start=True, stop=True)
            ins.then_inc(sem("f_hidden"), 1)
        pe.wait_ge(sem("f_gelu"), 4)
        for t in range(NT):
            pe.matmul(PS[:, 3072 + 128 * t:3072 + 128 * t + 128], ones[0:1, :], lines["ffn_b2"][0:1, :], start=True, stop=False)
            for k in range(4):
                ins = pe.matmul(PS[:, 3072 + 128 * t:3072 + 128 * t + 128], gelu[:, T * k + 128 * t:T * k + 128 * t + 128],
                                ffn["W2"][:, 128 * k:128 * k + 128], start=False, stop=(k == 3))
        ins.then_inc(sem("f_out"), 1)

    def b_act_ssm(act):
        for t in range(NT):
            act.wait_ge(sem("x_film"), t + 1)
            act.activation(film[:, 512 * t:512 * t + 512], bank(t % 2), ACT.Copy).then_inc(sem("x_film_in"), 1)
        act.wait_ge(sem("turned"), 2)
        act.wait_ge(sem("ffn_in"), 16)
        act.wait_ge(sem("f_inner_kept"), 1)
        act.activation(hT, bank(4, 2), ACT.Identity, scale=ffn["ffn_g"], bias=ffn["ffn_b"]).then_inc(sem("turned_in"), 1)
        for k in range(4):
            act.wait_ge(sem("f_hidden"), k + 1)
            act.activation(gelu[:, T * k:T * k + T], bank(2 * (k % 2), 2), ACT.Gelu, bias=ffn["ffn_b1"][:, k:k + 1])\
               .then_inc(sem("f_gelu"), 1)

    def b_dve_ssm(dve, follow):
        fv = film.rearrange("p (t k d) -> p t k d", t=NT, k=4)
        dve.wait_ge(sem("x_film_in"), NT)
        dve.wait_ge(sem("u_affine"), 1)
        follow(dve.tensor_tensor(tiled(u), tiled(u_n), fv[:, :, 0], ALU.mult))
        dve.tensor_tensor(tiled(u), tiled(u), fv[:, :, 1], ALU.add).then_inc(sem("s_u"), 1)
        two = lambda a, j: a[:, None, 128 * j:128 * j + 128].to_broadcast([P, 2, 128])
        bd = lambda a: a.rearrange("p (b d) -> p b d", b=2)
        for j in range(4):
            dve.wait_ge(sem("s_spectra"), j + 1)
            re, im = bd(bank(j)[:, 0:256]), bd(bank(4 + j)[:, 0:256])
            at = slice(256 * j, 256 * j + 256)
            dve.tensor_tensor(bd(Y_re[:, at]), re, two(taps_re, j), ALU.mult)
            dve.tensor_tensor(bd(prod_a[:, at]), im, two(taps_im2, j), ALU.mult)
            dve.tensor_tensor(bd(Y_im[:, at]), im, two(taps_re2, j), ALU.mult)
            follow(dve.tensor_tensor(bd(prod_b[:, at]), re, two(taps_im2, j), ALU.mult))
            dve.tensor_tensor(Y_re[:, at], Y_re[:, at], prod_a[:, at], ALU.subtract)
            dve.tensor_tensor(Y_im[:, at], Y_im[:, at], prod_b[:, at], ALU.add).then_inc(sem("s_product"), 1)
        dve.memset(dft["dft_sin"].rearrange("p (c l) -> p c l", c=4)[:, 1:4, 0:1], 0.0).then_inc(sem("s_product"), 1)
        dve.wait_ge(sem("s_conv"), 4)
        y = PS[:, 0:2048].rearrange("p (c b d) -> p c b d", c=4, b=4)
        i4 = inner.rearrange("p (b c d) -> p b c d", b=B, c=4)
        f4 = film.rearrange("p (b c k d) -> p b c k d", b=B, c=4, k=4)
        for b in range(B):
            ins = dve.tensor_tensor(i4[:, b], y[:, :, b], f4[:, b, :, 2], ALU.mult)
        follow(ins)
        follow(dve.tensor_tensor(tiled(inner), tiled(inner), fv[:, :, 3], ALU.add))
        follow(dve.tensor_tensor(inner, inner, xs, ALU.add))
        norm(dve, follow, tiled(inner), tiled(inner_n), first_half="f_half").then_inc(sem("f_normed"), 1)
        dve.tensor_copy(xsum, inner).then_inc(sem("f_inner_kept"), 1)
        every = lambda a: a[:, None, :].to_broadcast([P, NT, 128])
        follow(dve.tensor_tensor(tiled(u_n), tiled(xs), every(rows["b_out"]), ALU.add))
        dve.wait_ge(sem("f_out"), 1)
        follow(dve.tensor_tensor(xsum, xsum, bank(6, 2), ALU.add))
        follow(norm(dve, follow, tiled(xsum), tiled(xn)))
        follow(dve.tensor_tensor(tiled(xn), tiled(xn), every(rows["g_out"]), ALU.mult))
        follow(dve.tensor_tensor(xsum, xn, u_n, ALU.add))
        norm(dve, follow, tiled(xsum), tiled(xs), first_half="stage_half").then_inc(sem("stage_done"), 1)

    W3 = Space(after_small, END)
    moe = views(PACK_MOE, Space(END - 8192, END)(8192))
    mha_at = W3.at
    mha = views(PACK_MHA, W3(width(PACK_MHA)))
    C = Space(W3.at, END - 8192)
    C0 = Space(stream.at, stream.at + 8792)
    merged, merged_bias = C0(E0 * 128), C0(128)
    d_x, d_k, d_v, v_1 = C0(512), C0(512), C0(512), C0(512)
    q_dk, attended = C(T), C(T)
    y1, y1T, y1_bias = C(T), C(T), C(T)
    g_logit, g_cand, g_hot, g_pos, g_coef = (C(NT * E0) for _ in range(5))
    g_max, g_sum = C(NT), C(NT)
    coef_T = C(T)
    moe_sum = C(T)
    by_tile = C(NT * E0)

    def c_sp(sp):
        sp.wait_ge(sem("s_product"), 5)
        sp.wait_ge(sem("f_normed"), 1)
        sp.dma_start(SB[:, mha_at:mha_at + width(PACK_MHA)], dram["mha"]).then_inc(sem("mha_in"), 16)
        sp.wait_ge(sem("stage_done"), 2)
        sp.dma_start(SB[:, END - 8192:END], dram["moe"]).then_inc(sem("moe_in"), 16)

    def c_pe(pe):
        turn_pe(pe, tiled(xs), 0, (sem("stage_done"), 2), (sem("stage_half"), 2))
        pe.wait_ge(sem("mha_in"), 16)
        pe.wait_ge(sem("turned_in"), 3)
        pe.wait_ge(sem("c_dx"), 1)
        for n in range(2):
            ins = pe.matmul(bank(2 + n), mha["qkv_T"][:, 0:128], xsT[:, 512 * n:512 * n + 512], start=True, stop=True)
        ins.then_inc(sem("c_qkv"), 1)
        pe.matmul(bank(4), mha["qkv_T"][:, 128:256], d_x, start=True, stop=True).then_inc(sem("c_qkv"), 1)
        pe.matmul(bank(5), mha["qkv_T"][:, 256:384], d_x, start=True, stop=True).then_inc(sem("c_qkv"), 1)
        pe.matmul(bank(6), mha["qkv_T"][:, 256:384], xsT[:, 512:], start=True, stop=True).then_inc(sem("c_qkv"), 1)
        pe.wait_ge(sem("c_qdk"), 1)
        for n in range(2):
            ins = pe.matmul(bank(n), mha["head_sum"], q_dk[:, 512 * n:512 * n + 512], start=True, stop=True)
        ins.then_inc(sem("c_scores"), 1)
        pe.wait_ge(sem("c_attended"), 1)
        for t in range(NT):
            o = PS[:, 3072 + 128 * t:3072 + 128 * t + 128]
            if t == 0:
                pe.wait_ge(sem("c_v_in"), 4)
            pe.matmul(o, ones[0:1, :], lines["m_ob"][0:1, :], start=True, stop=False)
            ins = pe.matmul(o, attended[:, 128 * t:128 * t + 128], mha["ow_T"], start=False, stop=True)
        ins.then_inc(sem("c_out"), 1)
        pe.wait_ge(sem("moe_in"), 16)
        for e in range(E0):
            o = bank(2 + e // 4)[:, 128 * (e % 4):128 * (e % 4) + 128]
            for k in range(4):
                i = 4 * e + k
                ins = pe.matmul(o, moe["m_w1T"][:, 128 * i:128 * i + 128], moe["m_w2"][:, 128 * i:128 * i + 128],
                                start=(k == 0), stop=(k == 3))
        ins.then_inc(sem("c_merged"), 1)
        for e in range(E0):
            for k in range(4):
                ins = pe.matmul(bank(4)[0:E0, 0:128], mha["m_b1"][:, 64 * k + 8 * e:64 * k + 8 * e + 8],
                                moe["m_w2"][:, 128 * (4 * e + k):128 * (4 * e + k) + 128], start=(e + k == 0), stop=(e == 7 and k == 3))
        ins.then_inc(sem("c_merged"), 1)
        turn_pe(pe, tiled(xn), 0, (sem("c_normed"), 1), (sem("c_half"), 1))
        pe.wait_ge(sem("turned_in"), 4)
        for t in range(NT):
            ins = pe.matmul(bank(5)[:, E0 * t:E0 * t + E0], y1T[:, 128 * t:128 * t + 128], mha["m_wg"], start=True, stop=True)
        ins.then_inc(sem("g_logits"), 1)
        pe.wait_ge(sem("g_hot"), 1)
        pe.matmul(bank(6)[:, 0:NT * E0], mha["earlier"], g_hot, start=True, stop=False)
        pe.matmul(bank(6)[:, 0:NT * E0], ones, by_tile, start=False, stop=True).then_inc(sem("g_counted"), 1)
        pe.wait_ge(sem("g_coef"), 1)
        for t in range(NT):
            ins = pe.transpose(PS[0:E0, 128 * t:128 * t + 128], g_coef[:, E0 * t:E0 * t + E0], ident)
        ins.then_inc(sem("g_coef_turned"), 1)
        pe.wait_ge(sem("g_coef_in"), 1)
        for t in range(NT):
            ins = pe.matmul(PS[:, 3072 + 128 * t:3072 + 128 * t + 128], coef_T[0:E0, 128 * t:128 * t + 128],
                            merged_bias[0:E0, :], start=True, stop=True)
        ins.then_inc(sem("c_bias"), 1)
        pe.wait_ge(sem("c_merged_in"), 2)
        for t in range(NT):
            if t >= 3:
                pe.wait_ge(sem("c_combined"), t - 2)
            for n in range(2):
                ins = pe.matmul(bank(2 * (t % 3) + n), y1T[:, 128 * t:128 * t + 128], merged[:, 512 * n:512 * n + 512],
                                start=True, stop=True)
            ins.then_inc(sem("c_expert"), 1)

    def c_act(act):
        act.wait_ge(sem("turned"), 3)
        act.activation(xsT, bank(0, 2), ACT.Copy).then_inc(sem("turned_in"), 1)
        act.wait_ge(sem("c_qkv"), 2)
        act.activation(d_k, bank(4), ACT.Copy).then_inc(sem("c_v_in"), 1)
        act.wait_ge(sem("c_qkv"), 3)
        act.activation(d_v, bank(5), ACT.Copy).then_inc(sem("c_v_in"), 1)
        act.wait_ge(sem("c_qkv"), 4)
        act.activation(v_1, bank(6), ACT.Identity, bias=mha["b_v"]).then_inc(sem("c_v_in"), 1)
        act.wait_ge(sem("c_scores"), 1)
        act.activation(attended, bank(0, 2), ACT.Sigmoid, scale=float(1.0 / np.sqrt(DH_X))).then_inc(sem("c_v_in"), 1)
        act.wait_ge(sem("c_merged"), 1)
        act.activation(merged, bank(2, 2), ACT.Copy).then_inc(sem("c_merged_in"), 1)
        act.wait_ge(sem("turned"), 4)
        act.activation(y1T, bank(0, 2), ACT.Identity, scale=mha["ln1_g"], bias=mha["ln1_b"]).then_inc(sem("turned_in"), 1)
        act.wait_ge(sem("g_hot"), 1)
        act.activation(g_cand, g_logit, ACT.Exp).then_inc(sem("g_exp"), 1)
        act.wait_ge(sem("g_coef_turned"), 1)
        act.activation(coef_T[0:E0, :], PS[0:E0, 0:1024], ACT.Copy).then_inc(sem("g_coef_in"), 1)

    def c_dve(dve, follow):
        every = lambda a: a[:, None, :].to_broadcast([P, NT, 128])
        dve.wait_ge(sem("turned_in"), 3)
        dve.tensor_tensor(d_x, xsT[:, 0:512], xsT[:, 512:], ALU.subtract).then_inc(sem("c_dx"), 1)
        dve.wait_ge(sem("c_qkv"), 1)
        dve.wait_ge(sem("c_v_in"), 1)
        for n in range(2):
            ins = dve.scalar_tensor_tensor(q_dk[:, 512 * n:512 * n + 512], bank(2 + n), mha["b_q"], d_k, ALU.add, ALU.mult)
        ins.then_inc(sem("c_qdk"), 1)
        dve.wait_ge(sem("c_v_in"), 4)
        two = lambda a: a[:, None, :].to_broadcast([P, 2, 512])
        a2 = attended.rearrange("p (l n) -> p l n", l=2)
        follow(dve.tensor_tensor(a2, a2, two(d_v), ALU.mult))
        dve.tensor_tensor(a2, a2, two(v_1), ALU.add).then_inc(sem("c_attended"), 1)
        dve.wait_ge(sem("c_out"), 1)
        follow(dve.tensor_tensor(xsum, xs, bank(6, 2), ALU.add))
        norm(dve, follow, tiled(xsum), tiled(xn), first_half="c_half").then_inc(sem("c_normed"), 1)
        dve.wait_ge(sem("c_normed"), 1)
        follow(dve.tensor_tensor(tiled(y1), tiled(xn), every(rows["n1_g"]), ALU.mult))
        follow(dve.tensor_tensor(tiled(y1), tiled(y1), every(rows["n1_b"]), ALU.add))
        follow(dve.tensor_tensor(tiled(y1_bias), tiled(xs), every(rows["n2_b"]), ALU.add))
        dve.wait_ge(sem("c_merged"), 2)
        dve.tensor_tensor(merged_bias[0:E0, :], bank(4)[0:E0, 0:128], mha["m_b2"][0:E0, :], ALU.add).then_inc(sem("c_merged_in"), 1)
        dve.wait_ge(sem("lat_in"), 16)
        dve.wait_ge(sem("g_logits"), 1)
        te = lambda a: a.rearrange("p (t e) -> p t e", t=NT)
        eight = lambda a: a[:, :, None].to_broadcast([P, NT, E0])
        follow(dve.tensor_copy(g_logit, bank(5)[:, 0:NT * E0]))
        follow(dve.tensor_reduce(g_max, te(g_logit), AX_X, ALU.max))
        follow(dve.tensor_tensor(te(g_logit), te(g_logit), eight(g_max), ALU.subtract))
        follow(dve.tensor_scalar(g_cand, g_logit, 0.0, None, ALU.is_equal))
        follow(dve.tensor_tensor(te(g_cand), te(g_cand), lat["expert_rank"][:, None, :].to_broadcast([P, NT, E0]), ALU.mult))
        follow(dve.tensor_reduce(g_max, te(g_cand), AX_X, ALU.max))
        follow(dve.tensor_tensor(te(g_hot), te(g_cand), eight(g_max), ALU.is_equal))
        follow(dve.memset(by_tile[:, 0:E0], 0.0))
        for t in range(1, NT):
            ins = dve.tensor_tensor(te(by_tile)[:, t], te(by_tile)[:, t - 1], te(g_hot)[:, t - 1], ALU.add)
            if t < NT - 1:
                follow(ins)
        ins.then_inc(sem("g_hot"), 1)
        dve.wait_ge(sem("g_hot"), 1)
        dve.wait_ge(sem("g_exp"), 1)
        follow(dve.tensor_reduce(g_sum, te(g_cand), AX_X, ALU.add))
        follow(dve.reciprocal(g_sum, g_sum))
        dve.wait_ge(sem("g_counted"), 1)
        follow(dve.scalar_tensor_tensor(g_coef, bank(6)[:, 0:NT * E0], float(CAP), g_hot, ALU.is_lt, ALU.mult))
        dve.tensor_tensor(te(g_coef), te(g_coef), eight(g_sum), ALU.mult).then_inc(sem("g_coef"), 1)
        dve.wait_ge(sem("c_bias"), 1)
        follow(dve.tensor_tensor(moe_sum, y1, bank(6, 2), ALU.add))
        for t in range(NT):
            dve.wait_ge(sem("c_expert"), t + 1)
            dve.wait_ge(sem("g_coef"), 1)
            for e in range(E0):
                o = tiled(moe_sum)[:, t]
                ins = dve.scalar_tensor_tensor(o, PS[:, 1024 * (t % 3) + 128 * e:1024 * (t % 3) + 128 * e + 128],
                                               g_coef[:, E0 * t + e:E0 * t + e + 1], o, ALU.mult, ALU.add)
                if e < E0 - 1:
                    follow(ins)
            ins.then_inc(sem("c_combined"), 1)
        dve.wait_ge(sem("c_combined"), NT)
        follow(norm(dve, follow, tiled(moe_sum), tiled(xn)))
        follow(dve.tensor_tensor(tiled(xn), tiled(xn), every(rows["n2_g"]), ALU.mult))
        follow(dve.tensor_tensor(xsum, xn, y1_bias, ALU.add))
        norm(dve, follow, tiled(xsum), tiled(xs), first_half="stage_half").then_inc(sem("stage_done"), 1)

    D1 = Space(stream.at, stream.at + 8792)
    value = D1(8192)
    D2 = Space(W2.end, END)
    headed = D2(8192)
    expd = [D2(4096) for _ in range(2)]
    q_ring, k_ring = [D2(1024) for _ in range(3)], [D2(1024) for _ in range(3)]
    qb_ring, kb_ring = [D2(512, BF16) for _ in range(3)], [D2(512, BF16) for _ in range(3)]
    half_sum, key_sum, unit = D2(1024), D2(1024), D2(512)
    shift = [D2(8) for _ in range(2)]
    NP_ = B * PAIRS

    def two_heads(a):
        return a.rearrange("p (h n) -> p h n", h=2)

    def d_pe(pe):
        turn_pe(pe, tiled(xs), 0, (sem("stage_done"), 3), (sem("stage_half"), 3))
        pe.wait_ge(sem("turned_in"), 5)
        pe.wait_ge(sem("att_in"), 16)

        def project(i, which):
            b, pair = divmod(i, PAIRS)
            if which:
                pe.wait_ge(sem("d_qk_in"), 4 * i + 2)
            elif i >= 1:
                pe.wait_ge(sem("d_qk_in"), 4 * i)
                if i >= 4:
                    pe.wait_ge(sem("d_unit"), i - 3)
            w = att["w_k"] if which else att["w_q"]
            pe.matmul(bank(7), w[:, 128 * pair:128 * pair + 128], xsT[:, 512 * b:512 * b + 512], start=True, stop=True)\
              .then_inc(sem("d_qk"), 1)

        def maxima(i, qt):
            n = 4 * i + qt
            if qt == 0:
                pe.wait_ge(sem("d_bf16"), 2 * i + 2)
                if i >= 1:
                    pe.wait_ge(sem("d_shift_in"), i)
            if n >= 1:
                pe.wait_ge(sem("d_max"), n)
            for h in range(2):
                ins = pe.matmul(bank(4 + h), two_heads(qb_ring[i % 3])[0:DK, h, 128 * qt:128 * qt + 128],
                                two_heads(kb_ring[i % 3])[0:DK, h, :], start=True, stop=True)
            ins.then_inc(sem("d_rough"), 1)

        def shifts(i):
            pe.wait_ge(sem("d_max"), 4 * i + 4)
            for qt in range(4):
                for h in range(2):
                    c = 2 * qt + h
                    ins = pe.matmul(bank(4 + h)[0:1, 128 * qt:128 * qt + 128], shift[i % 2][:, c:c + 1], ident,
                                    start=True, stop=True)
            ins.then_inc(sem("d_shifts"), 1)

        def score(i, u):
            h, half = divmod(u, 2)
            n = 4 * i + u
            if u == 0:
                pe.wait_ge(sem("d_shift_in"), i + 1)
            if n >= 2:
                pe.wait_ge(sem("d_exp"), n - 1)
            for k in range(2):
                kt = 2 * half + k
                ins = pe.matmul(bank(2 * (n % 2) + k), two_heads(k_ring[i % 3])[0:DK + 1, h, 128 * kt:128 * kt + 128],
                                two_heads(q_ring[i % 3])[0:DK + 1, h, :], start=True, stop=True)
            ins.then_inc(sem("d_scores"), 1)

        def weigh(i, kt):
            b, pair = divmod(i, PAIRS)
            if kt == 0:
                pe.wait_ge(sem("d_exp"), 4 * i + 4)
                if i >= 1:
                    pe.wait_ge(sem("d_headed"), i)
            for h in range(2):
                v = value[:, 1024 * (4 * b + kt) + 128 * pair + DK * h:1024 * (4 * b + kt) + 128 * pair + DK * h + DK]
                ins = pe.matmul(bank(6)[DK * h:DK * h + DK, :], v, expd[i % 2][:, 2048 * h + 512 * kt:2048 * h + 512 * kt + 512],
                                start=(kt == 0), stop=(kt == 3))
            if kt == 3:
                ins.then_inc(sem("d_weighed"), 1)

        def sums(i):
            pe.wait_ge(sem("d_key_sum"), i + 1)
            if i + 3 < NP_:
                pe.wait_ge(sem("d_qk_in"), 4 * (i + 4))
            else:
                pe.wait_ge(sem("d_unit"), i)
            for h in range(2):
                ins = pe.matmul(bank(7)[DK * h:DK * h + DK, :], ones[:, 0:DK], two_heads(key_sum)[:, h, :], start=True, stop=True)
            ins.then_inc(sem("d_sums"), 1)

        for t in range(NT):
            if t in (0, 1, 2):
                project(t // 2, t % 2)
            if t >= 2:
                pe.wait_ge(sem(("d_v_even", "d_v_odd")[t % 2]), t // 2)
            for n in range(2):
                ins = pe.matmul(bank(2 * (t % 2) + n), xsT[:, 128 * t:128 * t + 128], att["w_v"][:, 512 * n:512 * n + 512],
                                start=True, stop=True)
            ins.then_inc(sem("d_v"), 1)
            if t == 3:
                project(1, 1)
            if 2 <= t < 6:
                maxima(0, t - 2)
        shifts(0)
        pe.wait_ge(sem("d_v_even"), NT // 2)
        pe.wait_ge(sem("d_v_odd"), NT // 2)
        pe.wait_ge(sem("d_ones"), 3)
        for i in range(NP_ + 1):
            now, ahead, before = i < NP_, i + 1 < NP_, i >= 1
            for u in range(4):
                if ahead and u == 3:
                    shifts(i + 1)
                if now:
                    score(i, u)
                if ahead and u in (0, 2):
                    maxima(i + 1, (0, None, 3)[u])
                if before:
                    weigh(i - 1, u)
                if ahead and u == 1:
                    maxima(i + 1, 2)
                if i + 2 < NP_ and u < 2:
                    project(i + 2, u)
                if ahead and u == 0:
                    maxima(i + 1, 1)
                if before and u == 2:
                    sums(i - 1)
        for t in range(NT):
            b, c = divmod(t, 4)
            if t == 0:
                pe.wait_ge(sem("d_headed"), NP_)
            for pair in range(PAIRS):
                ins = pe.matmul(PS[:, 128 * t:128 * t + 128], headed[:, 512 * (PAIRS * b + pair) + 128 * c:512 * (PAIRS * b + pair) + 128 * c + 128],
                                att["w_o"][:, 128 * pair:128 * pair + 128], start=(pair == 0), stop=(pair == PAIRS - 1))
        ins.then_inc(sem("d_out"), 1)

    def d_act(act):
        act.wait_ge(sem("turned"), 5)
        act.activation(xsT, bank(0, 2), ACT.Copy).then_inc(sem("turned_in"), 1)

        def rows_in(i, which):
            ring, low, s = (k_ring, kb_ring, 1.0) if which else (q_ring, qb_ring, DK ** -0.5)
            if i >= 3:
                act.wait_ge(sem("d_scores"), 4 * (i - 2))
            act.wait_ge(sem("d_qk"), 2 * i + which + 1)
            for h in range(2):
                act.activation(two_heads(ring[i % 3])[0:DK, h, :], bank(7)[DK * h:DK * h + DK, :], ACT.Copy, scale=s)\
                   .then_inc(sem("d_qk_in"), 1)
            act.wait_ge(sem("d_qk_in"), 4 * i + 2 * which + 2)
            act.activation(low[i % 3][0:DK, :], ring[i % 3][0:DK, :], ACT.Copy).then_inc(sem("d_bf16"), 1)

        def shift_in(i):
            act.wait_ge(sem("d_shifts"), i + 1)
            act.activation(q_ring[i % 3][DK:DK + 1, :], bank(4, 2)[0:1, :], ACT.Copy).then_inc(sem("d_shift_in"), 1)

        def exp(i, u):
            if i >= 2 and u == 0:
                act.wait_ge(sem("d_weighed"), i - 1)
                act.wait_ge(sem("d_key_sum"), i - 1)
            act.wait_ge(sem("d_scores"), 4 * i + u + 1)
            act.activation(expd[i % 2][:, 1024 * u:1024 * u + 1024], bank(2 * (u % 2), 2), ACT.Exp).then_inc(sem("d_exp"), 1)

        for k in range(4):
            rows_in(k // 2, k % 2)
            act.wait_ge(sem("d_v"), 2 * k + 1)
            act.activation(value[:, 2048 * k:2048 * k + 1024], bank(0, 2), ACT.Copy).then_inc(sem("d_v_even"), 1)
        shift_in(0)
        for i in range(NP_):
            for u in range(4):
                if u == 3 and i + 1 < NP_:
                    shift_in(i + 1)
                exp(i, u)
                if u < 2 and i + 2 < NP_:
                    rows_in(i + 2, u)

    def d_pool(pool):
        pool.wait_ge(sem("stage_done"), 3)
        for r in k_ring:
            pool.memset(r[DK:DK + 1, :], 1.0).then_inc(sem("d_ones"), 1)

    def d_dve(dve, follow):
        def v_in(t):
            dve.wait_ge(sem("d_v"), t + 1)
            dve.tensor_copy(value[:, 1024 * t:1024 * t + 1024], bank(2, 2)).then_inc(sem("d_v_odd"), 1)

        def maximum(i, qt):
            n = 4 * i + qt
            dve.wait_ge(sem("d_rough"), n + 1)
            if qt == 0 and i >= 2:
                dve.wait_ge(sem("d_shifts"), i - 1)
            dve.tensor_reduce(shift[i % 2][:, 2 * qt:2 * qt + 2], two_heads(bank(4, 2)), AX_X, ALU.max, negate=True)\
               .then_inc(sem("d_max"), 1)

        def key_sums(i, h):
            dve.wait_ge(sem("d_exp"), 4 * i + 2 * h + 2)
            if h == 0 and i >= 1:
                dve.wait_ge(sem("d_sums"), i)
            e = expd[i % 2][:, 2048 * h:2048 * h + 2048]
            follow(dve.tensor_tensor(half_sum, e[:, 0:1024], e[:, 1024:], ALU.add))
            ins = dve.tensor_tensor(two_heads(key_sum)[:, h, :], half_sum[:, 0:512], half_sum[:, 512:], ALU.add)
            if h:
                ins.then_inc(sem("d_key_sum"), 1)
            else:
                follow(ins)

        v_in(1)
        maximum(0, 0)
        v_in(3)
        maximum(0, 1)
        maximum(0, 2)
        v_in(5)
        maximum(0, 3)
        v_in(7)
        for i in range(NP_ + 1):
            ahead, before = i + 1 < NP_, i >= 1
            if ahead:
                maximum(i + 1, 0)
                maximum(i + 1, 1)
            if before:
                key_sums(i - 1, 0)
            if ahead:
                maximum(i + 1, 2)
            if before:
                key_sums(i - 1, 1)
            if ahead:
                maximum(i + 1, 3)
            if before:
                dve.wait_ge(sem("d_sums"), i)
                dve.reciprocal(unit, bank(7)).then_inc(sem("d_unit"), 1)
            if before:
                dve.wait_ge(sem("d_weighed"), i)
                dve.wait_ge(sem("d_unit"), i)
                dve.tensor_tensor(headed[:, 512 * (i - 1):512 * i], bank(6), unit, ALU.mult).then_inc(sem("d_headed"), 1)
        dve.wait_ge(sem("d_out"), 1)
        follow(dve.scalar_tensor_tensor(xsum, xs, 2.0, bank(0, 2), ALU.mult, ALU.add))
        norm(dve, follow, tiled(xsum), tiled(xs), first_half="stage_half").then_inc(sem("stage_done"), 1)

    E_ = Space(W2.end, END)
    ctx_n, ctx_T = E_(4 * DC), E_(512)
    qkv, ctx_kv = E_(NT * 384), E_(4 * 256)
    squares, ctx_squares = E_(NT * 256), E_(512)
    norm2, rnorm = E_(40), E_(40)
    latT = E_(T)
    q_T, k_T = E_(T), E_(B * KEYS)
    weights = [E_(KEYS) for _ in range(2)]
    neg_max, w_sum, w_unit = E_(16), E_(16), E_(16)
    turned_w = [E_(768) for _ in range(2)]
    heads_T = E_(T)
    q_gain = E_(1)
    mask_row = E_(B * 333)[0:1, :]
    HALF = KEYS // 2
    EI = B * 4 * H_C

    lat_at = width(PACK_MIX)

    def e_sp(sp):
        sp.wait_ge(sem("stage_done"), 4)
        sp.dma_start(SB[:, stream.at:stream.at + width(PACK_EXP)], dram["exp"]).then_inc(sem("exp_in"), 16)

    def e_pool(pool, follow):
        pool.wait_ge(sem("stage_done"), 4)
        follow(pool.memset(mask_row, 0.0))
        m = mask_row.rearrange("p (b k) -> p b k", b=B)[:, :, 0:S2]
        follow(pool.tensor_copy(m, key_bytes.rearrange("p (b k) -> p b k", b=B)))
        follow(pool.tensor_scalar(m, m, 1.0, None, ALU.subtract))
        pool.tensor_scalar(m, m, -NEG, None, ALU.mult).then_inc(sem("e_mask"), 1)
        pool.wait_ge(sem("e_mask"), 1)
        pool_rstd(pool, 4)
        pool_rstd(pool)
        pool.wait_ge(sem("e_norm2"), 1)
        pool.tensor_tensor(rnorm, norm2, minus_half[:, 0:40], ALU.pow).then_inc(sem("e_rnorm"), 1)

    def e_pe(pe):
        pe.wait_ge(sem("e_ctx_n"), 1)
        for i in range(4):
            ins = pe.transpose(bank(2)[0:DC, 128 * i:128 * i + 128], ctx_n[:, DC * i:DC * i + DC], ident)
        ins.then_inc(sem("e_ctx_turned"), 1)
        turn_pe(pe, tiled(xn), 0, (sem("e_normed"), 1), (sem("e_half"), 1))
        pe.wait_ge(sem("e_ctx_T"), 1)
        for i in range(4):
            ins = pe.matmul(bank(4 + i // 2)[:, 256 * (i % 2):256 * (i % 2) + 256], ctx_T[0:DC, 128 * i:128 * i + 128],
                            lat["l_WkvT"][0:DC, :], start=True, stop=True)
        ins.then_inc(sem("e_ctx_kv"), 1)
        pe.wait_ge(sem("turned_in"), 6)
        wide = SB[:, lat_at + 264:lat_at + 264 + 384]
        for t in range(NT):
            if t >= 2:
                pe.wait_ge(sem("e_qkv_in"), t - 1)
            pe.matmul(bank(6 + t % 2)[:, 0:384], latT[:, 128 * t:128 * t + 128], wide, start=True, stop=True)\
              .then_inc(sem("e_qkv"), 1)
        pe.wait_ge(sem("e_scaled"), 1)
        for t in range(NT):
            pe.transpose(PS[:, 128 * t:128 * t + 128], qkv[:, 384 * t:384 * t + 128], ident)
            ins = pe.transpose(PS[:, 1024 + 128 * t:1024 + 128 * t + 128], qkv[:, 384 * t + 128:384 * t + 256], ident)
        for i in range(4):
            ins = pe.transpose(bank(4)[:, 128 * i:128 * i + 128], ctx_kv[:, 256 * i:256 * i + 128], ident)
        ins.then_inc(sem("e_qk_turned"), 1)
        pe.wait_ge(sem("e_qk_T"), 4)
        pe.wait_ge(sem("e_mask"), 1)

        def score(i):
            b, qt, h = i // 8, i // 2 % 4, i % 2
            r = slice(DK * h, DK * h + DK)
            if i >= 2:
                pe.wait_ge(sem("e_exp"), i - 1)
            pe.matmul(bank(2 * (i % 2))[:, 0:HALF], ones[0:1, :], mask_row[:, HALF * b:HALF * b + HALF], start=True, stop=False)
            for n in range(2):
                ins = pe.matmul(bank(2 * (i % 2) + n)[:, 0:HALF], q_T[r, 512 * b + 128 * qt:512 * b + 128 * qt + 128],
                                k_T[r, KEYS * b + HALF * n:KEYS * b + HALF * n + HALF], start=(n == 1), stop=True)
            ins.then_inc(sem("e_scores"), 1)

        def turn(i):
            pe.wait_ge(sem("e_weights"), i + 1)
            if i >= 1:
                pe.wait_ge(sem("e_weights_T"), 2 * i)
            w = weights[i % 2]
            for c in range(5):
                at = 0 if c == 0 else S2 + 128 * (c - 1)
                pe.transpose(PS[:, 2048 + 128 * c:2048 + 128 * c + 128], w[:, at:at + 128], ident)
            pe.transpose(PS[0:REST, 2048 + 640:2048 + 768], w[:, 128:S2], ident).then_inc(sem("e_turned"), 1)

        def weigh(i):
            b, qt, h = i // 8, i // 2 % 4, i % 2
            pe.wait_ge(sem("e_weights_T"), 2 * i + 2)
            o = bank(6 + b)[DK * h:DK * h + DK, 128 * qt:128 * qt + 128]
            w = turned_w[i % 2]
            c0 = 512 * b + 128 + DK * h
            pe.matmul(o, ctx_kv[:, c0:c0 + DK], w[:, 0:128], start=True, stop=False)
            pe.matmul(o, ctx_kv[0:REST, c0 + 256:c0 + 256 + DK], w[0:REST, 640:768], start=False, stop=False)
            for c in range(4):
                v0 = 384 * (4 * b + c) + 256 + DK * h
                ins = pe.matmul(o, qkv[:, v0:v0 + DK], w[:, 128 * (c + 1):128 * (c + 2)], start=False, stop=(c == 3))
            ins.then_inc(sem("e_weighed"), 1)

        for i in range(EI + 2):
            if i < EI:
                score(i)
            if 1 <= i <= EI:
                turn(i - 1)
            if i >= 2:
                weigh(i - 2)
        pe.wait_ge(sem("e_heads"), 1)
        for t in range(NT):
            o = PS[:, 128 * t:128 * t + 128]
            pe.matmul(o, ones[0:1, :], lines["l_bo"][0:1, :], start=True, stop=False)
            ins = pe.matmul(o, heads_T[:, 128 * t:128 * t + 128], lat["l_WoT"], start=False, stop=True)
        ins.then_inc(sem("e_out"), 1)

    def e_act(act):
        act.wait_ge(sem("e_ctx_turned"), 1)
        act.activation(ctx_T[0:DC, :], bank(2)[0:DC, :], ACT.Identity, scale=lat["lx_g"][0:DC, :], bias=lat["lx_b"][0:DC, :])\
           .then_inc(sem("e_ctx_T"), 1)
        act.wait_ge(sem("turned"), 6)
        act.activation(latT, bank(0, 2), ACT.Identity, scale=lat["ll_g"], bias=lat["ll_b"]).then_inc(sem("turned_in"), 1)
        act.wait_ge(sem("e_ctx_kv"), 1)
        act.activation(ctx_kv, bank(4, 2), ACT.Copy).then_inc(sem("e_ctx_kv_raw"), 1)
        for t in range(NT):
            act.wait_ge(sem("e_qkv"), t + 1)
            act.activation(qkv[:, 384 * t:384 * t + 384], bank(6 + t % 2)[:, 0:384], ACT.Copy).then_inc(sem("e_qkv_in"), 1)
        act.wait_ge(sem("e_qk_turned"), 1)
        act.wait_ge(sem("e_gain"), 1)
        act.activation(q_T, bank(0, 2), ACT.Copy, scale=q_gain).then_inc(sem("e_qk_T"), 1)
        k3 = k_T.rearrange("p (b k) -> p b k", b=B)
        act.activation(k3[:, :, S2:], bank(2, 2).rearrange("p (b k) -> p b k", b=B), ACT.Copy, scale=lat["kn_g"])\
           .then_inc(sem("e_qk_T"), 1)
        c4 = bank(4).rearrange("p (b k) -> p b k", b=B)
        act.activation(k3[:, :, 0:S2], c4[:, :, 0:S2], ACT.Copy, scale=lat["kn_g"]).then_inc(sem("e_qk_T"), 2)

        def turned_in(i):
            act.wait_ge(sem("e_turned"), i + 1)
            if i >= 2:
                act.wait_ge(sem("e_weighed"), i - 1)
            w = turned_w[i % 2]
            act.activation(w[:, 0:640], PS[:, 2048:2688], ACT.Copy).then_inc(sem("e_weights_T"), 1)
            act.activation(w[0:REST, 640:768], PS[0:REST, 2688:2816], ACT.Copy).then_inc(sem("e_weights_T"), 1)

        for i in range(EI + 1):
            if i < EI:
                act.wait_ge(sem("e_max"), i + 1)
                if i >= 2:
                    act.wait_ge(sem("e_turned"), i - 1)
                s = bank(2 * (i % 2), 2).rearrange("p (n k) -> p n k", n=2)[:, :, 0:HALF]
                act.activation(weights[i % 2].rearrange("p (n k) -> p n k", n=2), s, ACT.Exp, bias=neg_max[:, i:i + 1],
                               accum_out=w_sum[:, i:i + 1]).then_inc(sem("e_exp"), 1)
            if i >= 1:
                turned_in(i - 1)
        act.wait_ge(sem("e_weighed"), EI)
        act.activation(heads_T, bank(6, 2), ACT.Copy).then_inc(sem("e_heads"), 1)

    def e_dve(dve, follow):
        dve.wait_ge(sem("stage_done"), 4)
        dve.tensor_scalar(q_gain, lat["qn_g"], DK ** -0.5, None, ALU.mult).then_inc(sem("e_gain"), 1)
        c4 = lat["ctx"].rearrange("p (i d) -> p i d", d=DC)
        norm(dve, follow, c4, ctx_n.rearrange("p (i d) -> p i d", d=DC), 4).then_inc(sem("e_ctx_n"), 1)
        dve.wait_ge(sem("e_ctx_n"), 1)
        norm(dve, follow, tiled(xs), tiled(xn), first_half="e_half").then_inc(sem("e_normed"), 1)
        g = lambda a, n: a.rearrange("p (t g k) -> p t g k", g=n, k=DK)
        dve.wait_ge(sem("e_ctx_kv_raw"), 1)
        ck = ctx_kv.rearrange("p (i w) -> p i w", w=256)[:, :, 0:128]
        csq = ctx_squares.rearrange("p (i w) -> p i w", w=128)
        follow(dve.tensor_tensor(csq, ck, ck, ALU.mult))
        follow(dve.tensor_reduce(norm2[:, 32:40], ctx_squares.rearrange("p (g k) -> p g k", k=DK), AX_X, ALU.add))
        dve.wait_ge(sem("e_qkv_in"), NT)
        qk = qkv.rearrange("p (t w) -> p t w", w=384)[:, :, 0:256]
        follow(dve.tensor_tensor(squares.rearrange("p (t w) -> p t w", w=256), qk, qk, ALU.mult))
        follow(dve.tensor_reduce(norm2[:, 0:32], squares.rearrange("p (g k) -> p g k", k=DK), AX_X, ALU.add))
        dve.tensor_scalar(norm2, norm2, 1.0 / DK, 1e-16, ALU.mult, ALU.max).then_inc(sem("e_norm2"), 1)
        dve.wait_ge(sem("e_rnorm"), 1)
        for t in range(NT):
            q4 = qkv[:, 384 * t:384 * t + 256].rearrange("p (g k) -> p g k", k=DK)
            dve.tensor_tensor(q4, q4, rnorm[:, 4 * t:4 * t + 4][:, :, None].to_broadcast([P, 4, DK]), ALU.mult)
        for i in range(4):
            k2 = ctx_kv[:, 256 * i:256 * i + 128].rearrange("p (g k) -> p g k", k=DK)
            ins = dve.tensor_tensor(k2, k2, rnorm[:, 32 + 2 * i:34 + 2 * i][:, :, None].to_broadcast([P, 2, DK]), ALU.mult)
        ins.then_inc(sem("e_scaled"), 1)
        for i in range(EI + 1):
            if i < EI:
                dve.wait_ge(sem("e_scores"), i + 1)
                s = bank(2 * (i % 2), 2).rearrange("p (n k) -> p n k", n=2)[:, :, 0:HALF]
                dve.tensor_reduce(neg_max[:, i:i + 1], s, mybir.AxisListType.XY, ALU.max, negate=True)\
                   .then_inc(sem("e_max"), 1)
            if i >= 1:
                j = i - 1
                dve.wait_ge(sem("e_exp"), j + 1)
                follow(dve.reciprocal(w_unit[:, j:j + 1], w_sum[:, j:j + 1]))
                dve.tensor_scalar(weights[j % 2], weights[j % 2], w_unit[:, j:j + 1], None, ALU.mult).then_inc(sem("e_weights"), 1)
        dve.wait_ge(sem("e_out"), 1)
        follow(dve.tensor_tensor(xsum, xs, bank(0, 2), ALU.add))
        norm(dve, follow, tiled(xsum), tiled(xs), first_half="stage_half").then_inc(sem("stage_done"), 1)

    F_ = Space(W2.end, END)
    hidden = [F_(FCH * T) for _ in range(2)]
    silu = [F_(512) for _ in range(3)]
    logits, marks, hot1, hot2, e_logits, weight = (F_(NT * E1_LIVE) for _ in range(6))
    peak, w_total = F_(NT), F_(NT)
    HIDES = FCH * 2

    def f_rows(k):
        return min(128, FF1 - 128 * k)

    def f_pe(pe):
        turn_pe(pe, tiled(xs), 0, (sem("stage_done"), 5), (sem("stage_half"), 5))
        pe.wait_ge(sem("turned_in"), 7)
        for t in range(NT):
            ins = pe.matmul(bank(6)[:, 4 * t:4 * t + 4], xsT[:, 128 * t:128 * t + 128], lat["gate_T"], start=True, stop=True)
        ins.then_inc(sem("top2_logits"), 1)
        pe.wait_ge(sem("exp_in"), 16)

        def hide(i):
            e, k, n = i // HIDES, i % HIDES // 2, i % 2
            if i >= 3:
                pe.wait_ge(sem("top2_hidden"), i - 2)
            m, c = f_rows(k), FF1 * e + 128 * k
            for w, side in (("e_w1", 0), ("e_w3", 1)):
                ins = pe.matmul(bank(2 * (i % 3) + side)[0:m, :], exp_w[w][:, c:c + m], xsT[:, 512 * n:512 * n + 512],
                                start=True, stop=True)
                if side == 0:
                    ins.then_inc(sem("top2_w1"), 1)
            ins.then_inc(sem("top2_w3"), 1)

        def output(e, t):
            j = NT * e + t
            if t == 0:
                pe.wait_ge(sem("top2_hidden"), HIDES * (e + 1))
            if j == 0:
                pe.wait_ge(sem("top2_logits_in"), 1)
            if j >= 2:
                pe.wait_ge(sem("top2_added"), j - 1)
            for k in range(FCH):
                m = f_rows(k)
                w2 = exp_w["e_w2"][0:m, 128 * (FCH * e + k):128 * (FCH * e + k) + 128]
                ins = pe.matmul(bank(6 + j % 2)[:, 0:128], hidden[e % 2][0:m, T * k + 128 * t:T * k + 128 * t + 128], w2,
                                start=(k == 0), stop=(k == FCH - 1))
            ins.then_inc(sem("top2_output"), 1)

        for i in range(HIDES):
            hide(i)
        for e in range(E1_LIVE):
            for s in range(HIDES):
                if e + 1 < E1_LIVE:
                    hide(HIDES * (e + 1) + s)
                if s < NT:
                    output(e, s)

    def f_act(act):
        act.wait_ge(sem("turned"), 7)
        act.activation(xsT, bank(0, 2), ACT.Copy).then_inc(sem("turned_in"), 1)
        act.wait_ge(sem("top2_shifted"), 1)
        act.activation(e_logits, logits, ACT.Exp).then_inc(sem("top2_exp"), 1)
        for i in range(E1_LIVE * HIDES):
            m = f_rows(i % HIDES // 2)
            act.wait_ge(sem("top2_w1"), i + 1)
            if i >= 3:
                act.wait_ge(sem("top2_hidden"), i - 2)
            act.activation(silu[i % 3][0:m, :], bank(2 * (i % 3))[0:m, :], ACT.Silu).then_inc(sem("top2_silu"), 1)

    def f_dve(dve, follow):
        by_token = lambda a: a.rearrange("p (t e) -> p t e", e=E1_LIVE)
        each = lambda a: a[:, :, None].to_broadcast([P, NT, E1_LIVE])
        rank = lat["expert_rank"][:, None, 0:E1_LIVE].to_broadcast([P, NT, E1_LIVE])
        tt = lambda o, a, b, op: follow(dve.tensor_tensor(by_token(o), a, b, op))

        def largest(a, out):
            follow(dve.tensor_reduce(peak, by_token(a), AX_X, ALU.max))
            tt(marks, by_token(a), each(peak), ALU.is_equal)
            tt(marks, by_token(marks), rank, ALU.mult)
            follow(dve.tensor_reduce(peak, by_token(marks), AX_X, ALU.max))
            tt(out, by_token(marks), each(peak), ALU.is_equal)

        dve.wait_ge(sem("top2_logits"), 1)
        dve.tensor_copy(logits, bank(6)[:, 0:NT * E1_LIVE]).then_inc(sem("top2_logits_in"), 1)
        dve.wait_ge(sem("top2_logits_in"), 1)
        follow(dve.tensor_reduce(peak, by_token(logits), AX_X, ALU.max))
        dve.tensor_tensor(by_token(logits), by_token(logits), each(peak), ALU.subtract).then_inc(sem("top2_shifted"), 1)
        dve.wait_ge(sem("top2_shifted"), 1)
        largest(logits, hot1)
        follow(dve.scalar_tensor_tensor(hot2, hot1, NEG, logits, ALU.mult, ALU.add))
        follow(dve.tensor_copy(weight, hot2))
        largest(weight, hot2)
        tt(hot1, by_token(hot1), by_token(hot2), ALU.add)
        dve.wait_ge(sem("top2_exp"), 1)
        tt(weight, by_token(hot1), by_token(e_logits), ALU.mult)
        follow(dve.tensor_reduce(peak, by_token(weight), AX_X, ALU.add))
        follow(dve.reciprocal(w_total, peak))
        tt(weight, by_token(weight), each(w_total), ALU.mult)

        def multiply(i):
            e, k, n = i // HIDES, i % HIDES // 2, i % 2
            m = f_rows(k)
            dve.wait_ge(sem("top2_w3"), i + 1)
            dve.wait_ge(sem("top2_silu"), i + 1)
            if e >= 2 and i % HIDES == 0:
                dve.wait_ge(sem("top2_output"), NT * (e - 1))
            dve.tensor_tensor(hidden[e % 2][0:m, T * k + 512 * n:T * k + 512 * n + 512], silu[i % 3][0:m, :],
                              bank(2 * (i % 3) + 1)[0:m, :], ALU.mult).then_inc(sem("top2_hidden"), 1)

        def add(e, t):
            j = NT * e + t
            dve.wait_ge(sem("top2_output"), j + 1)
            if e:
                dve.wait_ge(sem("top2_added"), j - NT + 1)
            dve.scalar_tensor_tensor(tiled(xsum)[:, t, :], bank(6 + j % 2)[:, 0:128], weight[:, 4 * t + e:4 * t + e + 1],
                                     tiled(xsum if e else xs)[:, t, :], ALU.mult, ALU.add).then_inc(sem("top2_added"), 1)

        for i in range(HIDES):
            multiply(i)
        for e in range(E1_LIVE):
            for s in range(HIDES):
                if e + 1 < E1_LIVE:
                    multiply(HIDES * (e + 1) + s)
                if s < NT:
                    add(e, s)
        dve.wait_ge(sem("top2_added"), NT * E1_LIVE)
        norm(dve, follow, tiled(xsum), tiled(xs), first_half="stage_half").then_inc(sem("stage_done"), 1)

    block = ctx.enter_context(nc.Block())

    @block.sync
    def _(sp):
        a_sp(sp)
        c_sp(sp)
        e_sp(sp)
        sp.wait_ge(sem("stage_done"), 6)
        sp.dma_start(dram["out"].rearrange("b (c p) d -> p (b c) d", p=P), tiled(xs)).then_inc(sem("out_written"), 16)
        sp.wait_ge(sem("out_written"), 16)

    @block.tensor
    def _(pe):
        a_pe(pe)
        b_pe_pre(pe)
        b_pe_attention(pe)
        b_pe_ssm(pe)
        c_pe(pe)
        d_pe(pe)
        e_pe(pe)
        f_pe(pe)

    @block.scalar
    def _(act):
        a_act(act)
        b_act_pre(act)
        b_act_tables(act)
        b_act_attention(act)
        b_act_ssm(act)
        c_act(act)
        d_act(act)
        e_act(act)
        f_act(act)

    @block.gpsimd
    def _(pool):
        follow = chain(pool, "pool_step")
        pool.wait_ge(sem("ones_set"), 2)
        pool_rstd(pool)
        b_pool_pre(pool, follow)
        pool_rstd(pool)
        b_pool_norm(pool, follow)
        b_pool_attention(pool, follow)
        for _ in range(3):
            pool_rstd(pool)
        for _ in range(3):
            pool_rstd(pool)
        d_pool(pool)
        pool_rstd(pool)
        e_pool(pool, follow)
        pool_rstd(pool)
        pool_rstd(pool)

    @block.vector
    def _(dve):
        follow = chain(dve, "dve_step")
        a_dve(dve, follow)
        b_dve_tables(dve, follow)
        b_dve_norm(dve, follow)
        b_dve_factors(dve, follow)
        b_dve_attention(dve, follow)
        b_dve_ssm(dve, follow)
        c_dve(dve, follow)
        d_dve(dve, follow)
        e_dve(dve, follow)
        f_dve(dve, follow)


def _constants():
    n = np.arange(512)
    turn = 2.0 * np.pi * ((n[:, None] * n[None, :]) % 1024) / 1024.0
    cos, sin = np.cos(turn), -np.sin(turn)
    nyquist = 1.0 - 2.0 * (n % 2)
    fwd, inv = sin.copy(), sin.copy()
    fwd[:, 0] = nyquist
    inv[0, :] = nyquist
    rows = lambda a: a.reshape(4, 128, 512).transpose(1, 0, 2).reshape(128, 2048)
    p = np.arange(128)
    weight = np.full((128, 4), 4.0 / 1024)
    weight[0, 0] = 2.0 / 1024
    pick = np.zeros((128, 2, 128))
    pick[0, 0] = pick[1, 1] = 1.0
    return {
        "dft_cos": rows(cos), "dft_sin": rows(fwd), "inv_sin0": inv[:128], "ident": np.eye(128),
        "pair_sum": p[:, None] // 2 == p[None, :] // 2, "head_sum": p[:, None] // 32 == p[None, :] // 32,
        "earlier": p[:, None] < p[None, :], "low_lags": np.tile(np.arange(LOW), (128, 1)),
        "high_lags": np.tile(LOW * np.arange(HIGH), (128, 1)), "quarter": 0.25 * (p < 64)[:, None],
        "quarter_angle": 0.25 * TWO_PI * (p < 64)[:, None], "bin_weight": weight,
        "expert_rank": np.tile(8.0 - np.arange(8), (128, 1)), "head_pick": pick.reshape(128, 256),
    }


def _layout(i):
    f = lambda a: np.asarray(a, np.float32)
    col = lambda a: a.reshape(-1, 1)
    tiles = lambda a, n: a.reshape(-1, 128, n).transpose(1, 0, 2).reshape(128, -1)
    x = i["x"].reshape(T, D)
    ctx = i["ctx_768"]
    ctx_tm = np.zeros((2, 2, 128, DC), np.float32)
    ctx_tm[:, 0] = ctx[:, :128]
    ctx_tm[:, 1, :REST] = ctx[:, 128:]
    b1 = np.zeros((4, 128, E0, E0), np.float32)
    for e in range(E0):
        b1[:, :, e, e] = i["L0_ffn_b1"][e].reshape(4, 128)
    w2 = np.zeros((E1_LIVE, FCH * 128, 128), np.float32)
    w2[:, :FF1] = i["L1_ffn_w2"][:E1_LIVE]
    qkv = i["L0_ffn_in_proj_b"]
    names = {
        "xT": x.T, "x": tiles(x, D), "W_in": i["L0_attn_W_in"], "W_out": i["L0_attn_W_out"],
        "lower": col(i["L0_attn_lower_bound"]),
        "A_re": i["L0_xattn_A_re"], "A_im": i["L0_xattn_A_im"], "C_re": i["L0_xattn_C_re"],
        "C_im": i["L0_xattn_C_im"], "log_dt": col(i["L0_xattn_log_dt"]),
        "Wq_T": i["L0_xattn_Wq"].T, "Wk": i["L0_xattn_Wk"], "Wv": i["L0_xattn_Wv"],
        "ctx_T": ctx.reshape(B * S2, DC).T,
        "W_film": np.concatenate([i["L0_xattn_W_film_in"], i["L0_xattn_W_film_out"]], 1),
        "W1": i["L0_xattn_W1"], "W2": tiles(i["L0_xattn_W2"], 128), "ffn_b1": i["L0_xattn_b1"].reshape(4, 128).T,
        "ffn_g": col(i["L0_xattn_g_ffn"]), "ffn_b": col(i["L0_xattn_b_ffn"]),
        "m_w1T": tiles(i["L0_ffn_w1"].transpose(0, 2, 1).reshape(E0 * FF0, D), D),
        "m_w2": tiles(i["L0_ffn_w2"].reshape(E0 * FF0, D), D),
        "m_b1": b1.transpose(1, 0, 2, 3).reshape(128, 256),
        "qkv_T": i["L0_ffn_in_proj_w"].T, "ow_T": i["L0_ffn_out_proj_w"].T, "m_wg": i["L0_ffn_wg"],
        "b_q": col(qkv[:128]), "b_v": col(qkv[256:]), "ln1_g": col(i["L0_ffn_ln1_g"]),
        "ln1_b": col(i["L0_ffn_ln1_b"]), "m_b2": i["L0_ffn_b2"],
        "w_q": i["L1_attn_w_q"].transpose(1, 0, 2).reshape(D, -1),
        "w_k": i["L1_attn_w_k"].transpose(1, 0, 2).reshape(D, -1),
        "w_v": i["L1_attn_w_v"].transpose(1, 0, 2).reshape(D, -1), "w_o": tiles(i["L1_attn_w_o"], D),
        "l_WqT": i["L1_xattn_Wq"].T, "l_WkvT": i["L1_xattn_Wkv"].T, "l_WlkvT": i["L1_xattn_Wlkv"].T,
        "l_WoT": i["L1_xattn_Wo"].T, "ctx": ctx_tm.transpose(2, 0, 1, 3).reshape(128, -1),
        "lx_g": col(i["L1_xattn_ln_x_g"]), "lx_b": col(i["L1_xattn_ln_x_b"]),
        "ll_g": col(i["L1_xattn_ln_l_g"]), "ll_b": col(i["L1_xattn_ln_l_b"]),
        "qn_g": col(np.tile(i["L1_xattn_qn_g"], 2)), "kn_g": col(np.tile(i["L1_xattn_kn_g"], 2)),
        "gate_T": i["L1_ffn_gate_w"][:E1_LIVE].T,
        "e_w1": i["L1_ffn_w1"][:E1_LIVE].transpose(1, 0, 2).reshape(D, -1),
        "e_w3": i["L1_ffn_w3"][:E1_LIVE].transpose(1, 0, 2).reshape(D, -1),
        "e_w2": tiles(w2.reshape(-1, D), D),
    }
    names.update(_constants())
    packed = {}
    for key, pack in PACKS.items():
        a = np.zeros((128, width(pack)), np.float32)
        at = 0
        for name, n in pack:
            v = f(names[name])
            a[:v.shape[0], at:at + n] = v
            at += n
        packed[key] = a
    rows = {"g_in": "L0_xattn_g_norm_in", "b_in": "L0_xattn_b_norm_in", "g_out": "L0_xattn_g_norm_out",
            "b_out": "L0_xattn_b_norm_out", "n1_g": "L0_ffn_ln1_g", "n1_b": "L0_ffn_ln1_b", "n2_g": "L0_ffn_ln2_g",
            "n2_b": "L0_ffn_ln2_b"}
    packed["rows"] = np.concatenate([f(i[rows[r]]) for r in ROWS]).reshape(1, -1)
    packed["lines"] = np.concatenate([f(i["L0_xattn_b2"]), f(i["L0_ffn_out_proj_b"]), f(i["L1_xattn_bo"]),
                                      f(i["L0_xattn_b_film_in"]), f(i["L0_xattn_b_film_out"])]).reshape(1, -1)
    packed["mod_gate"] = f(i["L0_xattn_mod_gate"]).reshape(1, 1)
    packed["d_skip"] = f(i["L0_xattn_D_skip"]).reshape(1, 128)
    packed["text_mask"] = np.ascontiguousarray(i["mask_BxS_bf1"].reshape(NT, 128).T)
    packed["ctx_mask"] = i["mask_BxS2_bf1"].reshape(1, B * S2)
    packed["key_mask"] = i["mask_BxS2_bk0"].reshape(1, B * S2)
    return packed


def kernel(**inputs):
    import concourse.bacc as bacc
    from concourse.bass_utils import run_bass_kernel_spmd

    inputs = {k: np.asarray(v) for k, v in inputs.items()}
    arrays = _layout(inputs)
    nc = bacc.Bacc("TRN2", target_bir_lowering=False, num_devices=1)
    aps = {k: nc.dram_tensor(k, a.shape, mybir.dt.from_np(a.dtype), kind="ExternalInput").ap()
           for k, a in arrays.items()}
    aps["out"] = nc.dram_tensor("out", (B, S, D), F32, kind="ExternalOutput").ap()
    build(nc, aps)
    r = run_bass_kernel_spmd(nc, [arrays], core_ids=[0])
    return r.results[0]["out"]
```
